# Optimizing a Trainium2 kernel written in Bass

```python
import numpy as np
import jax
import jax.numpy as jnp

def _softmax(x, axis=-1):
    return jax.nn.softmax(x, axis=axis)

def _gelu(x):
    return jax.nn.gelu(x, approximate=True)

def _silu(x):
    return jax.nn.silu(x)

def _sigmoid(x):
    return jax.nn.sigmoid(x)

def _layernorm(x, axis=-1, eps=1e-05):
    m = jnp.mean(x, axis=axis, keepdims=True)
    v = jnp.var(x, axis=axis, keepdims=True)
    return (x - m) / jnp.sqrt(v + eps)

def _scatter_add(tgt, idx, src, axis=0):
    return tgt.at[idx].add(src)

def _segment_sum(src, seg, n):
    return jax.ops.segment_sum(src, seg, n)
kernel_name = 'mk_flamingo_gated_d2_seqx_r4_d9348f'

def setup_inputs(seed: int=0):
    np.random.seed(seed)
    _w = jnp.asarray

    def _rec_inputs():
        import jax
        import jax.numpy as jnp
        _rk = jax.random.key(seed)
        x = -0.0002928 + 1 * jax.random.normal(jax.random.fold_in(_rk, 1), (2, 1024, 256), jnp.float32)
        _lenS = 1024 - jax.random.randint(jax.random.fold_in(_rk, 7), (2,), 0, max(1, 1024 // 4) + 1, jnp.int32)
        _lenS2 = 77 - jax.random.randint(jax.random.fold_in(_rk, 8), (2,), 0, max(1, 77 // 4) + 1, jnp.int32)
        _ctx_1024P = jax.random.normal(jax.random.fold_in(_rk, 11), (2, 16, 256), jnp.float32)
        _ctx_1024c = jax.random.dirichlet(jax.random.fold_in(_rk, 511), 0.3 * jnp.ones((16,), jnp.float32), (2, 77))
        _ctx_1024t = jnp.einsum('bsk,bkd->bsd', _ctx_1024c, _ctx_1024P)
        _ctx_1024t = _ctx_1024t * jax.lax.rsqrt(jnp.mean(jnp.square(_ctx_1024t)) + 1e-12) * 0.953939
        ctx_1024 = 2.81802e-05 + 1.00001 * (_ctx_1024t + 0.3 * jax.random.normal(jax.random.fold_in(_rk, 611), (2, 77, 256), jnp.float32))
        _g = jax.random.normal(jax.random.fold_in(_rk, 9001), (2, 2), jnp.float32)
        _g = jnp.sign(_g) * jnp.maximum(jnp.abs(_g), 1.0) + (_g == 0) * 1.0
        g_xattn = _g[0]
        g_ffn = _g[1]
        return (x, ctx_1024, g_xattn, g_ffn)
    x, ctx_1024, g_xattn, g_ffn = _rec_inputs()

    def _L0_xattn_setup():
        import jax, jax.numpy as jnp
        import numpy as np
        DIM = 256
        NUM_HEADS = 16
        HEAD_DIM = DIM // NUM_HEADS
        SCALE = HEAD_DIM ** (-0.5)
        key = jax.random.key(seed)
        k1, k2, k3, k4 = jax.random.split(key, 4)
        B, N_q, N_kv = (4, 256, 1024)
        q = jax.random.normal(k1, (B, N_q, DIM), dtype=jnp.float32)
        kv = jax.random.normal(k2, (B, N_kv, DIM), dtype=jnp.float32)
        W_qkv = jax.random.normal(k3, (DIM, 3 * DIM), dtype=jnp.float32) * DIM ** (-0.5)
        W_proj = jax.random.normal(k4, (DIM, DIM), dtype=jnp.float32) * DIM ** (-0.5)
        b_proj = jnp.zeros((DIM,), dtype=jnp.float32)
        return {'q': q, 'kv': kv, 'W_qkv': W_qkv, 'W_proj': W_proj, 'b_proj': b_proj}
    _L0_xattn_all = _L0_xattn_setup()
    _L0_xattn_in = {k: v for k, v in _L0_xattn_all.items() if k in ('W_qkv', 'W_proj', 'b_proj')}
    del _L0_xattn_all

    def _L0_ffn_setup():
        import jax, jax.numpy as jnp
        import numpy as np
        TOP_K = 2
        key = jax.random.key(seed)
        ks = jax.random.split(key, 6)
        B, S, D, F, E = (2, 512, 256, 1024, 8)
        sd = 1.0 / np.sqrt(D)
        sf = 1.0 / np.sqrt(F)
        return {'x': jax.random.normal(ks[0], (B, S, D), jnp.float32), 'gate_w': jax.random.normal(ks[1], (D, E), jnp.float32) * sd, 'w1': jax.random.normal(ks[2], (E, D, F), jnp.float32) * sd, 'b1': jax.random.normal(ks[3], (E, F), jnp.float32) * 0.01, 'w2': jax.random.normal(ks[4], (E, F, D), jnp.float32) * sf, 'b2': jax.random.normal(ks[5], (E, D), jnp.float32) * 0.01}
    _L0_ffn_all = _L0_ffn_setup()
    _L0_ffn_in = {k: v for k, v in _L0_ffn_all.items() if k in ('gate_w', 'w1', 'b1', 'w2', 'b2')}
    del _L0_ffn_all

    def _L1_xattn_setup():
        import jax, jax.numpy as jnp
        import numpy as np
        N_HEAD = 16
        key = jax.random.key(seed)
        ks = jax.random.split(key, 5)
        b, l, d = (4, 512, 256)
        dh = d // N_HEAD
        return {'q': jax.random.normal(ks[0], (b, l, d), dtype=jnp.float32), 'kv': jax.random.normal(ks[1], (b, l, d), dtype=jnp.float32), 'Wq': jax.random.normal(ks[2], (d, d), dtype=jnp.float32) * 0.02, 'Wkv': jax.random.normal(ks[3], (2 * dh, d), dtype=jnp.float32) * 0.02, 'Wc': jax.random.normal(ks[4], (d, d), dtype=jnp.float32) * 0.02}
    _L1_xattn_all = _L1_xattn_setup()
    _L1_xattn_in = {k: v for k, v in _L1_xattn_all.items() if k in ('Wq', 'Wkv', 'Wc')}
    del _L1_xattn_all

    def _L1_ffn_setup():
        import jax, jax.numpy as jnp
        import numpy as np
        B, S, H = (2, 1024, 256)
        E, K, I = (8, 2, 352)
        key = jax.random.key(seed)
        ks = jax.random.split(key, 9)
        sc = 0.02
        return {'hidden_states': jax.random.normal(ks[0], (B, S, H), jnp.float32), 'gate_w': jax.random.normal(ks[1], (E, H), jnp.float32) * sc, 'w_gate': jax.random.normal(ks[2], (E, H, I), jnp.float32) * sc, 'w_up': jax.random.normal(ks[3], (E, H, I), jnp.float32) * sc, 'w_down': jax.random.normal(ks[4], (E, I, H), jnp.float32) * sc, 'sw_gate': jax.random.normal(ks[5], (H, I), jnp.float32) * sc, 'sw_up': jax.random.normal(ks[6], (H, I), jnp.float32) * sc, 'sw_down': jax.random.normal(ks[7], (I, H), jnp.float32) * sc, 'shared_gate_w': jax.random.normal(ks[8], (1, H), jnp.float32) * sc}
    _L1_ffn_all = _L1_ffn_setup()
    _L1_ffn_in = {k: v for k, v in _L1_ffn_all.items() if k in ('gate_w', 'w_gate', 'w_up', 'w_down', 'sw_gate', 'sw_up', 'sw_down', 'shared_gate_w')}
    del _L1_ffn_all
    return {'x': x, 'ctx_1024': ctx_1024, 'g_xattn': g_xattn, 'g_ffn': g_ffn, 'L0_xattn_W_qkv': _L0_xattn_in['W_qkv'], 'L0_xattn_W_proj': _L0_xattn_in['W_proj'], 'L0_xattn_b_proj': _L0_xattn_in['b_proj'], 'L0_ffn_gate_w': _L0_ffn_in['gate_w'], 'L0_ffn_w1': _L0_ffn_in['w1'], 'L0_ffn_b1': _L0_ffn_in['b1'], 'L0_ffn_w2': _L0_ffn_in['w2'], 'L0_ffn_b2': _L0_ffn_in['b2'], 'L1_xattn_Wq': _L1_xattn_in['Wq'], 'L1_xattn_Wkv': _L1_xattn_in['Wkv'], 'L1_xattn_Wc': _L1_xattn_in['Wc'], 'L1_ffn_gate_w': _L1_ffn_in['gate_w'], 'L1_ffn_w_gate': _L1_ffn_in['w_gate'], 'L1_ffn_w_up': _L1_ffn_in['w_up'], 'L1_ffn_w_down': _L1_ffn_in['w_down'], 'L1_ffn_sw_gate': _L1_ffn_in['sw_gate'], 'L1_ffn_sw_up': _L1_ffn_in['sw_up'], 'L1_ffn_sw_down': _L1_ffn_in['sw_down'], 'L1_ffn_shared_gate_w': _L1_ffn_in['shared_gate_w']}

def reference(x, ctx_1024, g_xattn, g_ffn, L0_xattn_W_qkv, L0_xattn_W_proj, L0_xattn_b_proj, L0_ffn_gate_w, L0_ffn_w1, L0_ffn_b1, L0_ffn_w2, L0_ffn_b2, L1_xattn_Wq, L1_xattn_Wkv, L1_xattn_Wc, L1_ffn_gate_w, L1_ffn_w_gate, L1_ffn_w_up, L1_ffn_w_down, L1_ffn_sw_gate, L1_ffn_sw_up, L1_ffn_sw_down, L1_ffn_shared_gate_w):
    import jax
    import jax.numpy as jnp

    def _L0_xattn_ref(q, kv, W_qkv, W_proj, b_proj):
        import jax, jax.numpy as jnp
        import numpy as np
        DIM = 256
        NUM_HEADS = 16
        HEAD_DIM = DIM // NUM_HEADS
        SCALE = HEAD_DIM ** (-0.5)
        B, N_q, C = q.shape
        N_kv = kv.shape[1]
        H, hd = (NUM_HEADS, HEAD_DIM)
        kv_qkv = (kv @ W_qkv).reshape(B, N_kv, 3, H, hd)
        k = jnp.transpose(kv_qkv[:, :, 1], (0, 2, 1, 3))
        v = jnp.transpose(kv_qkv[:, :, 2], (0, 2, 1, 3))
        q_qkv = (q @ W_qkv).reshape(B, N_q, 3, H, hd)
        qh = jnp.transpose(q_qkv[:, :, 0], (0, 2, 1, 3))
        attn = jnp.einsum('bhqd,bhkd->bhqk', qh, k) * SCALE
        attn = jax.nn.softmax(attn, axis=-1)
        x = jnp.einsum('bhqk,bhkd->bhqd', attn, v)
        x = jnp.transpose(x, (0, 2, 1, 3)).reshape(B, N_q, C)
        return x @ W_proj + b_proj

    def _L0_ffn_ref(x, gate_w, w1, b1, w2, b2):
        import jax, jax.numpy as jnp
        import numpy as np
        TOP_K = 2
        B, S, D = x.shape
        T = B * S
        xf = x.reshape(T, D)
        gate_scores = jax.nn.softmax(xf @ gate_w, axis=-1)
        topk_scores, topk_idx = jax.lax.top_k(gate_scores, TOP_K)
        topk_scores = topk_scores / jnp.sum(topk_scores, axis=-1, keepdims=True)
        h = jax.nn.gelu(jnp.einsum('td,edf->etf', xf, w1) + b1[:, None, :], approximate=False)
        y = jnp.einsum('etf,efd->etd', h, w2) + b2[:, None, :]
        tok = jnp.arange(T)
        y_sel = y[topk_idx.T, tok[None, :]]
        out = jnp.einsum('kt,ktd->td', topk_scores.T, y_sel)
        return out.reshape(B, S, D)

    def _L1_xattn_ref(q, kv, Wq, Wkv, Wc):
        import jax, jax.numpy as jnp
        import numpy as np
        N_HEAD = 16
        b, l, d = q.shape
        h = N_HEAD
        dh = d // h
        qp = jnp.einsum('bld,ed->ble', q, Wq)
        scores = jnp.einsum('bld,bmd->blm', qp, kv)
        idx = jnp.argmax(scores, axis=-1)
        mem = jnp.take_along_axis(kv, idx[..., None], axis=1)
        mkv = jnp.einsum('bld,ed->ble', mem, Wkv)
        mk, mv = jnp.split(mkv, 2, axis=-1)
        qh = qp.reshape(b, l, h, dh).transpose(0, 2, 1, 3)
        scale = 1.0 / np.sqrt(dh).astype(np.float32)
        logits = jnp.einsum('bhld,bmd->bhlm', qh, mk) * scale
        attn = jax.nn.softmax(logits, axis=-1)
        out = jnp.einsum('bhlm,bmd->bhld', attn, mv)
        out = out.transpose(0, 2, 1, 3).reshape(b, l, d)
        return jnp.einsum('bld,ed->ble', out, Wc)

    def _L1_ffn_ref(hidden_states, gate_w, w_gate, w_up, w_down, sw_gate, sw_up, sw_down, shared_gate_w):
        import jax, jax.numpy as jnp
        import numpy as np
        B, S, H = (2, 1024, 256)
        E, K, I = (8, 2, 352)
        b, s, h = hidden_states.shape
        x = hidden_states.reshape(-1, h)
        logits = jnp.einsum('th,eh->te', x, gate_w)
        probs = jax.nn.softmax(logits.astype(jnp.float32), axis=-1)
        topk_w, topk_i = jax.lax.top_k(probs, K)
        topk_w = topk_w / jnp.sum(topk_w, axis=-1, keepdims=True)
        combine = jnp.sum(jax.nn.one_hot(topk_i, E, dtype=topk_w.dtype) * topk_w[..., None], axis=1)
        combine = combine.astype(x.dtype)
        g = jnp.einsum('th,ehi->eti', x, w_gate)
        u = jnp.einsum('th,ehi->eti', x, w_up)
        eo = jnp.einsum('eti,eih->eth', jax.nn.silu(g) * u, w_down)
        out = jnp.einsum('te,eth->th', combine, eo)
        sg = jax.nn.sigmoid(jnp.einsum('th,oh->to', x, shared_gate_w))
        so = jax.nn.silu(x @ sw_gate) * (x @ sw_up) @ sw_down
        out = out + sg * so
        return out.reshape(b, s, h)
    x = x + jnp.tanh(g_xattn[0]) * _L0_xattn_ref(_layernorm(x, axis=-1), ctx_1024, L0_xattn_W_qkv, L0_xattn_W_proj, L0_xattn_b_proj)
    x = x + jnp.tanh(g_ffn[0]) * _L0_ffn_ref(_layernorm(x, axis=-1), L0_ffn_gate_w, L0_ffn_w1, L0_ffn_b1, L0_ffn_w2, L0_ffn_b2)
    x = x + jnp.tanh(g_xattn[1]) * _L1_xattn_ref(_layernorm(x, axis=-1), ctx_1024, L1_xattn_Wq, L1_xattn_Wkv, L1_xattn_Wc)
    x = x + jnp.tanh(g_ffn[1]) * _L1_ffn_ref(_layernorm(x, axis=-1), L1_ffn_gate_w, L1_ffn_w_gate, L1_ffn_w_up, L1_ffn_w_down, L1_ffn_sw_gate, L1_ffn_sw_up, L1_ffn_sw_down, L1_ffn_shared_gate_w)
    return x

_drawn_inputs = setup_inputs


def setup_inputs(seed=0):
    import zlib

    import numpy as np

    out = dict(_drawn_inputs(seed))
    spreads = {'g_ffn': (-1.0, 0.6), 'L0_xattn_b_proj': (0.0, 0.1)}
    factors = {'L0_ffn_b1': 8.0,
     'L0_ffn_b2': 8.0,
     'L1_xattn_Wq': 2.954,
     'L1_ffn_gate_w': 6.449,
     'L1_ffn_w_gate': 5.682,
     'L1_ffn_w_up': 5.627,
     'L1_ffn_w_down': 5.621,
     'L1_ffn_sw_gate': 7.769,
     'L1_ffn_sw_up': 7.659,
     'L1_ffn_sw_down': 7.674,
     'L1_ffn_shared_gate_w': 8.0}
    for name, (base, spread) in spreads.items():
        noise = np.random.default_rng([zlib.crc32(name.encode()), seed]).standard_normal(out[name].shape)
        drawn = base * np.exp(spread * noise) if base else spread * noise
        out[name] = jnp.asarray(drawn.astype(out[name].dtype))
    for name, factor in factors.items():
        out[name] = (out[name] * factor).astype(out[name].dtype)
    return out
```

```python
from contextlib import ExitStack

import concourse.bass as bass
from concourse import mybir

F32 = mybir.dt.float32
BF16 = mybir.dt.bfloat16
I32 = mybir.dt.int32
U32 = mybir.dt.uint32
ALU = mybir.AluOpType
ACT = mybir.ActivationFunctionType
AX = mybir.AxisListType

P = 128
NB, S, D = 2, 1024, 256
NK = 77
H, HD = 16, 16
T = NB * S
NT = T // P
KC = D // P
G = 512
QT_ = G // P
GB = S // G
HH = H // 2
HK = HH * NK
JT = -(-HK // P)
ROWS = [min(P, HK - P * j) for j in range(JT)]
QK = HK // 2
VW = HD + 1
SCALE = HD ** -0.5
EPS = 1e-5
NE, TOPK = 8, 2
F0, F1 = 1024, 352
FC0 = F0 // P
C1 = [(0, 128), (128, 128), (256, 96)]
NS = (T * TOPK + NE * (P - 1)) // P
NG = NT * TOPK
W0E = KC * F0
WG1, WD1 = KC * 2 * F1, 3 * D
BIG = 1.0e30
LATE = 5
RING = 4


class Chain:

    def __init__(self, eng, sem, base=0, per=0):
        self.eng, self.sem, self.base, self.per, self.n = eng, sem, base, per, 0

    def done(self, ins, after=None):
        self.n += 1
        ins.then_inc(self.sem, 1)
        self.eng.wait_ge(self.sem, self.base * self.per + self.n if self.per else self.n)
        if after:
            after(self.eng)

    def close(self):
        assert self.n == self.per, self.n


def runs(L):
    n = NS + (NT if L else 0)
    found = [("one", i, 0) for i in range(4)]
    if L:
        found += [("loop", 2, NT // 2 - 1)] + [("one", i, 0) for i in range(NT - 2, NT + 2)]
        found += [("loop", NT // 2 + 1, (n - 1) // 2)]
    else:
        found += [("loop", 2, (n - 1) // 2)]
    return found + [("one", i, 0) for i in range((n - 1) // 2 * 2, n)]


def over_tiles(eng, L, step):
    for kind, a, b in runs(L):
        if kind == "loop":
            with eng.Fori(a, b) as h:
                step(h, 0)
                step(h, 1)
        else:
            step(a // 2, a % 2)


def program(nc, x, ctx, g_xattn, g_ffn, wqkv0, wproj0, bproj0, gate0, w1, b1, w2, b2,
            wq1, wkv1, wc1, gate1, wg1, wu1, wd1, swg, swu, swd, sgw, out):
    with ExitStack() as stack:
        def sb(name, shape, dt=F32):
            return stack.enter_context(nc.sbuf_tensor(name, shape, dt))

        def sem(name):
            return stack.enter_context(nc.semaphore(name))

        def sems(names, suffix):
            return {k: sem(k + suffix) for k in names.split()}

        xslots = nc.dram_tensor("xslots", [(NS + NT) * P, D], F32).ap()
        yslots = nc.dram_tensor("yslots", [(NS + NT) * P, D], F32).ap()
        X = sb("X", [P, NT * D])
        XN = sb("XN", [P, NT * D])
        W = sb("W", [P, 2 * NE * W0E])
        AW = sb("AW", [P, KC, 4 * D])
        CT = sb("CT", [P, KC, NB * NK])
        ident = sb("ident", [P, P])
        identb = sb("identb", [P, P], BF16)
        TG = sb("TG", [P, 4])
        blockm = sb("blockm", [P, HH])
        maskv = sb("maskv", [P, JT, HH])
        maskc = sb("maskc", [P, JT, HH])
        b1t = sb("b1t", [3 * NE, F0], BF16)
        b2t = sb("b2t", [3 * NE, D], BF16)
        gwt = sb("gwt", [P, KC, NE + 1])
        slot = sb("slot", [P, NG], U32)
        wgt = sb("wgt", [P, 3, NT])
        texp = sb("texp", [P, NS], I32)
        selc = sb("selc", [3 * NE, NS])
        onesb = sb("onesb", [24, P], BF16)
        onec = sb("onec", [P, 1])
        small = sb("small", [P, 128])
        arena = sb("arena", [P, 7936])
        PS = stack.enter_context(nc.psum_tensor("PS", [P, 8, 512], F32))

        STAT = small[:, 0:24].rearrange("p (t s) -> p t s", t=QT_)
        MV = small[:, 24:32].rearrange("p (t s) -> p t s", t=QT_)
        RSTD, VEPS, HALF = small[:, 32:36], small[:, 36:40], small[:, 40:44]
        RD = [small[:, 44:60], small[:, 104:120]]
        mark = small[:, 124:128]
        CNT = small[:, 60:65]
        KBI = small[:, 65:70]
        rmod = small[0:3 * NE, 70:71]
        prow = small[0:3 * NE, 71:72]
        bm = small[0:3 * NE, 72:75]
        TOP = small[:, 80:88]
        TOPI = small[:, 88:96].bitcast(U32)
        IDX = small[:, 96:97]

        iota77 = sb("iota77", [P, NK])
        SQ = sb("SQ", [P, NK])

        def cutter(memory):
            at = [0]

            def take(n, dt=F32):
                at[0] += n
                assert at[0] <= memory.shape[1], (at[0], memory.shape)
                view = memory[:, at[0] - n:at[0]]
                return view if dt is F32 else view.bitcast(dt)

            return take

        take = cutter(arena)
        PR = take(10 * G).rearrange("p (s q) -> p s q", s=2 * JT)
        CR = arena[:, 0:2 * HK].rearrange("p (k n) -> p k n", k=KC)
        SR = arena[:, 3 * G:3 * G + JT * P]
        XNT = arena[:, 6 * G:8 * G].rearrange("p (k q) -> p k q", k=KC)
        XNA = arena[:, 8 * G:10 * G].rearrange("p (t d) -> p t d", t=QT_)
        QF = take(GB * KC * G).rearrange("p (g k q) -> p g k q", g=GB, k=KC)
        LG = take(NT * (NE + 1))
        IND = take(HK, BF16).rearrange("p (f n) -> p f n", f=2)[0:H]
        take = cutter(W[:, (NE + LATE) * W0E:])
        KF = take(2 * HK).rearrange("p (f n) -> p f n", f=2)
        KB = take(HK, BF16).rearrange("p (f n) -> p f n", f=2)
        VF = take(2 * JT * HH * VW).rearrange("p (f j h v) -> p f j h v", f=2, j=JT, h=HH)
        QB = take(KC * G // 2, BF16).rearrange("p (k q) -> p k q", k=KC)
        MX = take(QT_ * H // 2, BF16).rearrange("p (t h) -> p t h", t=QT_)
        MT = take(G // 2, BF16)[0:H]
        OA = take(2 * D).rearrange("p (u d) -> p u d", u=2)
        OT = take(2 * D).rearrange("p (u k q) -> p u k q", u=2, k=KC)
        bproj = take(D)
        used = take(HK // 2, BF16)[0:1]

        take = cutter(arena)
        GE = NG * NE
        R_M = take(GE).rearrange("p (g e) -> p g e", g=NG)
        R_a, R_b, R_c, R_d = take(GE), take(GE), take(GE), take(320)
        R_u, R_1, R_i, R_rs, R_j = take(P), take(P), take(NT * NE), take(GE), take(NS + 1)

        FB = []
        for L in range(2):
            take = cutter(W[:, (NE + 1) * (WG1 + WD1):] if L else arena)
            FB.append({
                "H": take(2 * F0).rearrange("p (u n) -> p u n", u=2),
                "HT": take(2 * F0).rearrange("p (u c q) -> p u c q", u=2, c=FC0),
                "XS": take(2 * D).rearrange("p (u d) -> p u d", u=2),
                "XT": take(2 * D).rearrange("p (u k q) -> p u k q", u=2, k=KC),
                "Y": take(2 * D).rearrange("p (u d) -> p u d", u=2)})
        SEL = AW[0:3 * NE, 0, 0:2 * P].bitcast(BF16).rearrange("p (w u q) -> p w u q", w=2, u=2)
        raw1 = arena[:, 4 * F0 + 6 * D:]
        rq = raw1[:, 0:2 * D].rearrange("p (c d) -> p c d", c=2)
        rc = raw1[:, 2 * D:4 * D].rearrange("p (c d) -> p c d", c=2)
        rkv = raw1[0:2 * HD, 4 * D:5 * D]
        rg = raw1[0:NE + 1, 5 * D:6 * D]
        YG = XN[:, 0:RING * 3 * D].rearrange("p (r k d) -> p r k d", r=RING, k=3)

        zeros = XN[:, 0:3328]
        ctx_raw = XN[0:NK, 3400:3400 + NB * D].rearrange("p (b d) -> p b d", b=NB)
        bw = F0 + D
        bst, bpa0, bpa1, bpa2 = [arena[0:3 * NE, bw * i:bw * (i + 1)] for i in range(4)]
        bpb0, bpb1 = [arena[0:3 * NE, bw * i:bw * i + bw // 2].bitcast(BF16) for i in (4, 5)]
        Xt = X[:, :].rearrange("p (t d) -> p t d", t=NT)
        XNt = XN[:, :].rearrange("p (t d) -> p t d", t=NT)
        xtile = x.rearrange("b (t p) d -> p (b t) d", p=P)
        otile = out.rearrange("b (t p) d -> p (b t) d", p=P)
        W0a, W0b = W[:, 0:NE * W0E], W[:, NE * W0E:2 * NE * W0E]
        W1a, W1b = W[:, 0:(NE + 1) * WG1], W[:, (NE + 1) * WG1:(NE + 1) * (WG1 + WD1)]
        NW = [NE, NE + 1]
        NTB = S // P

        def tile_at(b, g, q=0):
            return b * (NTB * D) + (g * QT_ + q) * D

        U = sems("x_loaded ctx_loaded attn_w_loaded bias_loaded gates_loaded gate_w_loaded waits_settled zeros_set rows_zeroed "
                 "consts_set bias_split ctx_t ctx_copied tanh_done bproj_ready own_pool own_dve w0_loaded "
                 "w1_loaded w1_raw_loaded w1_t w1_copied out_stored", "")
        A = [sems("own_dve own_pool stats rstd ln_done x_t x_t_copied q_ready q_copied s77 s77_used counted "
                  "c_ready cnt_bias ctx_rep k_ready k_built kb_copied qb_copied v_ready v_built smax smax_used "
                  "mx_t mx_copied s_ready exp_done o_ready o_done o_t o_t_copied y_ready x_added xb_added xn_kept "
                  "logits logits_copied", str(L)) for L in range(2)]
        R = [sems("router_on r_consts onehot totals exp_in exp_out routed scattered router_own " + ("shared_stored" if L else ""), str(L))
             for L in range(2)]
        E = [sems("xs_loaded_0 xs_loaded_1 xs_t xt_copied h_ready h_act h_t ht_copied yt_ready "
                  "y_copied y_stored_0 y_stored_1 gathered_0 gathered_1 gathered_2 gathered_3 combined own " + ("h_mul" if L else "sel_up sel_down"), str(L))
             for L in range(2)]

        block = stack.enter_context(nc.Block())

        def settle(eng):
            eng.sem_inc(U["waits_settled"], 1)

        def after(eng, semaphore, n):
            eng.wait_ge(semaphore, n + 1)

        CREDITS = {
            "pool": "rstd xb_added xn_kept",
            "act": "x_t_copied q_copied kb_copied qb_copied mx_copied exp_done o_t_copied logits_copied",
            "dve": "stats ln_done s77_used counted cnt_bias ctx_rep k_built v_built smax_used o_done x_added",
            "pe": "x_t q_ready s77 c_ready k_ready v_ready smax mx_t s_ready o_ready o_t y_ready logits"}

        def count_from_one(eng, name):
            for L in range(2):
                for k in CREDITS[name].split():
                    eng.sem_inc(A[L][k], 1)

        def experts_io(sp, L):
            e, n = E[L], NS + (NT if L else 0)

            def row(h, u, shared):
                if shared:
                    return h * (2 * P) + (NS + u) * P
                return h * (2 * P) + (u - (NT if L else 0)) * P

            def load(h, u, first=False):
                shared = at[0] == "shared"
                if not first:
                    sp.wait_ge(e["xs_t"], h * 2 + u - 1)
                sp.dma_start(FB[L]["XS"][:, u], xslots[bass.ds(row(h, u, shared), P)]).then_inc(e[f"xs_loaded_{u}"], 16)

            def store(h, u, shared):
                sp.wait_ge(e["y_copied"], h * 2 + u + 1)
                sp.dma_start(yslots[bass.ds(row(h, u, shared), P)], FB[L]["Y"][:, u]).then_inc(e[f"y_stored_{u}"], 16)

            at = ["shared" if L else "routed"]
            if L:
                sp.wait_ge(R[1]["shared_stored"], 16)
                sp.wait_ge(R[1]["router_on"], 1)
            else:
                sp.wait_ge(R[0]["scattered"], 16 * NG)
            for u in range(2):
                load(0, u, first=True)
            for u in range(2):
                load(1, u)
            lo = 2
            if L:
                with sp.Fori(2, NT // 2) as h:
                    for u in range(2):
                        load(h, u)
                        store(h - 2, u, True)
                sp.wait_ge(R[1]["scattered"], 16 * NG)
                at[0] = "routed"
                lo = NT // 2 + 2
                for h in range(NT // 2, lo):
                    for u in range(2):
                        load(h, u)
                        store(h - 2, u, True)
            with sp.Fori(lo, n // 2) as h:
                for u in range(2):
                    load(h, u)
                    store(h - 2, u, False)
            if n % 2:
                load(n // 2, 0)
            for i in range(n // 2 * 2 - 4, n):
                store(i // 2, i % 2, False)

        @block.sync
        def _(sp):
            sp.dma_start(ctx_raw, ctx.rearrange("b k d -> k b d")).then_inc(U["ctx_loaded"], 16)
            sp.dma_start(Xt[:, 0:NTB], xtile[:, 0:NTB]).then_inc(U["x_loaded"], 16)
            sp.dma_start(AW[:, :, 0:3 * D], wqkv0.rearrange("(k p) n -> p k n", p=P)).then_inc(U["attn_w_loaded"], 16)
            sp.dma_start(Xt[:, NTB:], xtile[:, NTB:]).then_inc(U["x_loaded"], 16)
            sp.dma_start(AW[:, :, 3 * D:], wproj0.rearrange("(k p) n -> p k n", p=P)).then_inc(U["attn_w_loaded"], 16)

            def load_w1(e):
                sp.dma_start(W0a[:, bass.ds(e * W0E, W0E)].rearrange("p (k n) -> p k n", k=KC),
                             w1[bass.ds(e, 1)].rearrange("e (k p) n -> p (e k) n", p=P)).then_inc(U["w0_loaded"], 16)

            def load_w2(e):
                sp.dma_start(W0b[:, bass.ds(e * W0E, W0E)].rearrange("p (c n) -> p c n", c=FC0),
                             w2[bass.ds(e, 1)].rearrange("e (c p) n -> p (e c) n", p=P)).then_inc(U["w0_loaded"], 16)

            with sp.Fori(0, LATE) as e:
                load_w1(e)
                load_w2(e)
            with sp.Fori(LATE, NE) as e:
                load_w1(e)
            sp.wait_ge(R[0]["totals"], 1)
            with sp.Fori(LATE, NE) as e:
                load_w2(e)
            sp.wait_ge(R[0]["routed"], 1)
            sp.dma_start(rq, wq1.rearrange("(c p) d -> p c d", p=P)).then_inc(U["w1_raw_loaded"], 16)
            sp.dma_start(rc, wc1.rearrange("(c p) d -> p c d", p=P)).then_inc(U["w1_raw_loaded"], 16)
            sp.dma_start(rkv, wkv1).then_inc(U["w1_raw_loaded"], 16)
            sp.dma_start(rg[0:NE], gate1).then_inc(U["w1_raw_loaded"], 16)
            sp.dma_start(rg[NE:NE + 1], sgw).then_inc(U["w1_raw_loaded"], 16)
            experts_io(sp, 0)

            def expert_weights(e, g_, u_, d_):
                ga = W1a[:, bass.ds(e * WG1, WG1)].rearrange("p (w k n) -> p w k n", w=2, k=KC)
                da = W1b[:, bass.ds(e * WD1, WD1)].rearrange("p (c n) -> p c n", c=3)
                sp.dma_start(ga[:, 0], g_.rearrange("(k p) n -> p k n", p=P)).then_inc(U["w1_loaded"], 16)
                sp.dma_start(ga[:, 1], u_.rearrange("(k p) n -> p k n", p=P)).then_inc(U["w1_loaded"], 16)
                sp.dma_start(da[:, 0:2], d_[0:2 * P].rearrange("(c p) n -> p c n", p=P)).then_inc(U["w1_loaded"], 16)
                sp.dma_start(da[0:F1 - 2 * P, 2], d_[2 * P:F1]).then_inc(U["w1_loaded"], 16)

            sp.wait_ge(E[0]["yt_ready"], NS)
            expert_weights(NE, swg, swu, swd)
            with sp.Fori(0, NE) as e:
                expert_weights(e, wg1[bass.ds(e, 1)].rearrange("e a b -> (e a) b"),
                               wu1[bass.ds(e, 1)].rearrange("e a b -> (e a) b"),
                               wd1[bass.ds(e, 1)].rearrange("e a b -> (e a) b"))
            experts_io(sp, 1)
            for t in range(NT):
                sp.wait_ge(E[1]["combined"], t + 1)
                sp.dma_start(otile[:, t], Xt[:, t]).then_inc(U["out_stored"], 16)
            sp.wait_ge(U["out_stored"], 16 * NT)

        def pool_layer(pool, L):
            a, r, e = A[L], R[L], E[L]

            def rstd(own, n):
                after(pool, a["stats"], n)
                settle(pool)
                own.done(nc.gpsimd.tensor_scalar(VEPS, MV[:, :, 1], EPS, None, ALU.add))
                nc.gpsimd.tensor_tensor(RSTD, VEPS, HALF, ALU.pow).then_inc(a["rstd"], 1)

            with pool.Fori(0, NB) as b:
                own = Chain(pool, a["own_pool"], b, 2 * GB)
                for g in range(GB):
                    rstd(own, b * (2 * GB) + g + 1)
                if L == 0:
                    after(pool, a["ln_done"], b * (2 * GB) + GB)
                    pool.wait_ge(U["bproj_ready"], 1)
                    for g in range(GB):
                        xg = X[:, bass.ds(tile_at(b, g), QT_ * D)].rearrange("p (t d) -> p t d", t=QT_)
                        nc.gpsimd.tensor_tensor(xg, xg, bproj[:, None, :].to_broadcast([P, QT_, D]),
                                                ALU.add).then_inc(a["xb_added"], 1)
                for g in range(GB):
                    rstd(own, b * (2 * GB) + GB + g + 1)
                    after(pool, a["ln_done"], b * (2 * GB) + GB + g + 1)
                    nc.gpsimd.tensor_copy(XN[:, bass.ds(tile_at(b, g), QT_ * D)],
                                          XNA.rearrange("p t d -> p (t d)")).then_inc(a["xn_kept"], 1)
                own.close()
            if L:
                after(pool, a["xn_kept"], GB * NB)
                pool.dma_start(xslots[NS * P:(NS + NT) * P].rearrange("(t p) d -> p t d", p=P),
                               XNt).then_inc(r["shared_stored"], 16)
            pool.wait_ge(r["router_on"], 1)
            nc.gpsimd.memset(R_u, 1.0).then_inc(r["r_consts"], 1)
            nc.gpsimd.memset(R_1, 1.0).then_inc(r["r_consts"], 1)
            nc.gpsimd.memset(R_rs, 1.0).then_inc(r["r_consts"], 1)
            nc.gpsimd.iota(R_i.rearrange("p (t e) -> p t e", t=NT), pattern=[[0, NT], [1, NE]], base=0,
                           channel_multiplier=0, allow_small_or_imprecise_dtypes=True).then_inc(r["r_consts"], 1)
            nc.gpsimd.iota(R_j, pattern=[[1, NS + 1]], base=0, channel_multiplier=0,
                           allow_small_or_imprecise_dtypes=True).then_inc(r["r_consts"], 1)
            pool.wait_ge(r["r_consts"], 5)
            nc.gpsimd.affine_select(out=R_u, in_=R_u, compare_op=ALU.is_gt, fill=0.0, base=0,
                                    pattern=[[1, P]], channel_multiplier=-1).then_inc(r["r_consts"], 1)
            rs = R_rs.rearrange("p (e g) -> p e g", e=NE)
            nc.gpsimd.affine_select(out=rs, in_=rs, compare_op=ALU.not_equal, fill=0.0, base=0,
                                    pattern=[[0, NE], [1, NG]], channel_multiplier=0).then_inc(r["r_consts"], 1)
            pool.wait_ge(r["routed"], 1)
            pool.wait_ge(U["rows_zeroed"], 48)
            for g in range(NG):
                pool.indirect_dma_start(xslots[0:NS * P], bass.IndirectOffsetOnAxis(ap=slot[:, g:g + 1], axis=0),
                                        XNt[:, g % NT], None).then_inc(r["scattered"], 16)
            n = NS + (NT if L else 0)
            pool.wait_ge(r["scattered"], 16 * NG)
            pool.wait_ge(e["y_stored_0"], 16 * ((n + 1) // 2))
            pool.wait_ge(e["y_stored_1"], 16 * (n // 2))
            for t in range(NT):
                if t >= RING:
                    pool.wait_ge(e["combined"], t - RING + 1)
                arrived = e[f"gathered_{t % RING}"]
                for c in range(TOPK):
                    g = c * NT + t
                    pool.indirect_dma_start(YG[:, t % RING, c], None, yslots[0:NS * P],
                                            bass.IndirectOffsetOnAxis(ap=slot[:, g:g + 1], axis=0)
                                            ).then_inc(arrived, 16)
                if L:
                    pool.dma_start(YG[:, t % RING, 2], yslots[(NS + t) * P:(NS + t + 1) * P]).then_inc(arrived, 16)

        @block.gpsimd
        def _(pool):
            count_from_one(pool, "pool")
            own = Chain(pool, U["own_pool"])
            nc.gpsimd.memset(zeros, 0.0).then_inc(U["zeros_set"], 1)
            nc.gpsimd.memset(HALF, -0.5)
            nc.gpsimd.memset(onesb[:], 1.0)
            nc.gpsimd.memset(onec[:], 1.0)
            nc.gpsimd.memset(blockm[:], 1.0)
            nc.gpsimd.memset(maskv[:], 1.0)
            nc.gpsimd.memset(IND, -1.0)
            nc.gpsimd.memset(bm, 1.0)
            nc.gpsimd.iota(prow, pattern=[[0, 1]], base=0, channel_multiplier=1,
                           allow_small_or_imprecise_dtypes=True)
            nc.gpsimd.iota(iota77[:], pattern=[[1, NK]], base=0, channel_multiplier=0,
                           allow_small_or_imprecise_dtypes=True)
            own.done(nc.gpsimd.memset(ident[:], 0.0))
            own.done(nc.gpsimd.affine_select(out=ident[:], in_=ident[:], compare_op=ALU.not_equal, fill=1.0,
                                             base=0, pattern=[[-1, P]], channel_multiplier=1))

            def band(ap, pattern, base, mult, width):
                own.done(nc.gpsimd.affine_select(out=ap, in_=ap, compare_op=ALU.is_ge, fill=0.0, base=base,
                                                 pattern=pattern, channel_multiplier=mult))
                own.done(nc.gpsimd.affine_select(out=ap, in_=ap, compare_op=ALU.is_ge, fill=0.0,
                                                 base=width - 1 - base, pattern=[[-s, n] for s, n in pattern],
                                                 channel_multiplier=-mult))

            band(bm, [[-NE, 3]], 0, 1, NE)
            band(blockm[:], [[-HD, HH]], 0, 1, HD)
            band(maskv[:], [[P, JT], [-NK, HH]], 0, 1, NK)
            for f in range(2):
                band(IND[:, f], [[1, HK]], f * HH * NK, -NK, NK)
            nc.gpsimd.tensor_copy(identb[:], ident[:]).then_inc(U["consts_set"], 1)
            pool_layer(pool, 0)
            pool_layer(pool, 1)

        def act_attention(act, L):
            a, r = A[L], R[L]
            nh = 1 if L else 2

            def keep_transposed(b, n):
                after(act, a["x_t"], b * (2 * GB) + n)
                nc.scalar.activation(XNT, PS[:, 0:2], ACT.Copy).then_inc(a["x_t_copied"], 1)

            with act.Fori(0, NB) as b:
                for g in range(GB):
                    keep_transposed(b, g + 1)
                    after(act, a["q_ready"], b * GB + g + 1)
                    nc.scalar.activation(QF[:, g], PS[:, 2:4], ACT.Copy).then_inc(a["q_copied"], 1)
                after(act, a["k_built"], b + 1)
                nc.scalar.activation(KB[:, 0:nh], KF[:, 0:nh], ACT.Copy).then_inc(a["kb_copied"], 1)
                for g in range(GB):
                    n0 = b * GB + g
                    after(act, a["smax"], n0 * (4 * QT_))
                    after(act, a["q_copied"], b * GB + GB)
                    nc.scalar.activation(QB, QF[:, g], ACT.Copy).then_inc(a["qb_copied"], 1)
                    after(act, a["mx_t"], n0 + 1)
                    nc.scalar.activation(MT, PS[0:H, 0, 0:G // 2].bitcast(BF16), ACT.Copy).then_inc(a["mx_copied"], 1)
                    if L:
                        after(act, a["cnt_bias"], b + 1)
                    for i in range(2 * JT):
                        rows = ROWS[i % JT]
                        after(act, a["s_ready"], n0 * (2 * JT) + i + 1)
                        bias = {"bias": KBI[0:rows, i % JT:i % JT + 1]} if L else {}
                        nc.scalar.activation(PR[0:rows, i], PS[0:rows, 4 + i % 2], ACT.Exp, scale=SCALE,
                                             **bias).then_inc(a["exp_done"], 1)
                    for q in range(QT_):
                        after(act, a["o_t"], n0 * QT_ + q + 1)
                        nc.scalar.activation(OT[:, q % 2], PS[:, 0, 0:D].rearrange("p (k q) -> p k q", k=KC),
                                             ACT.Copy).then_inc(a["o_t_copied"], 1)
                for g in range(GB):
                    keep_transposed(b, GB + g + 1)
                    after(act, a["logits"], b * GB + g + 1)
                    w = NW[L]
                    nc.scalar.activation(LG[:, bass.ds(b * (NTB * w) + g * QT_ * w, QT_ * w)],
                                         PS[:, 6, 0:QT_ * w], ACT.Copy).then_inc(a["logits_copied"], 1)
            act.wait_ge(r["exp_in"], 1)
            nc.scalar.activation(wgt[:, 0], wgt[:, 0], ACT.Exp).then_inc(r["exp_out"], 1)
            if L:
                lg = LG[:, 0:NT * NW[1]].rearrange("p (t e) -> p t e", t=NT)
                nc.scalar.activation(wgt[:, 2], lg[:, :, NE], ACT.Exp, scale=-1.0).then_inc(r["exp_out"], 1)

        def act_experts(act, L):
            e, n = E[L], NS + (NT if L else 0)

            def keep_xt(i, u):
                act.wait_ge(e["xs_t"], i + 1)
                nc.scalar.activation(FB[L]["XT"][:, u], PS[:, 7, 0:D].rearrange("p (k q) -> p k q", k=KC),
                                     ACT.Copy).then_inc(e["xt_copied"], 1)

            def step(h, u):
                i = h * 2 + u
                later = not (isinstance(i, int) and i < 2)
                if L:
                    act.wait_ge(e["h_ready"], i * 2 + 1)
                    if later:
                        act.wait_ge(e["h_mul"], i - 1)
                    nc.scalar.activation(FB[L]["H"][:, u, 0:F1], PS[:, 2 * u, 0:F1], ACT.Silu).then_inc(e["h_act"], 1)
                else:
                    if later:
                        act.wait_ge(e["h_t"], i - 1)
                    for s in range(2):
                        act.wait_ge(e["h_ready"], i * 2 + s + 1)
                        nc.scalar.activation(FB[L]["H"][:, u, s * 512:(s + 1) * 512], PS[:, 2 * u + s],
                                             ACT.Gelu).then_inc(e["h_act"], 1)
                if not (isinstance(i, int) and i == n - 1):
                    keep_xt(i + 1, 1 - u)

            keep_xt(0, 0)
            over_tiles(act, L, step)

        @block.scalar
        def _(act):
            for part in range(3):
                act.dma_start(bst[part * NE:(part + 1) * NE, 0:F0], b1).then_inc(U["bias_loaded"], 16)
                act.dma_start(bst[part * NE:(part + 1) * NE, F0:], b2).then_inc(U["bias_loaded"], 16)
            act.dma_start(TG[:, 0:2], g_xattn.partition_broadcast(P)).then_inc(U["gates_loaded"], 16)
            act.dma_start(TG[:, 2:4], g_ffn.partition_broadcast(P)).then_inc(U["gates_loaded"], 16)
            act.dma_start(bproj[:], bproj0.partition_broadcast(P)).then_inc(U["gates_loaded"], 16)
            act.dma_start(gwt[:, :, 0:NE], gate0.rearrange("(k p) e -> p k e", p=P)).then_inc(U["gate_w_loaded"], 16)
            count_from_one(act, "act")
            act.wait_ge(U["zeros_set"], 1)
            z = xslots[0:NS * P].rearrange("(p r) d -> p (r d)", p=P)
            for i in range(3):
                act.dma_start(z[:, i * 3328:(i + 1) * 3328], zeros).then_inc(U["rows_zeroed"], 16)
            act.wait_ge(U["gates_loaded"], 48)
            nc.scalar.activation(TG[:], TG[:], ACT.Tanh).then_inc(U["tanh_done"], 1)
            act.wait_ge(U["tanh_done"], 1)
            nc.scalar.activation(bproj[:], bproj[:], ACT.Copy, scale=TG[:, 0:1]).then_inc(U["bproj_ready"], 1)
            act.wait_ge(U["ctx_t"], 1)
            nc.scalar.activation(CT[:], PS[:, 0, 0:KC * NB * NK].rearrange("p (k n) -> p k n", k=KC),
                                 ACT.Copy).then_inc(U["ctx_copied"], 1)
            act_attention(act, 0)
            act_experts(act, 0)
            act.wait_ge(U["w1_t"], 1)
            nc.scalar.activation(AW[:, :, 0:D], PS[:, 0:2, 0:D], ACT.Copy)
            nc.scalar.activation(AW[:, :, 3 * D:4 * D], PS[:, 2:4, 0:D], ACT.Copy)
            for i in range(2):
                for k in range(KC):
                    nc.scalar.activation(
                        AW[:, k, (1 + i) * D:(1 + i) * D + P].rearrange("p (h d) -> p h d", h=HH),
                        PS[:, 4 + k, i * HD:(i + 1) * HD][:, None, :].to_broadcast([P, HH, HD]), ACT.Copy)
            nc.scalar.activation(gwt[:], PS[:, 6:8, 0:NE + 1], ACT.Copy).then_inc(U["w1_copied"], 1)
            act_attention(act, 1)
            act_experts(act, 1)

        def dve_attention(dve, L):
            a = A[L]
            nh = 1 if L else 2
            mask = maskc if L else maskv
            gate = TG[:, L:L + 1]

            def norm(own, b, n):
                g = n % GB
                for q in range(QT_):
                    last = nc.vector.bn_stats(STAT[:, q], X[:, bass.ds(tile_at(b, g, q), D)])
                own.done(last, settle)
                for q in range(QT_):
                    last = nc.vector.bn_aggr(MV[:, q], STAT[:, q])
                last.then_inc(a["stats"], 1)
                after(dve, a["rstd"], b * (2 * GB) + n + 1)
                after(dve, a["x_t"], b * (2 * GB) + n)
                after(dve, a["xn_kept"], b * GB + max(n - GB, 0))
                for q in range(QT_):
                    last = nc.vector.tensor_scalar(XNA[:, q], X[:, bass.ds(tile_at(b, g, q), D)], MV[:, q, 0:1],
                                                   RSTD[:, q:q + 1], ALU.subtract, ALU.mult)
                last.then_inc(a["ln_done"], 1)

            def choose(own, b, g):
                for q in range(QT_):
                    n = b * NTB + g * QT_ + q
                    after(dve, a["s77"], n + 1)
                    settle(dve)
                    sc = PS[:, 6 + q % 2, 0:NK]
                    own.done(nc.vector.max(TOP, sc), settle)
                    own.done(nc.vector.max_index(TOPI, TOP, sc))
                    own.done(nc.vector.tensor_copy(IDX, TOPI[:, 0:1]))
                    if g == 0 and q == 0:
                        ins = nc.vector.tensor_scalar(SQ[:], iota77[:], IDX, None, ALU.is_equal)
                    else:
                        ins = nc.vector.scalar_tensor_tensor(SQ[:], iota77[:], IDX, SQ[:], ALU.is_equal, ALU.add)
                    ins.then_inc(a["s77_used"], 1)
                    after(dve, a["s77_used"], n + 1)

            with dve.Fori(0, NB) as b:
                own = Chain(dve, a["own_dve"], b, 2 * GB + NTB + (3 * NTB + 4 if L else 0))
                for g in range(GB):
                    norm(own, b, g)
                    if L:
                        choose(own, b, g)
                after(dve, a["x_t"], b * (2 * GB) + GB)
                for k in range(KC):
                    last = nc.vector.tensor_copy(CR[:, k].rearrange("p (h m) -> p h m", h=HH),
                                                 CT[:, k, bass.ds(b * NK, NK)][:, None, :].to_broadcast([P, HH, NK]))
                last.then_inc(a["ctx_rep"], 1)
                after(dve, a["k_ready"], b + 1)
                for f in range(nh):
                    last = nc.vector.tensor_tensor(KF[:, f].rearrange("p (h m) -> p h m", h=HH),
                                                   PS[:, f, 0:NK][:, None, :].to_broadcast([P, HH, NK]),
                                                   blockm[:, :, None].to_broadcast([P, HH, NK]), ALU.mult)
                last.then_inc(a["k_built"], 1)
                if L:
                    own.done(nc.vector.memset(SR[:, HK:], 0.0))
                    nc.vector.tensor_copy(SR[:, 0:HK].rearrange("p (h m) -> p h m", h=HH),
                                          SQ[:, None, :].to_broadcast([P, HH, NK])).then_inc(a["counted"], 1)
                    after(dve, a["c_ready"], b + 1)
                    own.done(nc.vector.tensor_copy(CNT, PS[:, 6, 0:JT]))
                    own.done(nc.vector.tensor_scalar(KBI, CNT, 0.0, -BIG, ALU.is_equal, ALU.mult))
                    own.done(nc.vector.tensor_scalar(used[:].rearrange("p (w n) -> p w n", w=2), PS[0:1, 2:4, 0:QK],
                                                     0.0, -BIG, ALU.is_equal, ALU.mult))
                    nc.vector.tensor_tensor(maskc[:], maskv[:], CNT[:, :, None].to_broadcast([P, JT, HH]),
                                            ALU.mult).then_inc(a["cnt_bias"], 1)
                    after(dve, a["cnt_bias"], b + 1)
                for f in range(nh):
                    after(dve, a["v_ready"], b * nh + f + 1)
                    rows = ROWS[JT - 1]
                    nc.vector.tensor_tensor(VF[:, f, 0:4, :, 0:HD],
                                            PS[:, 4].rearrange("p (j h d) -> p j h d", j=4, h=HH),
                                            mask[:, 0:4, :, None].to_broadcast([P, 4, HH, HD]), ALU.mult)
                    nc.vector.tensor_copy(VF[:, f, :, :, HD], mask[:])
                    nc.vector.tensor_tensor(VF[0:rows, f, 4, :, 0:HD],
                                            PS[0:rows, 5, 0:P].rearrange("p (h d) -> p h d", h=HH),
                                            mask[0:rows, 4, :, None].to_broadcast([rows, HH, HD]),
                                            ALU.mult).then_inc(a["v_built"], 1)
                for g in range(GB):
                    n0 = b * GB + g
                    after(dve, a["mx_t"], n0)
                    for i in range(4 * QT_):
                        q, c = i // 4, i % 4
                        after(dve, a["smax"], n0 * (4 * QT_) + i + 1)
                        nc.vector.tensor_reduce(MX[:, q, c * 4:c * 4 + 4],
                                                PS[:, 2 + i % 2, 0:QK].rearrange("p (h m) -> p h m", h=4),
                                                AX.X, ALU.max).then_inc(a["smax_used"], 1)
                    for s in range(QT_ + 2):
                        if s < QT_:
                            o = PS[:, 6 + s % 2, 0:2 * HH * VW].rearrange("p (h v) -> p h v", h=H)
                            after(dve, a["o_ready"], n0 * QT_ + s + 1)
                            own.done(nc.vector.reciprocal(RD[s % 2], o[:, :, HD]))
                            if s >= 2:
                                after(dve, a["o_t"], n0 * QT_ + s - 1)
                            nc.vector.tensor_tensor(OA[:, s % 2].rearrange("p (h d) -> p h d", h=H), o[:, :, 0:HD],
                                                    RD[s % 2][:, :, None].to_broadcast([P, H, HD]),
                                                    ALU.mult).then_inc(a["o_done"], 1)
                        if s >= 2:
                            xq = X[:, bass.ds(tile_at(b, g, s - 2), D)]
                            after(dve, a["y_ready"], n0 * QT_ + s - 1)
                            if L == 0:
                                after(dve, a["xb_added"], b * GB + GB)
                            nc.vector.scalar_tensor_tensor(xq, PS[:, 1, 0:D], gate, xq, ALU.mult,
                                                           ALU.add).then_inc(a["x_added"], 1)
                after(dve, a["x_added"], b * NTB + NTB)
                settle(dve)
                for g in range(GB):
                    norm(own, b, GB + g)
                own.close()

        def dve_router(dve, L, own):
            a, r = A[L], R[L]
            after(dve, a["logits_copied"], GB * NB)
            nc.vector.memset(mark[:, 0:1], 0.0).then_inc(r["router_on"], 1)
            lg = LG[:, 0:NT * NW[L]].rearrange("p (t e) -> p t e", t=NT)[:, :, 0:NE]
            te = lambda ap: ap[:, 0:NT * NE].rearrange("p (t e) -> p t e", t=NT)
            wide = lambda ap: ap[:, :, None].to_broadcast([P, NT, NE])
            dve.wait_ge(r["r_consts"], 7)
            first = R_c[:, 0:NT]
            for c in range(TOPK):
                src = lg if c == 0 else te(R_d)
                own.done(nc.vector.tensor_reduce(wgt[:, c], src, AX.X, ALU.max))
                own.done(nc.vector.tensor_tensor(te(R_a), src, wide(wgt[:, c]), ALU.is_equal))
                own.done(nc.vector.scalar_tensor_tensor(te(R_b), te(R_a), -99.0, te(R_i), ALU.mult, ALU.add))
                own.done(nc.vector.tensor_reduce(first, te(R_b), AX.X, ALU.min))
                own.done(nc.vector.tensor_scalar(first, first, 99.0, None, ALU.add))
                oh = R_M[:, c * NT:(c + 1) * NT]
                nc.vector.tensor_tensor(oh, te(R_i), wide(first), ALU.is_equal).then_inc(r["onehot"], 1)
                dve.wait_ge(r["onehot"], c + 1)
                if c == 0:
                    own.done(nc.vector.scalar_tensor_tensor(te(R_d), oh, -BIG, lg, ALU.mult, ALU.add))
            nc.vector.tensor_tensor(wgt[:, 0], wgt[:, 1], wgt[:, 0], ALU.subtract).then_inc(r["exp_in"], 1)
            eg = lambda ap: ap.rearrange("p (e g) -> p e g", e=NE)
            dve.wait_ge(r["totals"], 1)
            own.done(nc.vector.tensor_copy(eg(R_a), PS[:, 5, 0:GE].rearrange("p (g e) -> p e g", e=NE)))
            own.done(nc.vector.tensor_tensor_scan(R_b, R_rs, R_a, 0.0, ALU.mult, ALU.add))
            ni, nsh, nf, ends, base = [R_c[:, 48 + 8 * i:56 + 8 * i] for i in range(5)]
            own.done(nc.vector.tensor_scalar(ni.bitcast(I32), eg(R_b)[:, :, NG - 1], float(P - 1), None, ALU.add))
            own.done(nc.vector.tensor_scalar(nsh.bitcast(I32), ni.bitcast(I32), P.bit_length() - 1, None,
                                             ALU.arith_shift_right))
            own.done(nc.vector.tensor_copy(nf, nsh.bitcast(I32)))
            own.done(nc.vector.tensor_tensor_scan(ends, R_1[:, 0:NE], nf, 0.0, ALU.mult, ALU.add))
            own.done(nc.vector.tensor_tensor(base, ends, nf, ALU.subtract))
            jt = R_d[:, 0:NS * (NE - 1)].rearrange("p (j e) -> p j e", j=NS)
            own.done(nc.vector.tensor_tensor(jt, R_j[:, 0:NS, None].to_broadcast([P, NS, NE - 1]),
                                             ends[:, None, 0:NE - 1].to_broadcast([P, NS, NE - 1]), ALU.is_ge))
            tex = R_c[:, 96:96 + NS]
            own.done(nc.vector.tensor_reduce(tex, jt, AX.X, ALU.add))
            own.done(nc.vector.tensor_copy(texp[:], tex))
            own.done(nc.vector.tensor_scalar(selc[:], tex[0:3 * NE], rmod, None, ALU.is_equal))
            own.done(nc.vector.tensor_tensor(R_a, R_b, R_a, ALU.subtract))
            own.done(nc.vector.scalar_tensor_tensor(eg(R_a), base[:, :, None].to_broadcast([P, NE, NG]), float(P),
                                                    eg(R_a), ALU.mult, ALU.add))
            ge = R_b.rearrange("p (g e) -> p g e", g=NG)
            own.done(nc.vector.tensor_tensor(ge, PS[:, 4, 0:GE].rearrange("p (g e) -> p g e", g=NG),
                                             R_a.rearrange("p (e g) -> p g e", e=NE), ALU.add))
            own.done(nc.vector.tensor_tensor(ge, ge, R_M, ALU.mult))
            own.done(nc.vector.tensor_reduce(R_c[:, 144:144 + NG], ge, AX.X, ALU.add))
            nc.vector.tensor_copy(slot[:], R_c[:, 144:144 + NG]).then_inc(r["routed"], 1)
            dve.wait_ge(r["exp_out"], 2 if L else 1)
            gate = TG[:, 2 + L:3 + L]
            own.done(nc.vector.tensor_scalar(R_c[:, 0:NT], wgt[:, 0], 1.0, None, ALU.add))
            own.done(nc.vector.reciprocal(R_c[:, 16:16 + NT], R_c[:, 0:NT]))
            own.done(nc.vector.scalar_tensor_tensor(wgt[:, 1], wgt[:, 0], gate, R_c[:, 16:16 + NT], ALU.mult,
                                                    ALU.mult))
            own.done(nc.vector.tensor_scalar(wgt[:, 0], R_c[:, 16:16 + NT], gate, None, ALU.mult))
            if L:
                own.done(nc.vector.tensor_scalar(R_c[:, 0:NT], wgt[:, 2], 1.0, None, ALU.add))
                own.done(nc.vector.reciprocal(R_c[:, 16:16 + NT], R_c[:, 0:NT]))
                own.done(nc.vector.tensor_scalar(wgt[:, 2], R_c[:, 16:16 + NT], gate, None, ALU.mult))

        def dve_experts(dve, L):
            e, n = E[L], NS + (NT if L else 0)

            def select(w, i, u, later=True):
                if later:
                    dve.wait_ge(e["yt_ready"], i - 1) if w else dve.wait_ge(e["h_ready"], i * 2 - 2)
                nc.vector.tensor_copy(SEL[:, w, u], selc[:, bass.ds(i, 1)].to_broadcast([3 * NE, P])
                                      ).then_inc(e["sel_down" if w else "sel_up"], 1)

            def multiply(i, u, later=True):
                dve.wait_ge(e["h_act"], i + 1)
                dve.wait_ge(e["h_ready"], i * 2 + 2)
                if later:
                    dve.wait_ge(e["h_t"], i - 1)
                nc.vector.tensor_tensor(FB[L]["H"][:, u, 512:512 + F1], PS[:, 2 * u + 1, 0:F1], FB[L]["H"][:, u, 0:F1],
                                        ALU.mult).then_inc(e["h_mul"], 1)

            def keep_ht(i, u, later=True):
                dve.wait_ge(e["h_t"], i + 1)
                if later:
                    dve.wait_ge(e["yt_ready"], i - 1)
                if L:
                    for c, (_, w) in enumerate(C1):
                        last = nc.vector.tensor_copy(FB[L]["HT"][0:w, u, c], PS[0:w, 4, c * P:(c + 1) * P])
                    last.then_inc(e["ht_copied"], 1)
                else:
                    nc.vector.tensor_copy(FB[L]["HT"][:, u], PS[:, 4:6].rearrange("p b (c q) -> p (b c) q", c=4)
                                          ).then_inc(e["ht_copied"], 1)

            def keep_y(h, u):
                dve.wait_ge(e["yt_ready"], h * 2 + u + 1)
                if not (isinstance(h, int) and h == 0):
                    dve.wait_ge(e[f"y_stored_{u}"], h * 16)
                nc.vector.tensor_copy(FB[L]["Y"][:, u], PS[:, 6, 0:D]).then_inc(e["y_copied"], 1)

            def step(h, u):
                i = h * 2 + u
                first, last = (isinstance(i, int) and i == k for k in (0, n - 1))
                hp, up = (h, 0) if u else (h - 1, 1)
                if not L and not last:
                    select(0, i + 1, 1 - u, later=not (isinstance(i, int) and i < 1))
                if not L and not first:
                    select(1, i - 1, up, later=not (isinstance(i, int) and i < 3))
                if not first:
                    keep_ht(i - 1, up, later=not (isinstance(i, int) and i < 3))
                if L:
                    multiply(i, u, later=not (isinstance(i, int) and i < 2))
                if not first:
                    keep_y(hp, up)

            if not L:
                select(0, 0, 0, later=False)
            over_tiles(dve, L, step)
            if not L:
                select(1, n - 1, (n - 1) % 2)
            keep_ht(n - 1, (n - 1) % 2)
            keep_y((n - 1) // 2, (n - 1) % 2)
            with dve.Fori(0, NT // RING) as j:
                own = Chain(dve, e["own"], j, RING * (1 + L))
                for k in range(RING):
                    xt = X[:, bass.ds(j * (RING * D) + k * D, D)]
                    dve.wait_ge(e[f"gathered_{k}"], j * (16 * (2 + L)) + 16 * (2 + L))
                    for c in range(2 + L):
                        ins = nc.vector.scalar_tensor_tensor(xt, YG[:, k, c],
                                                             wgt[:, c, bass.ds(j * RING + k, 1)], xt,
                                                             ALU.mult, ALU.add)
                        if c < 1 + L:
                            own.done(ins)
                    ins.then_inc(e["combined"], 1)
                own.close()
            dve.wait_ge(e["combined"], NT)

        @block.vector
        def _(dve):
            count_from_one(dve, "dve")
            own = Chain(dve, U["own_dve"])
            dve.wait_ge(U["bias_loaded"], 96)
            dve.wait_ge(U["consts_set"], 1)
            own.done(nc.vector.tensor_copy(bpb0, bst))
            own.done(nc.vector.tensor_tensor(bpa0, bst, bpb0, ALU.subtract))
            own.done(nc.vector.tensor_copy(bpb1, bpa0))
            own.done(nc.vector.tensor_tensor(bpa1, bpa0, bpb1, ALU.subtract))
            own.done(nc.vector.tensor_scalar(bpa2, bpb0, bm[:, 0:1], None, ALU.mult))
            own.done(nc.vector.scalar_tensor_tensor(bpa0, bpb1, bm[:, 1:2], bpa2, ALU.mult, ALU.add))
            own.done(nc.vector.scalar_tensor_tensor(b1t[:], bpa1[:, 0:F0], bm[:, 2:3], bpa0[:, 0:F0],
                                                    ALU.mult, ALU.add))
            own.done(nc.vector.scalar_tensor_tensor(b2t[:], bpa1[:, F0:], bm[:, 2:3], bpa0[:, F0:],
                                                    ALU.mult, ALU.add))
            own.done(nc.vector.scalar_tensor_tensor(rmod, bm[:, 1:2], -float(NE), prow, ALU.mult, ALU.add))
            own.done(nc.vector.scalar_tensor_tensor(rmod, bm[:, 2:3], -2.0 * NE, rmod, ALU.mult, ALU.add))
            dve.wait_ge(U["x_loaded"], 32)
            dve.wait_ge(U["rows_zeroed"], 48)
            dve.wait_ge(U["ctx_copied"], 1)
            dve_attention(dve, 0)
            dve_router(dve, 0, Chain(dve, R[0]["router_own"]))
            dve_experts(dve, 0)
            dve.wait_ge(U["w1_copied"], 1)
            dve_attention(dve, 1)
            dve_router(dve, 1, Chain(dve, R[1]["router_own"]))
            dve_experts(dve, 1)

        def pe_attention(pe, L):
            a, r = A[L], R[L]
            nh = 1 if L else 2
            f_of = (lambda f: 0) if L else (lambda f: f)

            def turn(b, n):
                after(pe, a["ln_done"], b * (2 * GB) + n + 1)
                after(pe, a["x_t_copied"], b * (2 * GB) + n)
                if n == GB:
                    after(pe, a["k_built"], b + 1)
                for q in range(QT_):
                    for k in range(KC):
                        last = nc.tensor.transpose(PS[:, k, q * P:(q + 1) * P], XNA[:, q, k * P:(k + 1) * P],
                                                   ident[:])
                last.then_inc(a["x_t"], 1)
                after(pe, a["x_t_copied"], b * (2 * GB) + n + 1)

            with pe.Fori(0, NB) as b:
                for g in range(GB):
                    turn(b, g)
                    after(pe, a["smax_used"], b * (GB * 4 * QT_))
                    after(pe, a["q_copied"], b * GB + g)
                    for f in range(2):
                        for k in range(KC):
                            last = nc.tensor.matmul(PS[:, 2 + f], AW[:, k, f * P:(f + 1) * P], XNT[:, k],
                                                    start=k == 0, stop=k == KC - 1)
                    last.then_inc(a["q_ready"], 1)
                    if L:
                        after(pe, a["q_copied"], b * GB + g + 1)
                        after(pe, a["logits_copied"], b * GB)
                        after(pe, a["x_added"], b * NTB)
                        for q in range(QT_):
                            after(pe, a["s77_used"], b * NTB + max(g * QT_ + q - 1, 0))
                            for f in range(2):
                                last = nc.tensor.matmul(PS[:, 6 + q % 2, 0:NK], QF[:, g, f, q * P:(q + 1) * P],
                                                        CT[:, f, bass.ds(b * NK, NK)], start=f == 0, stop=f == 1)
                            last.then_inc(a["s77"], 1)
                for f in range(nh):
                    for k in range(KC):
                        last = nc.tensor.matmul(PS[:, f, 0:NK], AW[:, k, D + f * P:D + (f + 1) * P],
                                                CT[:, k, bass.ds(b * NK, NK)], start=k == 0, stop=k == KC - 1)
                last.then_inc(a["k_ready"], 1)
                if L:
                    after(pe, a["counted"], b + 1)
                    after(pe, a["s77_used"], b * NTB + NTB)
                    for j in range(JT):
                        nc.tensor.matmul(PS[:, 6, j:j + 1], SR[:, j * P:(j + 1) * P], onec[:], start=True, stop=True)
                    for w in range(2):
                        last = nc.tensor.matmul(PS[0:1, 2 + w, 0:QK], onec[:], SR[:, w * QK:(w + 1) * QK],
                                                start=True, stop=True)
                    last.then_inc(a["c_ready"], 1)
                after(pe, a["ctx_rep"], b + 1)
                for f in range(nh):
                    after(pe, a["v_built"], b * nh + f)
                    for j in range(JT):
                        for k in range(KC):
                            last = nc.tensor.matmul(PS[0:ROWS[j], 4 + j // 4, (j % 4) * P:(j % 4 + 1) * P],
                                                    CR[:, k, j * P:j * P + ROWS[j]],
                                                    AW[:, k, 2 * D + f * P:2 * D + (f + 1) * P],
                                                    start=k == 0, stop=k == KC - 1)
                    last.then_inc(a["v_ready"], 1)
                after(pe, a["kb_copied"], b + 1)
                if L:
                    after(pe, a["cnt_bias"], b + 1)
                for g in range(GB):
                    n0 = b * GB + g
                    after(pe, a["qb_copied"], n0 + 1)
                    for i in range(4 * QT_):
                        q, c = i // 4, i % 4
                        after(pe, a["smax_used"], n0 * (4 * QT_) + max(i - 1, 0))
                        cols = slice(c % 2 * QK, (c % 2 + 1) * QK)
                        last = nc.tensor.matmul(PS[:, 2 + i % 2, 0:QK], QB[:, c // 2, q * P:(q + 1) * P],
                                                KB[:, f_of(c // 2), cols], start=True, stop=not L)
                        if L:
                            last = nc.tensor.matmul(PS[:, 2 + i % 2, 0:QK], onesb[0:1], used[:, cols],
                                                    start=False, stop=True)
                        last.then_inc(a["smax"], 1)
                    after(pe, a["smax_used"], n0 * (4 * QT_) + 4 * QT_)
                    after(pe, a["o_t_copied"], n0 * QT_)
                    if g == 0:
                        after(pe, a["k_built"], b + 1)
                    for q in range(QT_):
                        last = nc.tensor.transpose(PS[0:H, 0, 0:G // 2].bitcast(BF16)[:, q * P:(q + 1) * P],
                                                   MX[:, q], identb[:])
                    last.then_inc(a["mx_t"], 1)
                    after(pe, a["mx_copied"], n0 + 1)
                    if g == 0:
                        after(pe, a["v_built"], b * nh + nh)
                    for i in range(2 * JT):
                        f, j = i // JT, i % JT
                        rows = ROWS[j]
                        after(pe, a["exp_done"], n0 * (2 * JT) + max(i - 1, 0))
                        nc.tensor.matmul(PS[0:rows, 4 + i % 2], KF[:, f_of(f), j * P:j * P + rows], QF[:, g, f],
                                         start=True, stop=False)
                        nc.tensor.matmul(PS[0:rows, 4 + i % 2], IND[:, f, j * P:j * P + rows], MT,
                                         start=False, stop=True).then_inc(a["s_ready"], 1)
                    after(pe, a["exp_done"], n0 * (2 * JT) + 2 * JT)
                    for s in range(QT_ + 2):
                        if s < QT_:
                            after(pe, a["o_done"], n0 * QT_ + max(s - 1, 0))
                            for f in range(2):
                                for j in range(JT):
                                    last = nc.tensor.matmul(
                                        PS[:, 6 + s % 2, f * HH * VW:(f + 1) * HH * VW],
                                        PR[0:ROWS[j], f * JT + j, s * P:(s + 1) * P],
                                        VF[0:ROWS[j], f_of(f), j].rearrange("p h v -> p (h v)"),
                                        start=j == 0, stop=j == JT - 1)
                            last.then_inc(a["o_ready"], 1)
                        if s >= 2:
                            u = s % 2
                            after(pe, a["o_t_copied"], n0 * QT_ + s - 1)
                            after(pe, a["x_added"], n0 * QT_ + s - 2)
                            for k in range(KC):
                                last = nc.tensor.matmul(PS[:, 1, 0:D], OT[:, u, k], AW[:, k, 3 * D:4 * D],
                                                        start=k == 0, stop=k == KC - 1)
                            last.then_inc(a["y_ready"], 1)
                        if 1 <= s <= QT_:
                            after(pe, a["o_done"], n0 * QT_ + s)
                            after(pe, a["o_t_copied"], n0 * QT_ + s - 1)
                            for k in range(KC):
                                last = nc.tensor.transpose(PS[:, 0, k * P:(k + 1) * P],
                                                           OA[:, (s - 1) % 2, k * P:(k + 1) * P], ident[:])
                            last.then_inc(a["o_t"], 1)
                for g in range(GB):
                    turn(b, GB + g)
                    after(pe, a["logits_copied"], b * GB + g)
                    after(pe, a["o_done"], b * NTB + NTB)
                    w = NW[L]
                    for q in range(QT_):
                        for k in range(KC):
                            last = nc.tensor.matmul(PS[:, 6, q * w:(q + 1) * w], XNT[:, k, q * P:(q + 1) * P],
                                                    gwt[:, k, 0:w], start=k == 0, stop=k == KC - 1)
                    last.then_inc(a["logits"], 1)
            pe.wait_ge(r["onehot"], TOPK)
            pe.wait_ge(r["r_consts"], 7)
            nc.tensor.matmul(PS[:, 4, 0:GE], R_u, R_M.rearrange("p g e -> p (g e)"), start=True, stop=True)
            nc.tensor.matmul(PS[:, 5, 0:GE], R_1, R_M.rearrange("p g e -> p (g e)"), start=True,
                             stop=True).then_inc(r["totals"], 1)

        def pe_experts(pe, L):
            e, n, lead = E[L], NS + (NT if L else 0), (NT if L else 0)
            hw = F1 if L else 512

            held = [pe.alloc_register(f"expert{u}_{L}") for u in range(2)]

            def look_up(i, u):
                pe.reg_load(held[u], texp[0:1, bass.ds(i - lead, 1)])

            def expert(u, shared):
                return NE if shared else pe.snap(held[u], min_val=0, max_val=NE - 1)

            def turn(h, u):
                i = h * 2 + u
                pe.wait_ge(e[f"xs_loaded_{u}"], h * 16 + 16)
                pe.wait_ge(e["xt_copied"], i)
                for k in range(KC):
                    last = nc.tensor.transpose(PS[:, 7, k * P:(k + 1) * P], FB[L]["XS"][:, u, k * P:(k + 1) * P], ident[:])
                last.then_inc(e["xs_t"], 1)

            def up(i, u, s, ex, later):
                if later:
                    if L:
                        pe.wait_ge(e["h_mul" if s else "h_act"], i - 1)
                    else:
                        pe.wait_ge(e["h_act"], i * 2 + s - 3)
                for k in range(KC):
                    if L:
                        rhs = W1a[:, bass.ds(ex * WG1 + (s * KC + k) * F1, F1)]
                    else:
                        rhs = W0a[:, bass.ds(ex * W0E + k * F0 + s * 512, 512)]
                    last = nc.tensor.matmul(PS[:, 2 * u + s, 0:hw], FB[L]["XT"][:, u, k], rhs, start=k == 0,
                                            stop=bool(L) and k == KC - 1)
                if not L:
                    if s == 0:
                        pe.wait_ge(e["sel_up"], i + 1)
                    last = nc.tensor.matmul(PS[:, 2 * u + s], SEL[:, 0, u], b1t[:, s * 512:(s + 1) * 512],
                                            start=False, stop=True)
                last.then_inc(e["h_ready"], 1)

            def turn_hidden(i, u):
                pe.wait_ge(e["h_mul"], i + 1) if L else pe.wait_ge(e["h_act"], i * 2 + 2)
                pe.wait_ge(e["ht_copied"], i)
                for c in range(3 if L else FC0):
                    if L:
                        at, w = C1[c]
                        last = nc.tensor.transpose(PS[0:w, 4, c * P:(c + 1) * P], FB[L]["H"][:, u, 512 + at:512 + at + w], ident[:])
                    else:
                        last = nc.tensor.transpose(PS[:, 4 + c // 4, c % 4 * P:(c % 4 + 1) * P],
                                                   FB[L]["H"][:, u, c * P:(c + 1) * P], ident[:])
                last.then_inc(e["h_t"], 1)

            def down(i, u, ex):
                pe.wait_ge(e["ht_copied"], i + 1)
                pe.wait_ge(e["y_copied"], i)
                nch = 3 if L else FC0
                for c in range(nch):
                    w = C1[c][1] if L else P
                    base = W1b[0:w, bass.ds(ex * WD1 + c * D, D)] if L else W0b[:, bass.ds(ex * W0E + c * D, D)]
                    last = nc.tensor.matmul(PS[:, 6, 0:D], FB[L]["HT"][0:w, u, c], base, start=c == 0,
                                            stop=bool(L) and c == nch - 1)
                if not L:
                    pe.wait_ge(e["sel_down"], i + 1)
                    last = nc.tensor.matmul(PS[:, 6, 0:D], SEL[:, 1, u], b2t[:], start=False, stop=True)
                last.then_inc(e["yt_ready"], 1)

            def step(h, u):
                i = h * 2 + u
                fixed = isinstance(i, int)
                now = L == 1 and (i < lead if fixed else loops[0] == 0)
                before = L == 1 and (i <= lead if fixed else loops[0] == 0)
                ex = expert(u, now)
                pe.wait_ge(e["xt_copied"], i + 1)
                later = not (fixed and i < 2)
                up(i, u, 0, ex, later)
                if not (fixed and i == 0):
                    turn_hidden(i - 1, 1 - u)
                up(i, u, 1, ex, later)
                if not (fixed and i == n - 1):
                    turn(*((h, 1) if u == 0 else (h + 1, 0)))
                if not (fixed and i == 0):
                    down(i - 1, 1 - u, expert(1 - u, before))
                if L and fixed and i == lead - 1:
                    pe.wait_ge(R[1]["routed"], 1)
                if not fixed and loops[0] or not L or fixed and lead - 1 <= i:
                    if not (fixed and i == n - 1):
                        look_up(i + 1, 1 - u)
                if not fixed and u == 1:
                    loops[0] += 1

            loops = [0]
            pe.wait_ge(U["w1_loaded"] if L else U["w0_loaded"], 16 * (4 * (NE + 1) if L else 2 * NE))
            turn(0, 0)
            if not L:
                pe.wait_ge(R[0]["routed"], 1)
                look_up(0, 0)
            over_tiles(pe, L, step)
            turn_hidden(n - 1, (n - 1) % 2)
            down(n - 1, (n - 1) % 2, expert((n - 1) % 2, False))

        @block.tensor
        def _(pe):
            count_from_one(pe, "pe")
            pe.wait_ge(U["ctx_loaded"], 16)
            pe.wait_ge(U["consts_set"], 1)
            for b in range(NB):
                for k in range(KC):
                    last = nc.tensor.transpose(PS[:, 0, (k * NB + b) * NK:(k * NB + b + 1) * NK],
                                               ctx_raw[:, b, k * P:(k + 1) * P], ident[0:NK, 0:NK])
            last.then_inc(U["ctx_t"], 1)
            pe.wait_ge(U["ctx_copied"], 1)
            pe.wait_ge(U["attn_w_loaded"], 32)
            pe.wait_ge(U["gate_w_loaded"], 16)
            pe_attention(pe, 0)
            pe_experts(pe, 0)
            pe.wait_ge(U["w1_raw_loaded"], 80)
            pe.wait_ge(E[0]["y_copied"], NS)
            for k in range(KC):
                for c in range(2):
                    nc.tensor.transpose(PS[:, k, c * P:(c + 1) * P], rq[:, c, k * P:(k + 1) * P], ident[:])
                    nc.tensor.transpose(PS[:, 2 + k, c * P:(c + 1) * P], rc[:, c, k * P:(k + 1) * P], ident[:])
                nc.tensor.transpose(PS[:, 4 + k, 0:2 * HD], rkv[:, k * P:(k + 1) * P], ident[0:2 * HD, 0:2 * HD])
                last = nc.tensor.transpose(PS[:, 6 + k, 0:NE + 1], rg[:, k * P:(k + 1) * P],
                                           ident[0:NE + 1, 0:NE + 1])
            last.then_inc(U["w1_t"], 1)
            pe.wait_ge(U["w1_copied"], 1)
            pe_attention(pe, 1)
            pe_experts(pe, 1)


_INS = ['x', 'ctx_1024', 'g_xattn', 'g_ffn', 'L0_xattn_W_qkv', 'L0_xattn_W_proj', 'L0_xattn_b_proj',
        'L0_ffn_gate_w', 'L0_ffn_w1', 'L0_ffn_b1', 'L0_ffn_w2', 'L0_ffn_b2', 'L1_xattn_Wq', 'L1_xattn_Wkv',
        'L1_xattn_Wc', 'L1_ffn_gate_w', 'L1_ffn_w_gate', 'L1_ffn_w_up', 'L1_ffn_w_down', 'L1_ffn_sw_gate',
        'L1_ffn_sw_up', 'L1_ffn_sw_down', 'L1_ffn_shared_gate_w']
_OUTS = [((NB, S, D), 'float32')]


def kernel(**inputs):
    import numpy as _np
    import concourse.bacc as _bacc
    from concourse import mybir as _mybir
    from concourse.bass_utils import run_bass_kernel_spmd as _run

    nc = _bacc.Bacc("TRN2", target_bir_lowering=False, num_devices=1)
    arrays, args = {}, []
    for name in _INS:
        a = _np.ascontiguousarray(inputs[name])
        arrays[f"in_{name}_dram"] = a
        args.append(nc.dram_tensor(f"in_{name}_dram", a.shape, _mybir.dt.from_np(a.dtype), kind="ExternalInput").ap())
    for i, (shape, dtype) in enumerate(_OUTS):
        dt = _mybir.dt.from_np(_np.dtype(dtype))
        args.append(nc.dram_tensor(f"out_{i}_dram", shape, dt, kind="ExternalOutput").ap())
    program(nc, *args)
    r = _run(nc, [arrays], core_ids=[0])
    return r.results[0]["out_0_dram"]
```

```python
from contextlib import ExitStack

import concourse.bass as bass
from concourse import mybir

F32 = mybir.dt.float32
BF16 = mybir.dt.bfloat16
I32 = mybir.dt.int32
U32 = mybir.dt.uint32
ALU = mybir.AluOpType
ACT = mybir.ActivationFunctionType
AX = mybir.AxisListType

P = 128
NB, S, D = 2, 1024, 256
NK = 77
H, HD = 16, 16
T = NB * S
NT = T // P
KC = D // P
G = 512
QT_ = G // P
GB = S // G
HH = H // 2
HK = HH * NK
JT = -(-HK // P)
ROWS = [min(P, HK - P * j) for j in range(JT)]
QK = HK // 2
VW = HD + 1
SCALE = HD ** -0.5
EPS = 1e-5
NE, TOPK = 8, 2
F0, F1 = 1024, 352
FC0 = F0 // P
C1 = [(0, 128), (128, 128), (256, 96)]
NS = (T * TOPK + NE * (P - 1)) // P
NG = NT * TOPK
W0E = KC * F0
WG1, WD1 = KC * 2 * F1, 3 * D
BIG = 1.0e30
LATE = 5
YG0 = (NE + LATE) * W0E - NT * TOPK * D


class Chain:

    def __init__(self, eng, sem, base=0, per=0):
        self.eng, self.sem, self.base, self.per, self.n = eng, sem, base, per, 0

    def done(self, ins, after=None):
        self.n += 1
        ins.then_inc(self.sem, 1)
        self.eng.wait_ge(self.sem, self.base * self.per + self.n if self.per else self.n)
        if after:
            after(self.eng)

    def close(self):
        assert self.n == self.per, self.n


def runs(L):
    n = NS + (NT if L else 0)
    found = [("one", i, 0) for i in range(4)]
    if L:
        found += [("loop", 2, NT // 2 - 1)] + [("one", i, 0) for i in range(NT - 2, NT + 4)]
        found += [("loop", NT // 2 + 2, (n - 1) // 2)]
    else:
        found += [("loop", 2, (n - 1) // 2)]
    return found + [("one", i, 0) for i in range((n - 1) // 2 * 2, n)]


def over_tiles(eng, L, step):
    for kind, a, b in runs(L):
        if kind == "loop":
            with eng.Fori(a, b) as h:
                step(h, 0)
                step(h, 1)
        else:
            step(a // 2, a % 2)


def program(nc, x, ctx, g_xattn, g_ffn, wqkv0, wproj0, bproj0, gate0, w1, b1, w2, b2,
            wq1, wkv1, wc1, gate1, wg1, wu1, wd1, swg, swu, swd, sgw, out):
    with ExitStack() as stack:
        def sb(name, shape, dt=F32):
            return stack.enter_context(nc.sbuf_tensor(name, shape, dt))

        def sem(name):
            return stack.enter_context(nc.semaphore(name))

        def sems(names, suffix):
            return {k: sem(k + suffix) for k in names.split()}

        xslots = nc.dram_tensor("xslots", [(NS + NT) * P, D], F32).ap()
        yslots = nc.dram_tensor("yslots", [NS * P, D], F32).ap()
        X = sb("X", [P, NT * D])
        XN = sb("XN", [P, NT * D])
        W = sb("W", [P, 2 * NE * W0E])
        AW = sb("AW", [P, KC, 4 * D])
        CT = sb("CT", [P, KC, NB * NK])
        ident = sb("ident", [P, P])
        identb = sb("identb", [P, P], BF16)
        TG = sb("TG", [P, 4])
        blockm = sb("blockm", [P, HH])
        maskv = sb("maskv", [P, JT, HH])
        maskc = sb("maskc", [P, JT, HH])
        b1t = sb("b1t", [3 * NE, F0], BF16)
        b2t = sb("b2t", [3 * NE, D], BF16)
        gwt = sb("gwt", [P, KC, NE + 1])
        slot = sb("slot", [P, NG], U32)
        wgt = sb("wgt", [P, 3, NT])
        texp = sb("texp", [P, NS], I32)
        selc = sb("selc", [3 * NE, NS])
        onesb = sb("onesb", [24, P], BF16)
        onec = sb("onec", [P, 1])
        small = sb("small", [P, 128])
        arena = sb("arena", [P, 7936])
        PS = stack.enter_context(nc.psum_tensor("PS", [P, 8, 512], F32))

        STAT = small[:, 0:24].rearrange("p (t s) -> p t s", t=QT_)
        MV = small[:, 24:32].rearrange("p (t s) -> p t s", t=QT_)
        RSTD, VEPS, HALF = small[:, 32:36], small[:, 36:40], small[:, 40:44]
        RD = [small[:, 44:60], small[:, 104:120]]
        mark = small[:, 124:128]
        CNT = small[:, 60:65]
        KBI = small[:, 65:70]
        rmod = small[0:3 * NE, 70:71]
        prow = small[0:3 * NE, 71:72]
        bm = small[0:3 * NE, 72:75]
        TOP = small[:, 80:88]
        TOPI = small[:, 88:96].bitcast(U32)
        IDX = small[:, 96:97]

        iota77 = sb("iota77", [P, NK])
        SQ = sb("SQ", [P, NK])

        def cutter(memory):
            at = [0]

            def take(n, dt=F32):
                at[0] += n
                assert at[0] <= memory.shape[1], (at[0], memory.shape)
                view = memory[:, at[0] - n:at[0]]
                return view if dt is F32 else view.bitcast(dt)

            return take

        take = cutter(arena)
        PR = take(10 * G).rearrange("p (s q) -> p s q", s=2 * JT)
        CR = arena[:, 0:2 * HK].rearrange("p (k n) -> p k n", k=KC)
        SR = arena[:, 3 * G:3 * G + JT * P]
        XNT = arena[:, 6 * G:8 * G].rearrange("p (k q) -> p k q", k=KC)
        XNA = arena[:, 8 * G:10 * G].rearrange("p (t d) -> p t d", t=QT_)
        QF = take(GB * KC * G).rearrange("p (g k q) -> p g k q", g=GB, k=KC)
        LG = take(NT * (NE + 1))
        IND = take(HK, BF16).rearrange("p (f n) -> p f n", f=2)[0:H]
        take = cutter(W[:, (NE + LATE) * W0E:])
        KF = take(2 * HK).rearrange("p (f n) -> p f n", f=2)
        KB = take(HK, BF16).rearrange("p (f n) -> p f n", f=2)
        VF = take(2 * JT * HH * VW).rearrange("p (f j h v) -> p f j h v", f=2, j=JT, h=HH)
        QB = take(KC * G // 2, BF16).rearrange("p (k q) -> p k q", k=KC)
        MX = take(QT_ * H // 2, BF16).rearrange("p (t h) -> p t h", t=QT_)
        MT = take(G // 2, BF16)[0:H]
        OA = take(2 * D).rearrange("p (u d) -> p u d", u=2)
        OT = take(2 * D).rearrange("p (u k q) -> p u k q", u=2, k=KC)
        bproj = take(D)
        RT = take(2 * D).rearrange("p (u k q) -> p u k q", u=2, k=KC)
        used = take(HK // 2, BF16)[0:1]

        take = cutter(arena)
        GE = NG * NE
        R_M = take(GE).rearrange("p (g e) -> p g e", g=NG)
        R_a, R_b, R_c, R_d = take(GE), take(GE), take(GE), take(320)
        R_u, R_1, R_i, R_rs, R_j = take(P), take(P), take(NT * NE), take(GE), take(NS + 1)

        FB = []
        for L in range(2):
            take = cutter(W[:, (NE + 1) * (WG1 + WD1):] if L else arena)
            FB.append({
                "H": take(2 * F0).rearrange("p (u n) -> p u n", u=2),
                "HT": take(2 * F0).rearrange("p (u c q) -> p u c q", u=2, c=FC0),
                "XS": take(2 * D).rearrange("p (u d) -> p u d", u=2),
                "XT": take(2 * D).rearrange("p (u k q) -> p u k q", u=2, k=KC),
                "Y": take(2 * D).rearrange("p (u d) -> p u d", u=2)})
        SEL = AW[0:3 * NE, 0, 0:2 * P].bitcast(BF16).rearrange("p (w u q) -> p w u q", w=2, u=2)
        raw1 = arena[:, 4 * F0 + 6 * D:]
        rq = raw1[:, 0:2 * D].rearrange("p (c d) -> p c d", c=2)
        rc = raw1[:, 2 * D:4 * D].rearrange("p (c d) -> p c d", c=2)
        rkv = raw1[0:2 * HD, 4 * D:5 * D]
        rg = raw1[0:NE + 1, 5 * D:6 * D]
        YG4 = W[:, YG0:(NE + LATE) * W0E].rearrange("p (j q k d) -> p j q k d", j=NB * GB, q=QT_, k=TOPK)
        YG = W[:, YG0:(NE + LATE) * W0E].rearrange("p (t k d) -> p t k d", t=NT, k=TOPK)

        XNR = XN[:, (NT - QT_) * D:].rearrange("p (t d) -> p t d", t=QT_)
        zeros = XN[:, 0:3328]
        ctx_raw = XN[0:NK, 3400:3400 + NB * D].rearrange("p (b d) -> p b d", b=NB)
        bw = F0 + D
        bst, bpa0, bpa1, bpa2 = [arena[0:3 * NE, bw * i:bw * (i + 1)] for i in range(4)]
        bpb0, bpb1 = [arena[0:3 * NE, bw * i:bw * i + bw // 2].bitcast(BF16) for i in (4, 5)]
        Xt = X[:, :].rearrange("p (t d) -> p t d", t=NT)
        XNt = XN[:, :].rearrange("p (t d) -> p t d", t=NT)
        xtile = x.rearrange("b (t p) d -> p (b t) d", p=P)
        otile = out.rearrange("b (t p) d -> p (b t) d", p=P)
        W0a, W0b = W[:, 0:NE * W0E], W[:, NE * W0E:2 * NE * W0E]
        W1a, W1b = W[:, 0:(NE + 1) * WG1], W[:, (NE + 1) * WG1:(NE + 1) * (WG1 + WD1)]
        NW = [NE, NE + 1]
        NTB = S // P

        def tile_at(b, g, q=0):
            return b * (NTB * D) + (g * QT_ + q) * D

        U = sems("x_loaded ctx_loaded attn_w_loaded bias_loaded gates_loaded gate_w_loaded waits_settled zeros_set rows_zeroed "
                 "consts_set bias_split ctx_t ctx_copied tanh_done bproj_ready own_pool own_dve w0_loaded "
                 "w1_loaded w1_raw_loaded w1_t w1_copied out_stored", "")
        A = [sems("own_dve own_pool stats rstd ln_done x_t x_t_copied q_ready q_copied s77 s77_used counted "
                  "c_ready cnt_bias ctx_rep k_ready k_built kb_copied qb_copied v_ready v_built smax smax_used "
                  "mx_t mx_copied s_ready exp_done o_ready o_done o_t o_t_copied y_ready x_added xb_added xn_kept "
                  "row_used logits_copied", str(L)) for L in range(2)]
        R = [sems("router_on r_consts onehot totals exp_in exp_out routed scattered router_own " + ("shared_stored" if L else ""), str(L))
             for L in range(2)]
        E = [sems("xs_loaded_0 xs_loaded_1 xs_t xt_copied h_ready h_act h_t ht_copied yt_ready "
                  "y_copied y_stored_0 y_stored_1 gathered_0 gathered_1 combined " + ("h_mul gathered_2 gathered_3 own" if L else
                                                                        "sel_up sel_down"), str(L))
             for L in range(2)]

        block = stack.enter_context(nc.Block())

        def settle(eng):
            eng.sem_inc(U["waits_settled"], 1)

        def after(eng, semaphore, n):
            eng.wait_ge(semaphore, n + 1)

        TURNS = GB + NTB
        R_AT = 4

        def first_maxima(nh, f, j):
            n, at = 4 * QT_, f * JT + j
            return range(n * at // (nh * JT), n * (at + 1) // (nh * JT))

        CREDITS = {
            "pool": "rstd xb_added xn_kept",
            "act": "x_t_copied q_copied kb_copied qb_copied mx_copied exp_done o_t_copied logits_copied",
            "dve": "stats ln_done s77_used counted cnt_bias ctx_rep k_built v_built smax_used o_done x_added",
            "pe": "x_t q_ready s77 c_ready k_ready v_ready smax mx_t s_ready o_ready o_t y_ready row_used"}

        def count_from_one(eng, name):
            for L in range(2):
                for k in CREDITS[name].split():
                    eng.sem_inc(A[L][k], 1)

        def experts_io(sp, L):
            e, n = E[L], NS + (NT if L else 0)

            def row(h, u, shared):
                if shared:
                    return h * (2 * P) + (NS + u) * P
                return h * (2 * P) + (u - (NT if L else 0)) * P

            def load(h, u, first=False):
                shared = at[0] == "shared"
                if not first:
                    sp.wait_ge(e["xs_t"], h * 2 + u - 1)
                sp.dma_start(FB[L]["XS"][:, u], xslots[bass.ds(row(h, u, shared), P)]).then_inc(e[f"xs_loaded_{u}"], 16)

            def store(h, u):
                sp.wait_ge(e["y_copied"], h * 2 + u + 1)
                sp.dma_start(yslots[bass.ds(row(h, u, False), P)], FB[L]["Y"][:, u]).then_inc(e[f"y_stored_{u}"], 16)

            at = ["shared" if L else "routed"]
            if L:
                sp.wait_ge(R[1]["shared_stored"], 16)
                sp.wait_ge(R[1]["router_on"], 1)
            else:
                sp.wait_ge(R[0]["scattered"], 16 * NG)
            for u in range(2):
                load(0, u, first=True)
            for u in range(2):
                load(1, u)
            lo = 2
            if L:
                with sp.Fori(2, NT // 2) as h:
                    for u in range(2):
                        load(h, u)
                sp.wait_ge(R[1]["scattered"], 16 * NG)
                at[0] = "routed"
                lo = NT // 2 + 2
                for h in range(NT // 2, lo):
                    for u in range(2):
                        load(h, u)
            with sp.Fori(lo, n // 2) as h:
                for u in range(2):
                    load(h, u)
                    store(h - 2, u)
            if n % 2:
                load(n // 2, 0)
            for i in range(n // 2 * 2 - 4, n):
                store(i // 2, i % 2)

        @block.sync
        def _(sp):
            sp.dma_start(Xt[:, 0:NTB], xtile[:, 0:NTB]).then_inc(U["x_loaded"], 16)
            sp.dma_start(ctx_raw, ctx.rearrange("b k d -> k b d")).then_inc(U["ctx_loaded"], 16)
            sp.dma_start(AW[:, :, 0:3 * D], wqkv0.rearrange("(k p) n -> p k n", p=P)).then_inc(U["attn_w_loaded"], 16)
            sp.dma_start(AW[:, :, 3 * D:], wproj0.rearrange("(k p) n -> p k n", p=P)).then_inc(U["attn_w_loaded"], 16)
            sp.wait_ge(U["x_loaded"], 16)
            sp.dma_start(Xt[:, NTB:], xtile[:, NTB:]).then_inc(U["x_loaded"], 16)
            sp.wait_ge(U["attn_w_loaded"], 32)
            sp.wait_ge(U["zeros_set"], 1)
            z = xslots[0:NS * P].rearrange("(p r) d -> p (r d)", p=P)
            for i in range(3):
                sp.dma_start(z[:, i * 3328:(i + 1) * 3328], zeros).then_inc(U["rows_zeroed"], 16)

            def load_w1(e):
                sp.dma_start(W0a[:, bass.ds(e * W0E, W0E)].rearrange("p (k n) -> p k n", k=KC),
                             w1[bass.ds(e, 1)].rearrange("e (k p) n -> p (e k) n", p=P)).then_inc(U["w0_loaded"], 16)

            def load_w2(e):
                sp.dma_start(W0b[:, bass.ds(e * W0E, W0E)].rearrange("p (c n) -> p c n", c=FC0),
                             w2[bass.ds(e, 1)].rearrange("e (c p) n -> p (e c) n", p=P)).then_inc(U["w0_loaded"], 16)

            with sp.Fori(0, LATE) as e:
                load_w1(e)
                load_w2(e)
            with sp.Fori(LATE, NE) as e:
                load_w1(e)
            sp.wait_ge(R[0]["totals"], 1)
            with sp.Fori(LATE, NE) as e:
                load_w2(e)
            sp.wait_ge(R[0]["routed"], 1)
            sp.dma_start(rq, wq1.rearrange("(c p) d -> p c d", p=P)).then_inc(U["w1_raw_loaded"], 16)
            sp.dma_start(rc, wc1.rearrange("(c p) d -> p c d", p=P)).then_inc(U["w1_raw_loaded"], 16)
            sp.dma_start(rkv, wkv1).then_inc(U["w1_raw_loaded"], 16)
            sp.dma_start(rg[0:NE], gate1).then_inc(U["w1_raw_loaded"], 16)
            sp.dma_start(rg[NE:NE + 1], sgw).then_inc(U["w1_raw_loaded"], 16)
            experts_io(sp, 0)

            def up_weights(e, g_, u_):
                ga = W1a[:, bass.ds(e * WG1, WG1)].rearrange("p (w k n) -> p w k n", w=2, k=KC)
                sp.dma_start(ga[:, 0], g_.rearrange("(k p) n -> p k n", p=P)).then_inc(U["w1_loaded"], 16)
                sp.dma_start(ga[:, 1], u_.rearrange("(k p) n -> p k n", p=P)).then_inc(U["w1_loaded"], 16)

            def down_weights(e, d_):
                da = W1b[:, bass.ds(e * WD1, WD1)].rearrange("p (c n) -> p c n", c=3)
                sp.dma_start(da[:, 0:2], d_[0:2 * P].rearrange("(c p) n -> p c n", p=P)).then_inc(U["w1_loaded"], 16)
                sp.dma_start(da[0:F1 - 2 * P, 2], d_[2 * P:F1]).then_inc(U["w1_loaded"], 16)

            one = lambda w, e: w[bass.ds(e, 1)].rearrange("e a b -> (e a) b")
            sp.wait_ge(E[0]["combined"], NTB)
            up_weights(NE, swg, swu)
            with sp.Fori(0, NE) as e:
                up_weights(e, one(wg1, e), one(wu1, e))
            clear = (YG0 - NE * WG1 - WG1) // WD1
            with sp.Fori(0, clear) as e:
                down_weights(e, one(wd1, e))
            sp.wait_ge(E[0]["combined"], NT)
            with sp.Fori(clear, NE) as e:
                down_weights(e, one(wd1, e))
            down_weights(NE, swd)
            experts_io(sp, 1)
            for t in range(NT):
                sp.wait_ge(E[1]["combined"], t + 1)
                sp.dma_start(otile[:, t], Xt[:, t]).then_inc(U["out_stored"], 16)
            sp.wait_ge(U["out_stored"], 16 * NT)

        def gather(L, b):
            for t in range(b * NTB, (b + 1) * NTB):
                for c in range(TOPK):
                    g = c * NT + t
                    nc.gpsimd.indirect_dma_start(
                        YG[:, t, c], None, yslots[0:NS * P],
                        bass.IndirectOffsetOnAxis(ap=slot[:, g:g + 1], axis=0)
                    ).then_inc(E[L][f"gathered_{t // QT_ % (4 if L else 2)}"], 16)

        def pool_layer(pool, L):
            a, r, e = A[L], R[L], E[L]

            def rstd(own, n):
                after(pool, a["stats"], n)
                settle(pool)
                own.done(nc.gpsimd.tensor_scalar(VEPS, MV[:, :, 1], EPS, None, ALU.add))
                nc.gpsimd.tensor_tensor(RSTD, VEPS, HALF, ALU.pow).then_inc(a["rstd"], 1)

            own = Chain(pool, a["own_pool"])
            for b in range(NB):
                for g in range(GB):
                    rstd(own, b * (2 * GB) + g + 1)
                if L == 0:
                    after(pool, a["ln_done"], b * (2 * GB) + GB)
                    pool.wait_ge(U["bproj_ready"], 1)
                    for g in range(GB):
                        xg = X[:, tile_at(b, g):tile_at(b, g) + QT_ * D].rearrange("p (t d) -> p t d", t=QT_)
                        nc.gpsimd.tensor_tensor(xg, xg, bproj[:, None, :].to_broadcast([P, QT_, D]),
                                                ALU.add).then_inc(a["xb_added"], 1)
                elif b == 0:
                    gather(0, 1)
                for g in range(GB):
                    rstd(own, b * (2 * GB) + GB + g + 1)
                    after(pool, a["ln_done"], b * (2 * GB) + GB + g + 1)
                    if (b, g) != (NB - 1, GB - 1):
                        nc.gpsimd.tensor_copy(XN[:, tile_at(b, g):tile_at(b, g) + QT_ * D],
                                              XNR.rearrange("p t d -> p (t d)")).then_inc(a["xn_kept"], 1)
            if L:
                after(pool, a["xn_kept"], GB * NB - 1)
                pool.dma_start(xslots[NS * P:(NS + NT) * P].rearrange("(t p) d -> p t d", p=P),
                               XNt).then_inc(r["shared_stored"], 16)
            pool.wait_ge(r["router_on"], 1)
            nc.gpsimd.memset(R_u, 1.0).then_inc(r["r_consts"], 1)
            nc.gpsimd.memset(R_1, 1.0).then_inc(r["r_consts"], 1)
            nc.gpsimd.memset(R_rs, 1.0).then_inc(r["r_consts"], 1)
            nc.gpsimd.iota(R_i.rearrange("p (t e) -> p t e", t=NT), pattern=[[0, NT], [1, NE]], base=0,
                           channel_multiplier=0, allow_small_or_imprecise_dtypes=True).then_inc(r["r_consts"], 1)
            nc.gpsimd.iota(R_j, pattern=[[1, NS + 1]], base=0, channel_multiplier=0,
                           allow_small_or_imprecise_dtypes=True).then_inc(r["r_consts"], 1)
            pool.wait_ge(r["r_consts"], 5)
            nc.gpsimd.affine_select(out=R_u, in_=R_u, compare_op=ALU.is_gt, fill=0.0, base=0,
                                    pattern=[[1, P]], channel_multiplier=-1).then_inc(r["r_consts"], 1)
            rs = R_rs.rearrange("p (e g) -> p e g", e=NE)
            nc.gpsimd.affine_select(out=rs, in_=rs, compare_op=ALU.not_equal, fill=0.0, base=0,
                                    pattern=[[0, NE], [1, NG]], channel_multiplier=0).then_inc(r["r_consts"], 1)
            pool.wait_ge(r["routed"], 1)
            for g in range(NG):
                pool.indirect_dma_start(xslots[0:NS * P], bass.IndirectOffsetOnAxis(ap=slot[:, g:g + 1], axis=0),
                                        XNt[:, g % NT], None).then_inc(r["scattered"], 16)
            pool.wait_ge(r["scattered"], 16 * NG)
            pool.wait_ge(e["y_stored_0"], 16 * ((NS + 1) // 2))
            pool.wait_ge(e["y_stored_1"], 16 * (NS // 2))
            gather(L, 0)
            if L:
                gather(L, 1)

        @block.gpsimd
        def _(pool):
            count_from_one(pool, "pool")
            own = Chain(pool, U["own_pool"])
            nc.gpsimd.memset(zeros, 0.0).then_inc(U["zeros_set"], 1)
            nc.gpsimd.memset(HALF, -0.5)
            nc.gpsimd.memset(onesb[:], 1.0)
            nc.gpsimd.memset(onec[:], 1.0)
            nc.gpsimd.memset(blockm[:], 1.0)
            nc.gpsimd.memset(maskv[:], 1.0)
            nc.gpsimd.memset(IND, -1.0)
            nc.gpsimd.memset(bm, 1.0)
            nc.gpsimd.iota(prow, pattern=[[0, 1]], base=0, channel_multiplier=1,
                           allow_small_or_imprecise_dtypes=True)
            nc.gpsimd.iota(iota77[:], pattern=[[1, NK]], base=0, channel_multiplier=0,
                           allow_small_or_imprecise_dtypes=True)
            own.done(nc.gpsimd.memset(ident[:], 0.0))
            own.done(nc.gpsimd.affine_select(out=ident[:], in_=ident[:], compare_op=ALU.not_equal, fill=1.0,
                                             base=0, pattern=[[-1, P]], channel_multiplier=1))

            def band(ap, pattern, base, mult, width):
                own.done(nc.gpsimd.affine_select(out=ap, in_=ap, compare_op=ALU.is_ge, fill=0.0, base=base,
                                                 pattern=pattern, channel_multiplier=mult))
                own.done(nc.gpsimd.affine_select(out=ap, in_=ap, compare_op=ALU.is_ge, fill=0.0,
                                                 base=width - 1 - base, pattern=[[-s, n] for s, n in pattern],
                                                 channel_multiplier=-mult))

            band(bm, [[-NE, 3]], 0, 1, NE)
            band(blockm[:], [[-HD, HH]], 0, 1, HD)
            band(maskv[:], [[P, JT], [-NK, HH]], 0, 1, NK)
            for f in range(2):
                band(IND[:, f], [[1, HK]], f * HH * NK, -NK, NK)
            nc.gpsimd.tensor_copy(identb[:], ident[:]).then_inc(U["consts_set"], 1)
            pool_layer(pool, 0)
            pool_layer(pool, 1)

        def act_attention(act, L):
            a, r = A[L], R[L]
            nh = 1 if L else 2

            def keep_transposed(b, n):
                after(act, a["x_t"], b * TURNS + n)
                nc.scalar.activation(XNT, PS[:, 0:2], ACT.Copy).then_inc(a["x_t_copied"], 1)

            def keep_row(b, g, q):
                after(act, a["x_t"], b * TURNS + GB + g * QT_ + q + 1)
                after(act, a["row_used"], b * NTB + g * QT_ + max(q - 1, 0))
                nc.scalar.activation(RT[:, q % 2], PS[:, 2 + q % 2, 0:D].rearrange("p (k q) -> p k q", k=KC),
                                     ACT.Copy).then_inc(a["x_t_copied"], 1)

            def keep_logits(b, g):
                after(act, a["row_used"], b * NTB + (g + 1) * QT_)
                w = NW[L]
                nc.scalar.activation(LG[:, bass.ds(b * (NTB * w) + g * QT_ * w, QT_ * w)],
                                     PS[:, 6, 0:QT_ * w], ACT.Copy).then_inc(a["logits_copied"], 1)

            with act.Fori(0, NB) as b:
                for g in range(GB):
                    keep_transposed(b, g + 1)
                    after(act, a["q_ready"], b * GB + g + 1)
                    nc.scalar.activation(QF[:, g], PS[:, 2:4], ACT.Copy).then_inc(a["q_copied"], 1)
                after(act, a["k_built"], b + 1)
                nc.scalar.activation(KB[:, 0:nh], KF[:, 0:nh], ACT.Copy).then_inc(a["kb_copied"], 1)
                for g in range(GB):
                    n0 = b * GB + g
                    if g == 0:
                        after(act, a["smax"], n0 * (4 * QT_))
                        after(act, a["q_copied"], b * GB + GB)
                        nc.scalar.activation(QB, QF[:, g], ACT.Copy).then_inc(a["qb_copied"], 1)
                    after(act, a["mx_t"], n0 + 1)
                    nc.scalar.activation(MT, PS[0:H, 0, 0:G // 2].bitcast(BF16), ACT.Copy).then_inc(a["mx_copied"], 1)
                    if g + 1 < GB:
                        after(act, a["smax"], (n0 + 1) * (4 * QT_))
                        nc.scalar.activation(QB, QF[:, g + 1], ACT.Copy).then_inc(a["qb_copied"], 1)
                    if L:
                        after(act, a["cnt_bias"], b + 1)
                    for i in range(2 * JT):
                        if g == 1 and R_AT < i <= R_AT + QT_:
                            keep_row(b, 0, i - R_AT - 1)
                        rows = ROWS[i % JT]
                        after(act, a["s_ready"], n0 * (2 * JT) + i + 1)
                        bias = {"bias": KBI[0:rows, i % JT:i % JT + 1]} if L else {}
                        nc.scalar.activation(PR[0:rows, i], PS[0:rows, 4 + i % 2], ACT.Exp, scale=SCALE,
                                             **bias).then_inc(a["exp_done"], 1)
                    if g == 1:
                        keep_logits(b, 0)
                    for q in range(QT_):
                        after(act, a["o_t"], n0 * QT_ + q + 1)
                        nc.scalar.activation(OT[:, q % 2], PS[:, 0, 0:D].rearrange("p (k q) -> p k q", k=KC),
                                             ACT.Copy).then_inc(a["o_t_copied"], 1)
                for q in range(QT_):
                    keep_row(b, 1, q)
                keep_logits(b, 1)
            act.wait_ge(r["exp_in"], 1)
            nc.scalar.activation(wgt[:, 0], wgt[:, 0], ACT.Exp).then_inc(r["exp_out"], 1)
            if L:
                lg = LG[:, 0:NT * NW[1]].rearrange("p (t e) -> p t e", t=NT)
                nc.scalar.activation(wgt[:, 2], lg[:, :, NE], ACT.Exp, scale=-1.0).then_inc(r["exp_out"], 1)

        def act_experts(act, L):
            e, n = E[L], NS + (NT if L else 0)

            def keep_xt(i, u):
                act.wait_ge(e["xs_t"], i + 1)
                nc.scalar.activation(FB[L]["XT"][:, u], PS[:, 7, 0:D].rearrange("p (k q) -> p k q", k=KC),
                                     ACT.Copy).then_inc(e["xt_copied"], 1)

            def step(h, u):
                i = h * 2 + u
                later = not (isinstance(i, int) and i < 2)
                if L:
                    act.wait_ge(e["h_ready"], i * 2 + 1)
                    if later:
                        act.wait_ge(e["h_mul"], i - 1)
                    nc.scalar.activation(FB[L]["H"][:, u, 0:F1], PS[:, 2 * u, 0:F1], ACT.Silu).then_inc(e["h_act"], 1)
                else:
                    if later:
                        act.wait_ge(e["h_t"], i - 1)
                    for s in range(2):
                        act.wait_ge(e["h_ready"], i * 2 + s + 1)
                        nc.scalar.activation(FB[L]["H"][:, u, s * 512:(s + 1) * 512], PS[:, 2 * u + s],
                                             ACT.Gelu).then_inc(e["h_act"], 1)
                if not (isinstance(i, int) and i == n - 1):
                    keep_xt(i + 1, 1 - u)

            keep_xt(0, 0)
            over_tiles(act, L, step)

        @block.scalar
        def _(act):
            for part in range(3):
                act.dma_start(bst[part * NE:(part + 1) * NE, 0:F0], b1).then_inc(U["bias_loaded"], 16)
                act.dma_start(bst[part * NE:(part + 1) * NE, F0:], b2).then_inc(U["bias_loaded"], 16)
            act.dma_start(TG[:, 0:2], g_xattn.partition_broadcast(P)).then_inc(U["gates_loaded"], 16)
            act.dma_start(TG[:, 2:4], g_ffn.partition_broadcast(P)).then_inc(U["gates_loaded"], 16)
            act.dma_start(bproj[:], bproj0.partition_broadcast(P)).then_inc(U["gates_loaded"], 16)
            act.dma_start(gwt[:, :, 0:NE], gate0.rearrange("(k p) e -> p k e", p=P)).then_inc(U["gate_w_loaded"], 16)
            count_from_one(act, "act")
            act.wait_ge(U["gates_loaded"], 48)
            nc.scalar.activation(TG[:], TG[:], ACT.Tanh).then_inc(U["tanh_done"], 1)
            act.wait_ge(U["tanh_done"], 1)
            nc.scalar.activation(bproj[:], bproj[:], ACT.Copy, scale=TG[:, 0:1]).then_inc(U["bproj_ready"], 1)
            act.wait_ge(U["ctx_t"], 1)
            nc.scalar.activation(CT[:], PS[:, 0, 0:KC * NB * NK].rearrange("p (k n) -> p k n", k=KC),
                                 ACT.Copy).then_inc(U["ctx_copied"], 1)
            act_attention(act, 0)
            act_experts(act, 0)
            act.wait_ge(U["w1_t"], 1)
            nc.scalar.activation(AW[:, :, 0:D], PS[:, 0:2, 0:D], ACT.Copy)
            nc.scalar.activation(AW[:, :, 3 * D:4 * D], PS[:, 2:4, 0:D], ACT.Copy)
            for i in range(2):
                for k in range(KC):
                    nc.scalar.activation(
                        AW[:, k, (1 + i) * D:(1 + i) * D + P].rearrange("p (h d) -> p h d", h=HH),
                        PS[:, 4 + k, i * HD:(i + 1) * HD][:, None, :].to_broadcast([P, HH, HD]), ACT.Copy)
            nc.scalar.activation(gwt[:], PS[:, 6:8, 0:NE + 1], ACT.Copy).then_inc(U["w1_copied"], 1)
            act_attention(act, 1)
            act_experts(act, 1)

        def dve_attention(dve, L):
            a = A[L]
            nh = 1 if L else 2
            mask = maskc if L else maskv
            gate = TG[:, L:L + 1]

            def norm(own, b, n):
                g = n % GB
                to = XNR if n >= GB else XNA
                for q in range(QT_):
                    last = nc.vector.bn_stats(STAT[:, q], X[:, bass.ds(tile_at(b, g, q), D)])
                own.done(last, settle)
                for q in range(QT_):
                    last = nc.vector.bn_aggr(MV[:, q], STAT[:, q])
                last.then_inc(a["stats"], 1)
                after(dve, a["rstd"], b * (2 * GB) + n + 1)
                after(dve, a["x_t"], b * TURNS + (GB + g * QT_ if n >= GB else n))
                if n >= GB:
                    after(dve, a["xn_kept"], b * GB + g)
                for q in range(QT_):
                    last = nc.vector.tensor_scalar(to[:, q], X[:, bass.ds(tile_at(b, g, q), D)], MV[:, q, 0:1],
                                                   RSTD[:, q:q + 1], ALU.subtract, ALU.mult)
                last.then_inc(a["ln_done"], 1)

            def choose(own, b, g):
                for q in range(QT_):
                    n = b * NTB + g * QT_ + q
                    after(dve, a["s77"], n + 1)
                    settle(dve)
                    sc = PS[:, 6 + q % 2, 0:NK]
                    own.done(nc.vector.max(TOP, sc), settle)
                    own.done(nc.vector.max_index(TOPI, TOP, sc))
                    own.done(nc.vector.tensor_copy(IDX, TOPI[:, 0:1]))
                    if g == 0 and q == 0:
                        ins = nc.vector.tensor_scalar(SQ[:], iota77[:], IDX, None, ALU.is_equal)
                    else:
                        ins = nc.vector.scalar_tensor_tensor(SQ[:], iota77[:], IDX, SQ[:], ALU.is_equal, ALU.add)
                    ins.then_inc(a["s77_used"], 1)
                    after(dve, a["s77_used"], n + 1)

            def maximum(n0, i):
                q, c = i // 4, i % 4
                if i == 0:
                    after(dve, a["mx_t"], n0)
                after(dve, a["smax"], n0 * (4 * QT_) + i + 1)
                nc.vector.tensor_reduce(MX[:, q, c * 4:c * 4 + 4],
                                        PS[:, 2 + i % 2, 0:QK].rearrange("p (h m) -> p h m", h=4),
                                        AX.X, ALU.max).then_inc(a["smax_used"], 1)

            with dve.Fori(0, NB) as b:
                own = Chain(dve, a["own_dve"], b, 2 * GB + NTB + (3 * NTB + 4 + NTB if L else 0))
                if L:
                    for g in range(GB):
                        combine(dve, 0, own, b, g, g)
                    dve.wait_ge(E[0]["combined"], b * NTB + NTB)
                else:
                    dve.wait_ge(U["x_loaded"], b * 16 + 16)
                settle(dve)
                for g in range(GB):
                    norm(own, b, g)
                    if L:
                        choose(own, b, g)
                        settle(dve)
                after(dve, a["x_t"], b * TURNS + GB)
                for k in range(KC):
                    last = nc.vector.tensor_copy(CR[:, k].rearrange("p (h m) -> p h m", h=HH),
                                                 CT[:, k, bass.ds(b * NK, NK)][:, None, :].to_broadcast([P, HH, NK]))
                last.then_inc(a["ctx_rep"], 1)
                after(dve, a["k_ready"], b + 1)
                for f in range(nh):
                    last = nc.vector.tensor_tensor(KF[:, f].rearrange("p (h m) -> p h m", h=HH),
                                                   PS[:, f, 0:NK][:, None, :].to_broadcast([P, HH, NK]),
                                                   blockm[:, :, None].to_broadcast([P, HH, NK]), ALU.mult)
                last.then_inc(a["k_built"], 1)
                if L:
                    own.done(nc.vector.memset(SR[:, HK:], 0.0))
                    nc.vector.tensor_copy(SR[:, 0:HK].rearrange("p (h m) -> p h m", h=HH),
                                          SQ[:, None, :].to_broadcast([P, HH, NK])).then_inc(a["counted"], 1)
                    after(dve, a["c_ready"], b + 1)
                    own.done(nc.vector.tensor_copy(CNT, PS[:, 6, 0:JT]))
                    own.done(nc.vector.tensor_scalar(KBI, CNT, 0.0, -BIG, ALU.is_equal, ALU.mult))
                    own.done(nc.vector.tensor_scalar(used[:].rearrange("p (w n) -> p w n", w=2), PS[0:1, 2:4, 0:QK],
                                                     0.0, -BIG, ALU.is_equal, ALU.mult))
                    nc.vector.tensor_tensor(maskc[:], maskv[:], CNT[:, :, None].to_broadcast([P, JT, HH]),
                                            ALU.mult).then_inc(a["cnt_bias"], 1)
                    after(dve, a["cnt_bias"], b + 1)
                for f in range(nh):
                    for j in range(JT):
                        for i in first_maxima(nh, f, j):
                            maximum(b * GB, i)
                    after(dve, a["v_ready"], b * nh + f + 1)
                    rows = ROWS[JT - 1]
                    nc.vector.tensor_tensor(VF[:, f, 0:4, :, 0:HD],
                                            PS[:, 4].rearrange("p (j h d) -> p j h d", j=4, h=HH),
                                            mask[:, 0:4, :, None].to_broadcast([P, 4, HH, HD]), ALU.mult)
                    nc.vector.tensor_copy(VF[:, f, :, :, HD], mask[:])
                    nc.vector.tensor_tensor(VF[0:rows, f, 4, :, 0:HD],
                                            PS[0:rows, 5, 0:P].rearrange("p (h d) -> p h d", h=HH),
                                            mask[0:rows, 4, :, None].to_broadcast([rows, HH, HD]),
                                            ALU.mult).then_inc(a["v_built"], 1)
                for g in range(GB):
                    n0 = b * GB + g
                    if g == 1:
                        after(dve, a["x_added"], b * NTB + QT_)
                        if L == 0:
                            dve.wait_ge(U["rows_zeroed"], 48)
                        settle(dve)
                        norm(own, b, GB)
                    for s in range(QT_ + 2):
                        between = s < QT_ and g + 1 < GB
                        if between:
                            for i in range(4 * s, 4 * s + 2):
                                maximum(n0 + 1, i)
                        if s < QT_:
                            o = PS[:, 6 + s % 2, 0:2 * HH * VW].rearrange("p (h v) -> p h v", h=H)
                            after(dve, a["o_ready"], n0 * QT_ + s + 1)
                            own.done(nc.vector.reciprocal(RD[s % 2], o[:, :, HD]))
                            if s >= 2:
                                after(dve, a["o_t"], n0 * QT_ + s - 1)
                            nc.vector.tensor_tensor(OA[:, s % 2].rearrange("p (h d) -> p h d", h=H), o[:, :, 0:HD],
                                                    RD[s % 2][:, :, None].to_broadcast([P, H, HD]),
                                                    ALU.mult).then_inc(a["o_done"], 1)
                        if between:
                            for i in range(4 * s + 2, 4 * s + 4):
                                maximum(n0 + 1, i)
                        if s >= 2:
                            xq = X[:, bass.ds(tile_at(b, g, s - 2), D)]
                            after(dve, a["y_ready"], n0 * QT_ + s - 1)
                            if L == 0:
                                after(dve, a["xb_added"], b * GB + GB)
                            nc.vector.scalar_tensor_tensor(xq, PS[:, 1, 0:D], gate, xq, ALU.mult,
                                                           ALU.add).then_inc(a["x_added"], 1)
                after(dve, a["x_added"], b * NTB + NTB)
                settle(dve)
                norm(own, b, GB + 1)
                own.close()

        def dve_router(dve, L, own):
            a, r = A[L], R[L]
            after(dve, a["logits_copied"], GB * NB)
            nc.vector.memset(mark[:, 0:1], 0.0).then_inc(r["router_on"], 1)
            lg = LG[:, 0:NT * NW[L]].rearrange("p (t e) -> p t e", t=NT)[:, :, 0:NE]
            te = lambda ap: ap[:, 0:NT * NE].rearrange("p (t e) -> p t e", t=NT)
            wide = lambda ap: ap[:, :, None].to_broadcast([P, NT, NE])
            dve.wait_ge(r["r_consts"], 7)
            first = R_c[:, 0:NT]
            for c in range(TOPK):
                src = lg if c == 0 else te(R_d)
                own.done(nc.vector.tensor_reduce(wgt[:, c], src, AX.X, ALU.max))
                own.done(nc.vector.tensor_tensor(te(R_a), src, wide(wgt[:, c]), ALU.is_equal))
                own.done(nc.vector.scalar_tensor_tensor(te(R_b), te(R_a), -99.0, te(R_i), ALU.mult, ALU.add))
                own.done(nc.vector.tensor_reduce(first, te(R_b), AX.X, ALU.min))
                own.done(nc.vector.tensor_scalar(first, first, 99.0, None, ALU.add))
                oh = R_M[:, c * NT:(c + 1) * NT]
                nc.vector.tensor_tensor(oh, te(R_i), wide(first), ALU.is_equal).then_inc(r["onehot"], 1)
                dve.wait_ge(r["onehot"], c + 1)
                if c == 0:
                    own.done(nc.vector.scalar_tensor_tensor(te(R_d), oh, -BIG, lg, ALU.mult, ALU.add))
            nc.vector.tensor_tensor(wgt[:, 0], wgt[:, 1], wgt[:, 0], ALU.subtract).then_inc(r["exp_in"], 1)
            eg = lambda ap: ap.rearrange("p (e g) -> p e g", e=NE)
            dve.wait_ge(r["totals"], 1)
            own.done(nc.vector.tensor_copy(eg(R_a), PS[:, 5, 0:GE].rearrange("p (g e) -> p e g", e=NE)))
            own.done(nc.vector.tensor_tensor_scan(R_b, R_rs, R_a, 0.0, ALU.mult, ALU.add))
            ni, nsh, nf, ends, base = [R_c[:, 48 + 8 * i:56 + 8 * i] for i in range(5)]
            own.done(nc.vector.tensor_scalar(ni.bitcast(I32), eg(R_b)[:, :, NG - 1], float(P - 1), None, ALU.add))
            own.done(nc.vector.tensor_scalar(nsh.bitcast(I32), ni.bitcast(I32), P.bit_length() - 1, None,
                                             ALU.arith_shift_right))
            own.done(nc.vector.tensor_copy(nf, nsh.bitcast(I32)))
            own.done(nc.vector.tensor_tensor_scan(ends, R_1[:, 0:NE], nf, 0.0, ALU.mult, ALU.add))
            own.done(nc.vector.tensor_tensor(base, ends, nf, ALU.subtract))
            jt = R_d[:, 0:NS * (NE - 1)].rearrange("p (j e) -> p j e", j=NS)
            own.done(nc.vector.tensor_tensor(jt, R_j[:, 0:NS, None].to_broadcast([P, NS, NE - 1]),
                                             ends[:, None, 0:NE - 1].to_broadcast([P, NS, NE - 1]), ALU.is_ge))
            tex = R_c[:, 96:96 + NS]
            own.done(nc.vector.tensor_reduce(tex, jt, AX.X, ALU.add))
            own.done(nc.vector.tensor_copy(texp[:], tex))
            own.done(nc.vector.tensor_scalar(selc[:], tex[0:3 * NE], rmod, None, ALU.is_equal))
            own.done(nc.vector.tensor_tensor(R_a, R_b, R_a, ALU.subtract))
            own.done(nc.vector.scalar_tensor_tensor(eg(R_a), base[:, :, None].to_broadcast([P, NE, NG]), float(P),
                                                    eg(R_a), ALU.mult, ALU.add))
            ge = R_b.rearrange("p (g e) -> p g e", g=NG)
            own.done(nc.vector.tensor_tensor(ge, PS[:, 4, 0:GE].rearrange("p (g e) -> p g e", g=NG),
                                             R_a.rearrange("p (e g) -> p g e", e=NE), ALU.add))
            own.done(nc.vector.tensor_tensor(ge, ge, R_M, ALU.mult))
            own.done(nc.vector.tensor_reduce(R_c[:, 144:144 + NG], ge, AX.X, ALU.add))
            nc.vector.tensor_copy(slot[:], R_c[:, 144:144 + NG]).then_inc(r["routed"], 1)
            dve.wait_ge(r["exp_out"], 2 if L else 1)
            gate = TG[:, 2 + L:3 + L]
            own.done(nc.vector.tensor_scalar(R_c[:, 0:NT], wgt[:, 0], 1.0, None, ALU.add))
            own.done(nc.vector.reciprocal(R_c[:, 16:16 + NT], R_c[:, 0:NT]))
            own.done(nc.vector.scalar_tensor_tensor(wgt[:, 1], wgt[:, 0], gate, R_c[:, 16:16 + NT], ALU.mult,
                                                    ALU.mult))
            own.done(nc.vector.tensor_scalar(wgt[:, 0], R_c[:, 16:16 + NT], gate, None, ALU.mult))
            if L:
                own.done(nc.vector.tensor_scalar(R_c[:, 0:NT], wgt[:, 2], 1.0, None, ALU.add))
                own.done(nc.vector.reciprocal(R_c[:, 16:16 + NT], R_c[:, 0:NT]))
                own.done(nc.vector.tensor_scalar(wgt[:, 2], R_c[:, 16:16 + NT], gate, None, ALU.mult))

        def dve_experts(dve, L):
            e, n = E[L], NS + (NT if L else 0)

            def select(w, i, u, later=True):
                if later:
                    dve.wait_ge(e["yt_ready"], i - 1) if w else dve.wait_ge(e["h_ready"], i * 2 - 2)
                nc.vector.tensor_copy(SEL[:, w, u], selc[:, bass.ds(i, 1)].to_broadcast([3 * NE, P])
                                      ).then_inc(e["sel_down" if w else "sel_up"], 1)

            def multiply(i, u, later=True):
                dve.wait_ge(e["h_act"], i + 1)
                dve.wait_ge(e["h_ready"], i * 2 + 2)
                if later:
                    dve.wait_ge(e["h_t"], i - 1)
                nc.vector.tensor_tensor(FB[L]["H"][:, u, 512:512 + F1], PS[:, 2 * u + 1, 0:F1], FB[L]["H"][:, u, 0:F1],
                                        ALU.mult).then_inc(e["h_mul"], 1)

            def keep_ht(i, u, later=True):
                dve.wait_ge(e["h_t"], i + 1)
                if later:
                    dve.wait_ge(e["yt_ready"], i - 1)
                if L:
                    for c, (_, w) in enumerate(C1):
                        last = nc.vector.tensor_copy(FB[L]["HT"][0:w, u, c], PS[0:w, 4, c * P:(c + 1) * P])
                    last.then_inc(e["ht_copied"], 1)
                else:
                    nc.vector.tensor_copy(FB[L]["HT"][:, u], PS[:, 4:6].rearrange("p b (c q) -> p (b c) q", c=4)
                                          ).then_inc(e["ht_copied"], 1)

            def keep_y(h, u):
                dve.wait_ge(e["yt_ready"], h * 2 + u + 1)
                if shared(h):
                    i = h * 2 + u
                    xt = X[:, bass.ds(i * D, D)]
                    nc.vector.scalar_tensor_tensor(xt, PS[:, 6, 0:D], wgt[:, 2, bass.ds(i, 1)], xt, ALU.mult,
                                                   ALU.add).then_inc(e["y_copied"], 1)
                    return
                if not (isinstance(h, int) and h == lead):
                    dve.wait_ge(e[f"y_stored_{u}"], (h - lead) * 16)
                nc.vector.tensor_copy(FB[L]["Y"][:, u], PS[:, 6, 0:D]).then_inc(e["y_copied"], 1)

            lead, loops = (NT // 2 if L else 0), [0]

            def shared(h):
                return h < lead if isinstance(h, int) else L == 1 and loops[0] == 0

            def step(h, u):
                i = h * 2 + u
                first, last = (isinstance(i, int) and i == k for k in (0, n - 1))
                hp, up = (h, 0) if u else (h - 1, 1)
                if not L and not last:
                    select(0, i + 1, 1 - u, later=not (isinstance(i, int) and i < 1))
                if not L and not first:
                    select(1, i - 1, up, later=not (isinstance(i, int) and i < 3))
                if not first:
                    keep_ht(i - 1, up, later=not (isinstance(i, int) and i < 3))
                if L:
                    multiply(i, u, later=not (isinstance(i, int) and i < 2))
                if not first:
                    keep_y(hp, up)
                if u and not isinstance(h, int):
                    loops[0] += 1

            if not L:
                select(0, 0, 0, later=False)
            over_tiles(dve, L, step)
            if not L:
                select(1, n - 1, (n - 1) % 2)
            keep_ht(n - 1, (n - 1) % 2)
            keep_y((n - 1) // 2, (n - 1) % 2)

        def combine(dve, L, own, b, g, arrived):
            dve.wait_ge(E[L][f"gathered_{arrived}"], b * (16 * TOPK * QT_) + 16 * TOPK * QT_ if L == 0 else
                        16 * TOPK * QT_)
            for q in range(QT_):
                xt = X[:, bass.ds(tile_at(b, g, q), D)]
                for c in range(TOPK):
                    ins = nc.vector.scalar_tensor_tensor(xt, YG4[:, bass.ds(b * GB + g, 1), q, c],
                                                         wgt[:, c, bass.ds(b * NTB + g * QT_ + q, 1)], xt,
                                                         ALU.mult, ALU.add)
                    if c == 0:
                        own.done(ins)
                ins.then_inc(E[L]["combined"], 1)

        @block.vector
        def _(dve):
            count_from_one(dve, "dve")
            own = Chain(dve, U["own_dve"])
            dve.wait_ge(U["bias_loaded"], 96)
            dve.wait_ge(U["consts_set"], 1)
            own.done(nc.vector.tensor_copy(bpb0, bst))
            own.done(nc.vector.tensor_tensor(bpa0, bst, bpb0, ALU.subtract))
            own.done(nc.vector.tensor_copy(bpb1, bpa0))
            own.done(nc.vector.tensor_tensor(bpa1, bpa0, bpb1, ALU.subtract))
            own.done(nc.vector.tensor_scalar(bpa2, bpb0, bm[:, 0:1], None, ALU.mult))
            own.done(nc.vector.scalar_tensor_tensor(bpa0, bpb1, bm[:, 1:2], bpa2, ALU.mult, ALU.add))
            own.done(nc.vector.scalar_tensor_tensor(b1t[:], bpa1[:, 0:F0], bm[:, 2:3], bpa0[:, 0:F0],
                                                    ALU.mult, ALU.add))
            own.done(nc.vector.scalar_tensor_tensor(b2t[:], bpa1[:, F0:], bm[:, 2:3], bpa0[:, F0:],
                                                    ALU.mult, ALU.add))
            own.done(nc.vector.scalar_tensor_tensor(rmod, bm[:, 1:2], -float(NE), prow, ALU.mult, ALU.add))
            own.done(nc.vector.scalar_tensor_tensor(rmod, bm[:, 2:3], -2.0 * NE, rmod, ALU.mult, ALU.add))
            dve.wait_ge(U["ctx_copied"], 1)
            dve_attention(dve, 0)
            dve_router(dve, 0, Chain(dve, R[0]["router_own"]))
            dve_experts(dve, 0)
            dve.wait_ge(U["w1_copied"], 1)
            dve_attention(dve, 1)
            dve_router(dve, 1, Chain(dve, R[1]["router_own"]))
            dve_experts(dve, 1)
            own = Chain(dve, E[1]["own"])
            for j in range(NB * GB):
                combine(dve, 1, own, j // GB, j % GB, j)

        def pe_attention(pe, L):
            a, r = A[L], R[L]
            nh = 1 if L else 2
            f_of = (lambda f: 0) if L else (lambda f: f)

            def turn(b, n):
                after(pe, a["ln_done"], b * (2 * GB) + n + 1)
                after(pe, a["x_t_copied"], b * TURNS + n)
                for q in range(QT_):
                    for k in range(KC):
                        last = nc.tensor.transpose(PS[:, k, q * P:(q + 1) * P], XNA[:, q, k * P:(k + 1) * P],
                                                   ident[:])
                last.then_inc(a["x_t"], 1)
                after(pe, a["x_t_copied"], b * TURNS + n + 1)

            def turn_row(b, g, q):
                if q == 0:
                    after(pe, a["ln_done"], b * (2 * GB) + GB + g + 1)
                after(pe, a["x_t_copied"], b * TURNS + GB + g * QT_ + max(q - 1, 0))
                for k in range(KC):
                    last = nc.tensor.transpose(PS[:, 2 + q % 2, k * P:(k + 1) * P], XNR[:, q, k * P:(k + 1) * P],
                                               ident[:])
                last.then_inc(a["x_t"], 1)

            def route(b, g, q):
                after(pe, a["x_t_copied"], b * TURNS + GB + g * QT_ + q + 1)
                if q == 0:
                    after(pe, a["logits_copied"], b * GB + g)
                    after(pe, a["o_done"], b * NTB + (g + 1) * QT_)
                w = NW[L]
                for k in range(KC):
                    last = nc.tensor.matmul(PS[:, 6, q * w:(q + 1) * w], RT[:, q % 2, k], gwt[:, k, 0:w],
                                            start=k == 0, stop=k == KC - 1)
                last.then_inc(a["row_used"], 1)

            def maximum(n0, i):
                q, c = i // 4, i % 4
                if i == 0:
                    after(pe, a["qb_copied"], n0 + 1)
                after(pe, a["smax_used"], n0 * (4 * QT_) + max(i - 1, 0))
                cols = slice(c % 2 * QK, (c % 2 + 1) * QK)
                last = nc.tensor.matmul(PS[:, 2 + i % 2, 0:QK], QB[:, c // 2, q * P:(q + 1) * P],
                                        KB[:, f_of(c // 2), cols], start=True, stop=not L)
                if L:
                    last = nc.tensor.matmul(PS[:, 2 + i % 2, 0:QK], onesb[0:1], used[:, cols],
                                            start=False, stop=True)
                last.then_inc(a["smax"], 1)

            with pe.Fori(0, NB) as b:
                for g in range(GB):
                    turn(b, g)
                    after(pe, a["smax_used"], b * (GB * 4 * QT_))
                    after(pe, a["q_copied"], b * GB + g)
                    for f in range(2):
                        for k in range(KC):
                            last = nc.tensor.matmul(PS[:, 2 + f], AW[:, k, f * P:(f + 1) * P], XNT[:, k],
                                                    start=k == 0, stop=k == KC - 1)
                    last.then_inc(a["q_ready"], 1)
                    if L:
                        after(pe, a["q_copied"], b * GB + g + 1)
                        after(pe, a["logits_copied"], b * GB)
                        after(pe, a["x_added"], b * NTB)
                        for q in range(QT_):
                            after(pe, a["s77_used"], b * NTB + max(g * QT_ + q - 1, 0))
                            for f in range(2):
                                last = nc.tensor.matmul(PS[:, 6 + q % 2, 0:NK], QF[:, g, f, q * P:(q + 1) * P],
                                                        CT[:, f, bass.ds(b * NK, NK)], start=f == 0, stop=f == 1)
                            last.then_inc(a["s77"], 1)
                for f in range(nh):
                    for k in range(KC):
                        last = nc.tensor.matmul(PS[:, f, 0:NK], AW[:, k, D + f * P:D + (f + 1) * P],
                                                CT[:, k, bass.ds(b * NK, NK)], start=k == 0, stop=k == KC - 1)
                last.then_inc(a["k_ready"], 1)
                if L:
                    after(pe, a["counted"], b + 1)
                    after(pe, a["s77_used"], b * NTB + NTB)
                    for j in range(JT):
                        nc.tensor.matmul(PS[:, 6, j:j + 1], SR[:, j * P:(j + 1) * P], onec[:], start=True, stop=True)
                    for w in range(2):
                        last = nc.tensor.matmul(PS[0:1, 2 + w, 0:QK], onec[:], SR[:, w * QK:(w + 1) * QK],
                                                start=True, stop=True)
                    last.then_inc(a["c_ready"], 1)
                after(pe, a["ctx_rep"], b + 1)
                after(pe, a["kb_copied"], b + 1)
                if L:
                    after(pe, a["cnt_bias"], b + 1)
                for f in range(nh):
                    after(pe, a["v_built"], b * nh + f)
                    for j in range(JT):
                        for k in range(KC):
                            last = nc.tensor.matmul(PS[0:ROWS[j], 4 + j // 4, (j % 4) * P:(j % 4 + 1) * P],
                                                    CR[:, k, j * P:j * P + ROWS[j]],
                                                    AW[:, k, 2 * D + f * P:2 * D + (f + 1) * P],
                                                    start=k == 0, stop=k == KC - 1)
                        if j == JT - 1:
                            last.then_inc(a["v_ready"], 1)
                        for i in first_maxima(nh, f, j):
                            maximum(b * GB, i)
                for g in range(GB):
                    n0 = b * GB + g
                    after(pe, a["smax_used"], n0 * (4 * QT_) + 4 * QT_)
                    after(pe, a["o_t_copied"], n0 * QT_)
                    if g == 0:
                        after(pe, a["k_built"], b + 1)
                    for q in range(QT_):
                        last = nc.tensor.transpose(PS[0:H, 0, 0:G // 2].bitcast(BF16)[:, q * P:(q + 1) * P],
                                                   MX[:, q], identb[:])
                    last.then_inc(a["mx_t"], 1)
                    after(pe, a["mx_copied"], n0 + 1)
                    if g == 0:
                        after(pe, a["v_built"], b * nh + nh)
                    for i in range(2 * JT):
                        f, j = i // JT, i % JT
                        rows = ROWS[j]
                        after(pe, a["exp_done"], n0 * (2 * JT) + max(i - 1, 0))
                        nc.tensor.matmul(PS[0:rows, 4 + i % 2], KF[:, f_of(f), j * P:j * P + rows], QF[:, g, f],
                                         start=True, stop=False)
                        nc.tensor.matmul(PS[0:rows, 4 + i % 2], IND[:, f, j * P:j * P + rows], MT,
                                         start=False, stop=True).then_inc(a["s_ready"], 1)
                        if g == 1:
                            if i > R_AT + 1:
                                route(b, 0, i - R_AT - 2)
                            if R_AT <= i < R_AT + QT_:
                                turn_row(b, 0, i - R_AT)
                    after(pe, a["exp_done"], n0 * (2 * JT) + 2 * JT)
                    if g == 1:
                        after(pe, a["logits_copied"], b * GB + 1)
                    for s in range(QT_ + 2):
                        if s < QT_:
                            after(pe, a["o_done"], n0 * QT_ + max(s - 1, 0))
                            for f in range(2):
                                for j in range(JT):
                                    last = nc.tensor.matmul(
                                        PS[:, 6 + s % 2, f * HH * VW:(f + 1) * HH * VW],
                                        PR[0:ROWS[j], f * JT + j, s * P:(s + 1) * P],
                                        VF[0:ROWS[j], f_of(f), j].rearrange("p h v -> p (h v)"),
                                        start=j == 0, stop=j == JT - 1)
                                if f == 1:
                                    last.then_inc(a["o_ready"], 1)
                                if g + 1 < GB:
                                    for i in range(4 * s + 2 * f, 4 * s + 2 * f + 2):
                                        maximum(n0 + 1, i)
                        if s >= 2:
                            u = s % 2
                            after(pe, a["o_t_copied"], n0 * QT_ + s - 1)
                            after(pe, a["x_added"], n0 * QT_ + s - 2)
                            for k in range(KC):
                                last = nc.tensor.matmul(PS[:, 1, 0:D], OT[:, u, k], AW[:, k, 3 * D:4 * D],
                                                        start=k == 0, stop=k == KC - 1)
                            last.then_inc(a["y_ready"], 1)
                        if 1 <= s <= QT_:
                            after(pe, a["o_done"], n0 * QT_ + s)
                            after(pe, a["o_t_copied"], n0 * QT_ + s - 1)
                            for k in range(KC):
                                last = nc.tensor.transpose(PS[:, 0, k * P:(k + 1) * P],
                                                           OA[:, (s - 1) % 2, k * P:(k + 1) * P], ident[:])
                            last.then_inc(a["o_t"], 1)
                for q in range(QT_ + 1):
                    if q < QT_:
                        turn_row(b, 1, q)
                    if q:
                        route(b, 1, q - 1)
            pe.wait_ge(r["onehot"], TOPK)
            pe.wait_ge(r["r_consts"], 7)
            nc.tensor.matmul(PS[:, 4, 0:GE], R_u, R_M.rearrange("p g e -> p (g e)"), start=True, stop=True)
            nc.tensor.matmul(PS[:, 5, 0:GE], R_1, R_M.rearrange("p g e -> p (g e)"), start=True,
                             stop=True).then_inc(r["totals"], 1)

        def pe_experts(pe, L):
            e, n, lead = E[L], NS + (NT if L else 0), (NT if L else 0)
            hw = F1 if L else 512

            held = [pe.alloc_register(f"expert{u}_{L}") for u in range(2)]

            def look_up(i, u):
                pe.reg_load(held[u], texp[0:1, bass.ds(i - lead, 1)])

            def expert(u, shared):
                return NE if shared else pe.snap(held[u], min_val=0, max_val=NE - 1)

            def turn(h, u):
                i = h * 2 + u
                pe.wait_ge(e[f"xs_loaded_{u}"], h * 16 + 16)
                pe.wait_ge(e["xt_copied"], i)
                for k in range(KC):
                    last = nc.tensor.transpose(PS[:, 7, k * P:(k + 1) * P], FB[L]["XS"][:, u, k * P:(k + 1) * P], ident[:])
                last.then_inc(e["xs_t"], 1)

            def up(i, u, s, ex, later):
                if later:
                    if L:
                        pe.wait_ge(e["h_mul" if s else "h_act"], i - 1)
                    else:
                        pe.wait_ge(e["h_act"], i * 2 + s - 3)
                for k in range(KC):
                    if L:
                        rhs = W1a[:, bass.ds(ex * WG1 + (s * KC + k) * F1, F1)]
                    else:
                        rhs = W0a[:, bass.ds(ex * W0E + k * F0 + s * 512, 512)]
                    last = nc.tensor.matmul(PS[:, 2 * u + s, 0:hw], FB[L]["XT"][:, u, k], rhs, start=k == 0,
                                            stop=bool(L) and k == KC - 1)
                if not L:
                    if s == 0:
                        pe.wait_ge(e["sel_up"], i + 1)
                    last = nc.tensor.matmul(PS[:, 2 * u + s], SEL[:, 0, u], b1t[:, s * 512:(s + 1) * 512],
                                            start=False, stop=True)
                last.then_inc(e["h_ready"], 1)

            def turn_hidden(i, u):
                pe.wait_ge(e["h_mul"], i + 1) if L else pe.wait_ge(e["h_act"], i * 2 + 2)
                pe.wait_ge(e["ht_copied"], i)
                for c in range(3 if L else FC0):
                    if L:
                        at, w = C1[c]
                        last = nc.tensor.transpose(PS[0:w, 4, c * P:(c + 1) * P], FB[L]["H"][:, u, 512 + at:512 + at + w], ident[:])
                    else:
                        last = nc.tensor.transpose(PS[:, 4 + c // 4, c % 4 * P:(c % 4 + 1) * P],
                                                   FB[L]["H"][:, u, c * P:(c + 1) * P], ident[:])
                last.then_inc(e["h_t"], 1)

            def down(i, u, ex):
                pe.wait_ge(e["ht_copied"], i + 1)
                pe.wait_ge(e["y_copied"], i)
                nch = 3 if L else FC0
                for c in range(nch):
                    w = C1[c][1] if L else P
                    base = W1b[0:w, bass.ds(ex * WD1 + c * D, D)] if L else W0b[:, bass.ds(ex * W0E + c * D, D)]
                    last = nc.tensor.matmul(PS[:, 6, 0:D], FB[L]["HT"][0:w, u, c], base, start=c == 0,
                                            stop=bool(L) and c == nch - 1)
                if not L:
                    pe.wait_ge(e["sel_down"], i + 1)
                    last = nc.tensor.matmul(PS[:, 6, 0:D], SEL[:, 1, u], b2t[:], start=False, stop=True)
                last.then_inc(e["yt_ready"], 1)

            def step(h, u):
                i = h * 2 + u
                fixed = isinstance(i, int)
                now = L == 1 and (i < lead if fixed else loops[0] == 0)
                before = L == 1 and (i <= lead if fixed else loops[0] == 0)
                ex = expert(u, now)
                pe.wait_ge(e["xt_copied"], i + 1)
                later = not (fixed and i < 2)
                up(i, u, 0, ex, later)
                if not (fixed and i == 0):
                    turn_hidden(i - 1, 1 - u)
                up(i, u, 1, ex, later)
                if not (fixed and i == n - 1):
                    turn(*((h, 1) if u == 0 else (h + 1, 0)))
                if not (fixed and i == 0):
                    down(i - 1, 1 - u, expert(1 - u, before))
                if L and fixed and i == lead - 1:
                    pe.wait_ge(R[1]["routed"], 1)
                if not fixed and loops[0] or not L or fixed and lead - 1 <= i:
                    if not (fixed and i == n - 1):
                        look_up(i + 1, 1 - u)
                if not fixed and u == 1:
                    loops[0] += 1

            loops = [0]
            pe.wait_ge(U["w1_loaded"] if L else U["w0_loaded"], 16 * (4 * (NE + 1) if L else 2 * NE))
            turn(0, 0)
            if not L:
                pe.wait_ge(R[0]["routed"], 1)
                look_up(0, 0)
            over_tiles(pe, L, step)
            turn_hidden(n - 1, (n - 1) % 2)
            down(n - 1, (n - 1) % 2, expert((n - 1) % 2, False))

        @block.tensor
        def _(pe):
            count_from_one(pe, "pe")
            pe.wait_ge(U["ctx_loaded"], 16)
            pe.wait_ge(U["consts_set"], 1)
            for b in range(NB):
                for k in range(KC):
                    last = nc.tensor.transpose(PS[:, 0, (k * NB + b) * NK:(k * NB + b + 1) * NK],
                                               ctx_raw[:, b, k * P:(k + 1) * P], ident[0:NK, 0:NK])
            last.then_inc(U["ctx_t"], 1)
            pe.wait_ge(U["ctx_copied"], 1)
            pe.wait_ge(U["attn_w_loaded"], 32)
            pe.wait_ge(U["gate_w_loaded"], 16)
            pe_attention(pe, 0)
            pe_experts(pe, 0)
            pe.wait_ge(U["w1_raw_loaded"], 80)
            pe.wait_ge(E[0]["y_copied"], NS)
            for k in range(KC):
                for c in range(2):
                    nc.tensor.transpose(PS[:, k, c * P:(c + 1) * P], rq[:, c, k * P:(k + 1) * P], ident[:])
                    nc.tensor.transpose(PS[:, 2 + k, c * P:(c + 1) * P], rc[:, c, k * P:(k + 1) * P], ident[:])
                nc.tensor.transpose(PS[:, 4 + k, 0:2 * HD], rkv[:, k * P:(k + 1) * P], ident[0:2 * HD, 0:2 * HD])
                last = nc.tensor.transpose(PS[:, 6 + k, 0:NE + 1], rg[:, k * P:(k + 1) * P],
                                           ident[0:NE + 1, 0:NE + 1])
            last.then_inc(U["w1_t"], 1)
            pe.wait_ge(U["w1_copied"], 1)
            pe_attention(pe, 1)
            pe_experts(pe, 1)


_INS = ['x', 'ctx_1024', 'g_xattn', 'g_ffn', 'L0_xattn_W_qkv', 'L0_xattn_W_proj', 'L0_xattn_b_proj',
        'L0_ffn_gate_w', 'L0_ffn_w1', 'L0_ffn_b1', 'L0_ffn_w2', 'L0_ffn_b2', 'L1_xattn_Wq', 'L1_xattn_Wkv',
        'L1_xattn_Wc', 'L1_ffn_gate_w', 'L1_ffn_w_gate', 'L1_ffn_w_up', 'L1_ffn_w_down', 'L1_ffn_sw_gate',
        'L1_ffn_sw_up', 'L1_ffn_sw_down', 'L1_ffn_shared_gate_w']
_OUTS = [((NB, S, D), 'float32')]


def kernel(**inputs):
    import numpy as _np
    import concourse.bacc as _bacc
    from concourse import mybir as _mybir
    from concourse.bass_utils import run_bass_kernel_spmd as _run

    nc = _bacc.Bacc("TRN2", target_bir_lowering=False, num_devices=1)
    arrays, args = {}, []
    for name in _INS:
        a = _np.ascontiguousarray(inputs[name])
        arrays[f"in_{name}_dram"] = a
        args.append(nc.dram_tensor(f"in_{name}_dram", a.shape, _mybir.dt.from_np(a.dtype), kind="ExternalInput").ap())
    for i, (shape, dtype) in enumerate(_OUTS):
        dt = _mybir.dt.from_np(_np.dtype(dtype))
        args.append(nc.dram_tensor(f"out_{i}_dram", shape, dt, kind="ExternalOutput").ap())
    program(nc, *args)
    r = _run(nc, [arrays], core_ids=[0])
    return r.results[0]["out_0_dram"]
```

```python
from contextlib import ExitStack

import concourse.bass as bass
from concourse import mybir

F32 = mybir.dt.float32
BF16 = mybir.dt.bfloat16
I32 = mybir.dt.int32
U32 = mybir.dt.uint32
ALU = mybir.AluOpType
ACT = mybir.ActivationFunctionType
AX = mybir.AxisListType

P = 128
NB, S, D = 2, 1024, 256
NK = 77
H, HD = 16, 16
T = NB * S
NT = T // P
KC = D // P
G = 512
QT_ = G // P
GB = S // G
HH = H // 2
HK = HH * NK
JT = -(-HK // P)
ROWS = [min(P, HK - P * j) for j in range(JT)]
QK = HK // 2
VW = HD + 1
SCALE = HD ** -0.5
EPS = 1e-5
NE, TOPK = 8, 2
DX = D + 1
F0, F1 = 1024, 352
FC0 = F0 // P
C1 = [(0, 128), (128, 128), (256, 96)]
NS = (T * TOPK + NE * (P - 1)) // P
NG = NT * TOPK
W0E = KC * F0
WG1, WD1 = KC * 2 * F1, 3 * D
BIG = 1.0e30
LATE = 5
YG0 = (NE + LATE) * W0E - NT * TOPK * D


class Chain:

    def __init__(self, eng, sem, base=0, per=0):
        self.eng, self.sem, self.base, self.per, self.n = eng, sem, base, per, 0

    def done(self, ins, after=None):
        self.n += 1
        ins.then_inc(self.sem, 1)
        self.eng.wait_ge(self.sem, self.base * self.per + self.n if self.per else self.n)
        if after:
            after(self.eng)

    def close(self):
        assert self.n == self.per, self.n


def runs(L):
    n = NS + (NT if L else 0)
    found = [("one", i, 0) for i in range(4)]
    if L:
        found += [("loop", 2, NT // 2 - 1)] + [("one", i, 0) for i in range(NT - 2, NT + 4)]
        found += [("loop", NT // 2 + 2, (n - 1) // 2)]
    else:
        found += [("loop", 2, (n - 1) // 2)]
    return found + [("one", i, 0) for i in range((n - 1) // 2 * 2, n)]


def over_tiles(eng, L, step):
    for kind, a, b in runs(L):
        if kind == "loop":
            with eng.Fori(a, b) as h:
                step(h, 0)
                step(h, 1)
        else:
            step(a // 2, a % 2)


def program(nc, x, ctx, g_xattn, g_ffn, wqkv0, wproj0, bproj0, gate0, w1, b1, w2, b2,
            wq1, wkv1, wc1, gate1, wg1, wu1, wd1, swg, swu, swd, sgw, out):
    with ExitStack() as stack:
        def sb(name, shape, dt=F32):
            return stack.enter_context(nc.sbuf_tensor(name, shape, dt))

        def sem(name):
            return stack.enter_context(nc.semaphore(name))

        def sems(names, suffix):
            return {k: sem(k + suffix) for k in names.split()}

        xslots_of = [nc.dram_tensor(f"xslots{L}", [(NS + NT * L) * P, DX], F32).ap() for L in range(2)]
        results = nc.dram_tensor("results", [1 + TOPK * T, D], F32).ap()
        X = sb("X", [P, NT * D])
        XN = sb("XN", [P, NT * DX])
        W = sb("W", [P, 2 * NE * W0E])
        AW = sb("AW", [P, KC, 4 * D])
        CT = sb("CT", [P, KC, NB * NK])
        ident = sb("ident", [P, P])
        identb = sb("identb", [P, P], BF16)
        TG = sb("TG", [P, 4])
        blockm = sb("blockm", [P, HH])
        maskv = sb("maskv", [P, JT, HH])
        maskc = sb("maskc", [P, JT, HH])
        b1t = sb("b1t", [3 * NE, F0], BF16)
        b2t = sb("b2t", [3 * NE, D], BF16)
        gwt = sb("gwt", [P, KC, NE + 1])
        slot = sb("slot", [P, NG], U32)
        wgt = sb("wgt", [P, 3, NT])
        texp = sb("texp", [P, NS], I32)
        selc = sb("selc", [3 * NE, NS])
        onesb = sb("onesb", [24, P], BF16)
        onec = sb("onec", [P, 1])
        small = sb("small", [P, 128])
        arena = sb("arena", [P, 7936])
        PS = stack.enter_context(nc.psum_tensor("PS", [P, 8, 512], F32))

        STAT = small[:, 0:24].rearrange("p (t s) -> p t s", t=QT_)
        MV = small[:, 24:32].rearrange("p (t s) -> p t s", t=QT_)
        RSTD, VEPS, HALF = small[:, 32:36], small[:, 36:40], small[:, 40:44]
        RD = [small[:, 44:60], small[:, 104:120]]
        YID = small[:, 80:82].bitcast(U32)
        mark = small[:, 124:128]
        CNT = small[:, 60:65]
        KBI = small[:, 65:70]
        rmod = small[0:3 * NE, 70:71]
        prow = small[0:3 * NE, 71:72]
        bm = small[0:3 * NE, 72:75]

        iota77 = sb("iota77", [P, NK])
        SQ = sb("SQ", [P, NK])

        def cutter(memory):
            at = [0]

            def take(n, dt=F32):
                at[0] += n
                assert at[0] <= memory.shape[1], (at[0], memory.shape)
                view = memory[:, at[0] - n:at[0]]
                return view if dt is F32 else view.bitcast(dt)

            return take

        take = cutter(arena)
        PR = take(10 * G).rearrange("p (s q) -> p s q", s=2 * JT)
        CR = arena[:, 0:2 * HK].rearrange("p (k n) -> p k n", k=KC)
        SR = arena[:, 3 * G:3 * G + JT * P]
        XNT = arena[:, 6 * G:8 * G].rearrange("p (k q) -> p k q", k=KC)
        XNA = arena[:, 8 * G:10 * G].rearrange("p (t d) -> p t d", t=QT_)
        QF = take(GB * KC * G).rearrange("p (g k q) -> p g k q", g=GB, k=KC)
        LG = take(NT * (NE + 1))
        IND = take(HK, BF16).rearrange("p (f n) -> p f n", f=2)[0:H]
        take = cutter(W[:, (NE + LATE) * W0E:])
        KF = take(2 * HK).rearrange("p (f n) -> p f n", f=2)
        KB = take(HK, BF16).rearrange("p (f n) -> p f n", f=2)
        VF = take(2 * JT * HH * VW).rearrange("p (f j h v) -> p f j h v", f=2, j=JT, h=HH)
        QB = take(KC * G // 2, BF16).rearrange("p (k q) -> p k q", k=KC)
        MX = take(QT_ * H // 2, BF16).rearrange("p (t h) -> p t h", t=QT_)
        MT = take(G // 2, BF16)[0:H]
        OA = take(2 * D).rearrange("p (u d) -> p u d", u=2)
        OT = take(2 * D).rearrange("p (u k q) -> p u k q", u=2, k=KC)
        bproj = take(D)
        rt = take(2 * D)
        TOP = rt[:, 0:8 * QT_].rearrange("p (t n) -> p t n", t=QT_)
        TOPI = rt[:, 8 * QT_:16 * QT_].bitcast(U32).rearrange("p (t n) -> p t n", t=QT_)
        IDX = rt[:, 16 * QT_:17 * QT_]
        RT = rt.rearrange("p (u k q) -> p u k q", u=2, k=KC)
        used = take(HK // 2, BF16)[0:1]

        take = cutter(arena)
        GE = NG * NE
        R_M = take(GE).rearrange("p (g e) -> p g e", g=NG)
        R_a, R_b, R_c, R_d = take(GE), take(GE), take(GE), take(320)
        R_u, R_1, R_i, R_rs, R_j = take(P), take(P), take(NT * NE), take(GE), take(NS + 1)

        FB = []
        for L in range(2):
            take = cutter(W[:, (NE + 1) * (WG1 + WD1):] if L else arena)
            FB.append({
                "H": take(2 * F0).rearrange("p (u n) -> p u n", u=2),
                "HT": take(2 * F0).rearrange("p (u c q) -> p u c q", u=2, c=FC0),
                "XS": take(2 * DX).rearrange("p (u d) -> p u d", u=2),
                "XT": take(2 * D).rearrange("p (u k q) -> p u k q", u=2, k=KC),
                "Y": take(2 * D).rearrange("p (u d) -> p u d", u=2)})
        SEL = AW[0:3 * NE, 0, 0:2 * P].bitcast(BF16).rearrange("p (w u q) -> p w u q", w=2, u=2)
        raw1 = arena[:, 4 * F0 + 4 * D + 2 * DX:]
        rq = raw1[:, 0:2 * D].rearrange("p (c d) -> p c d", c=2)
        rc = raw1[:, 2 * D:4 * D].rearrange("p (c d) -> p c d", c=2)
        rkv = raw1[0:2 * HD, 4 * D:5 * D]
        rg = raw1[0:NE + 1, 5 * D:6 * D]
        YG = W[:, YG0:(NE + LATE) * W0E].rearrange("p (t k d) -> p t k d", t=NT, k=TOPK)

        XNt = XN[:, :].rearrange("p (t d) -> p t d", t=NT)
        XNR = XNt[:, NT - QT_:, 0:D]
        FILLS = 13
        ZW = NS * DX // FILLS
        zeros = XN[:, 0:ZW]
        take = cutter(XN[:, ZW:])
        ctx_raw = take(NB * D)[0:NK].rearrange("p (b d) -> p b d", b=NB)
        bst = take(F0 + D)[0:3 * NE]
        bw = (F0 + D) // 2
        b_rest = take(bw)[0:3 * NE]
        b_high, b_mid = [take(bw // 2, BF16)[0:3 * NE] for _ in range(2)]
        Xt = X[:, :].rearrange("p (t d) -> p t d", t=NT)
        xtile = x.rearrange("b (t p) d -> p (b t) d", p=P)
        otile = out.rearrange("b (t p) d -> p (b t) d", p=P)
        W0a, W0b = W[:, 0:NE * W0E], W[:, NE * W0E:2 * NE * W0E]
        W1a, W1b = W[:, 0:(NE + 1) * WG1], W[:, (NE + 1) * WG1:(NE + 1) * (WG1 + WD1)]
        NW = [NE, NE + 1]
        NTB = S // P

        def tile_at(b, g, q=0):
            return b * (NTB * D) + (g * QT_ + q) * D

        U = sems("x_loaded ctx_loaded attn_w_loaded bias_loaded gates_loaded gate_w_loaded waits_settled zeros_set rows_zeroed "
                 "consts_set bias_split own_split ctx_t ctx_copied tanh_done bproj_ready own_pool own_dve w0_loaded "
                 "w1_loaded w1_raw_loaded w1_t w1_copied out_stored", "")
        A = [sems("own_dve own_pool rstd ln_done x_t x_t_copied q_ready q_copied stats "
                  "ctx_rep k_ready k_built kb_copied qb_copied v_ready v_built smax smax_used "
                  "mx_t mx_copied s_ready exp_done o_ready o_done o_t o_t_copied y_ready x_added xn_kept "
                  "row_used logits_copied "
                  + ("s77 s77_used counted c_ready cnt_bias own_first pool_added" if L else "xb_added"), str(L))
             for L in range(2)]
        R = [sems("router_on r_consts onehot totals exp_in exp_out routed scattered numbered router_own " + ("shared_stored" if L else ""), str(L))
             for L in range(2)]
        E = [sems("xs_loaded_0 xs_loaded_1 xs_t xt_copied h_ready h_act h_t ht_copied yt_ready "
                  "y_copied y_stored_0 y_stored_1 fetched_0 fetched_1 row_kept combined " + ("h_mul fetched_2 fetched_3 own" if L else
                                                                        "sel_up sel_down"), str(L))
             for L in range(2)]

        block = stack.enter_context(nc.Block())

        def settle(eng):
            eng.sem_inc(U["waits_settled"], 1)

        def after(eng, semaphore, n):
            eng.wait_ge(semaphore, n + 1)

        TURNS = GB + NTB
        AHEAD = 2
        R_AT = 4

        def q_bank(L, g):
            return 6 if L == 0 and g else 2

        def first_maxima(L, f, j):
            n = 4 * QT_
            at, tiles = f * JT + j - 2, 2 * JT - 2
            return range(n * at // tiles, n * (at + 1) // tiles) if L == 0 and at >= 0 else ()

        CREDITS = {
            "pool": "rstd xb_added xn_kept",
            "act": "x_t_copied q_copied kb_copied qb_copied mx_copied exp_done o_t_copied logits_copied",
            "dve": "stats ln_done s77_used counted cnt_bias ctx_rep k_built v_built smax_used o_done x_added",
            "pe": "x_t q_ready s77 c_ready k_ready v_ready smax mx_t s_ready o_ready o_t y_ready row_used"}

        def count_from_one(eng, name):
            for L in range(2):
                for k in CREDITS[name].split():
                    if k in A[L]:
                        eng.sem_inc(A[L][k], 1)

        def experts_io(sp, L):
            e, n, lead, xslots = E[L], NS + (NT if L else 0), (NT // 2 if L else 0), xslots_of[L]

            def row(h, u, shared):
                if shared:
                    return h * (2 * P) + (NS + u) * P
                return h * (2 * P) + (u - (NT if L else 0)) * P

            def load(h, u, first=False):
                shared = at[0] == "shared"
                if not first:
                    sp.wait_ge(e["xs_t"], h * 2 + u - 1)
                    if not shared and not (isinstance(h, int) and h == lead):
                        sp.wait_ge(e["row_kept"], (h - lead) * 2 + u - 1)
                w = D if shared else DX
                sp.dma_start(FB[L]["XS"][:, u, 0:w],
                             xslots[bass.ds(row(h, u, shared), P), 0:w]).then_inc(e[f"xs_loaded_{u}"], 16)

            at = ["shared" if L else "routed"]
            if L:
                sp.wait_ge(R[1]["shared_stored"], 16)
                sp.wait_ge(R[1]["router_on"], 1)
            else:
                sp.wait_ge(R[0]["scattered"], 16 * NG)
            for u in range(2):
                load(0, u, first=True)
            for u in range(2):
                load(1, u)
            lo = 2
            if L:
                with sp.Fori(2, NT // 2) as h:
                    for u in range(2):
                        load(h, u)
                sp.wait_ge(R[1]["scattered"], 16 * NG)
                at[0] = "routed"
                lo = NT // 2 + 2
                for h in range(NT // 2, lo):
                    for u in range(2):
                        load(h, u)
            with sp.Fori(lo, n // 2) as h:
                for u in range(2):
                    load(h, u)
            if n % 2:
                load(n // 2, 0)

        def fetch(sp, L, b):
            for g in range(GB):
                t = b * NTB + g * QT_
                for c in range(TOPK):
                    at = 1 + c * T + t * P
                    sp.dma_start(YG[:, t:t + QT_, c],
                                 results[at:at + QT_ * P].rearrange("(t p) d -> p t d", p=P)
                                 ).then_inc(E[L][f"fetched_{(t // QT_) if L else g}"], 16)

        def wait_results(sp, L):
            sp.wait_ge(E[L]["y_stored_0"], 16 * ((NS + 1) // 2))
            sp.wait_ge(E[L]["y_stored_1"], 16 * (NS // 2))

        @block.sync
        def _(sp):
            sp.dma_start(Xt[:, 0:NTB], xtile[:, 0:NTB]).then_inc(U["x_loaded"], 16)
            sp.dma_start(ctx_raw, ctx.rearrange("b k d -> k b d")).then_inc(U["ctx_loaded"], 16)
            sp.dma_start(AW[:, :, 0:3 * D], wqkv0.rearrange("(k p) n -> p k n", p=P)).then_inc(U["attn_w_loaded"], 16)
            sp.dma_start(AW[:, :, 3 * D:], wproj0.rearrange("(k p) n -> p k n", p=P)).then_inc(U["attn_w_loaded"], 16)
            sp.wait_ge(U["x_loaded"], 16)
            sp.dma_start(Xt[:, NTB:], xtile[:, NTB:]).then_inc(U["x_loaded"], 16)
            sp.wait_ge(U["attn_w_loaded"], 32)
            sp.wait_ge(U["zeros_set"], 1)
            for L in range(2):
                z = xslots_of[L][0:NS * P].rearrange("(p r) d -> p (r d)", p=P)
                for i in range(FILLS):
                    sp.dma_start(z[:, i * ZW:(i + 1) * ZW], zeros).then_inc(U["rows_zeroed"], 16)

            def load_w1(e):
                sp.dma_start(W0a[:, bass.ds(e * W0E, W0E)].rearrange("p (k n) -> p k n", k=KC),
                             w1[bass.ds(e, 1)].rearrange("e (k p) n -> p (e k) n", p=P)).then_inc(U["w0_loaded"], 16)

            def load_w2(e):
                sp.dma_start(W0b[:, bass.ds(e * W0E, W0E)].rearrange("p (c n) -> p c n", c=FC0),
                             w2[bass.ds(e, 1)].rearrange("e (c p) n -> p (e c) n", p=P)).then_inc(U["w0_loaded"], 16)

            with sp.Fori(0, LATE) as e:
                load_w1(e)
                load_w2(e)
            with sp.Fori(LATE, NE) as e:
                load_w1(e)
            sp.wait_ge(R[0]["totals"], 1)
            with sp.Fori(LATE, NE) as e:
                load_w2(e)
            sp.wait_ge(R[0]["routed"], 1)
            sp.dma_start(rq, wq1.rearrange("(c p) d -> p c d", p=P)).then_inc(U["w1_raw_loaded"], 16)
            sp.dma_start(rc, wc1.rearrange("(c p) d -> p c d", p=P)).then_inc(U["w1_raw_loaded"], 16)
            sp.dma_start(rkv, wkv1).then_inc(U["w1_raw_loaded"], 16)
            sp.dma_start(rg[0:NE], gate1).then_inc(U["w1_raw_loaded"], 16)
            sp.dma_start(rg[NE:NE + 1], sgw).then_inc(U["w1_raw_loaded"], 16)
            experts_io(sp, 0)

            def up_weights(e, g_, u_):
                ga = W1a[:, bass.ds(e * WG1, WG1)].rearrange("p (w k n) -> p w k n", w=2, k=KC)
                sp.dma_start(ga[:, 0], g_.rearrange("(k p) n -> p k n", p=P)).then_inc(U["w1_loaded"], 16)
                sp.dma_start(ga[:, 1], u_.rearrange("(k p) n -> p k n", p=P)).then_inc(U["w1_loaded"], 16)

            def down_weights(e, d_):
                da = W1b[:, bass.ds(e * WD1, WD1)].rearrange("p (c n) -> p c n", c=3)
                sp.dma_start(da[:, 0:2], d_[0:2 * P].rearrange("(c p) n -> p c n", p=P)).then_inc(U["w1_loaded"], 16)
                sp.dma_start(da[0:F1 - 2 * P, 2], d_[2 * P:F1]).then_inc(U["w1_loaded"], 16)

            one = lambda w, e: w[bass.ds(e, 1)].rearrange("e a b -> (e a) b")
            wait_results(sp, 0)
            for b in range(NB):
                fetch(sp, 0, b)
                for g in range(GB):
                    sp.wait_ge(E[0][f"fetched_{g}"], (b + 1) * (16 * TOPK))
            up_weights(NE, swg, swu)
            with sp.Fori(0, NE) as e:
                up_weights(e, one(wg1, e), one(wu1, e))
            clear = (YG0 - NE * WG1 - WG1) // WD1
            with sp.Fori(0, clear) as e:
                down_weights(e, one(wd1, e))
            sp.wait_ge(E[0]["combined"], NT)
            with sp.Fori(clear, NE) as e:
                down_weights(e, one(wd1, e))
            down_weights(NE, swd)
            experts_io(sp, 1)
            wait_results(sp, 1)
            for b in range(NB):
                fetch(sp, 1, b)
            for t in range(NT):
                sp.wait_ge(E[1]["combined"], t + 1)
                sp.dma_start(otile[:, t], Xt[:, t]).then_inc(U["out_stored"], 16)
            sp.wait_ge(U["out_stored"], 16 * NT)

        def combine(dve, L, own, b, g, arrived):
            dve.wait_ge(E[L][f"fetched_{arrived}"], (1 if L else b + 1) * (16 * TOPK))
            for c in range(TOPK):
                for t in range(b * NTB + g * QT_, b * NTB + (g + 1) * QT_):
                    ins = nc.vector.scalar_tensor_tensor(Xt[:, t], YG[:, t, c], wgt[:, c, t:t + 1], Xt[:, t],
                                                         ALU.mult, ALU.add)
                    if c == TOPK - 1:
                        ins.then_inc(E[L]["combined"], 1)
                if c == 0:
                    own.done(ins)

        def split_biases(pool):
            own = Chain(pool, U["own_split"])
            pool.wait_ge(U["bias_loaded"], 96)
            for to, at in ((b1t[:, 0:bw], 0), (b1t[:, bw:], bw), (b2t[:], F0)):
                n = to.shape[1]
                b, rest, high, mid = bst[:, at:at + n], b_rest[:, 0:n], b_high[:, 0:n], b_mid[:, 0:n]
                own.done(nc.gpsimd.tensor_copy(high, b))
                own.done(nc.gpsimd.tensor_tensor(rest, b, high, ALU.subtract))
                own.done(nc.gpsimd.tensor_copy(mid, rest))
                own.done(nc.gpsimd.tensor_tensor(rest, rest, mid, ALU.subtract))
                own.done(nc.gpsimd.tensor_scalar(b, high, bm[:, 0:1], None, ALU.mult))
                own.done(nc.gpsimd.tensor_scalar(rest, rest, bm[:, 2:3], None, ALU.mult))
                own.done(nc.gpsimd.tensor_tensor(rest, rest, b, ALU.add))
                own.done(nc.gpsimd.tensor_scalar(mid, mid, bm[:, 1:2], None, ALU.mult))
                own.done(nc.gpsimd.tensor_tensor(to, rest, mid, ALU.add))
            pool.sem_inc(U["bias_split"], 1)

        def pool_layer(pool, L):
            a, r, e, xslots = A[L], R[L], E[L], xslots_of[L]

            def rstd(own, n):
                after(pool, a["stats"], n)
                settle(pool)
                own.done(nc.gpsimd.tensor_scalar(VEPS, MV[:, :, 1], EPS, None, ALU.add))
                nc.gpsimd.tensor_tensor(RSTD, VEPS, HALF, ALU.pow).then_inc(a["rstd"], 1)

            own = Chain(pool, a["own_pool"])
            for b in range(NB):
                for g in range(GB):
                    rstd(own, b * (2 * GB) + g + 1)
                if L == 0:
                    after(pool, a["ln_done"], b * (2 * GB) + GB)
                    pool.wait_ge(U["bproj_ready"], 1)
                    for g in range(GB):
                        xg = X[:, tile_at(b, g):tile_at(b, g) + QT_ * D].rearrange("p (t d) -> p t d", t=QT_)
                        nc.gpsimd.tensor_tensor(xg, xg, bproj[:, None, :].to_broadcast([P, QT_, D]),
                                                ALU.add).then_inc(a["xb_added"], 1)
                    if b == 0:
                        split_biases(pool)
                elif b == 0:
                    added = Chain(pool, a["pool_added"])
                    for g in range(GB):
                        pool.wait_ge(E[0][f"fetched_{g}"], 2 * (16 * TOPK))
                        t0 = NTB + g * QT_
                        for t in range(t0, t0 + QT_):
                            for c in range(TOPK):
                                last = nc.gpsimd.tensor_scalar(YG[:, t, c], YG[:, t, c], wgt[:, c, t:t + 1], None,
                                                               ALU.mult)
                        added.done(last)
                        for c in range(TOPK):
                            ins = nc.gpsimd.tensor_tensor(Xt[:, t0:t0 + QT_], Xt[:, t0:t0 + QT_],
                                                          YG[:, t0:t0 + QT_, c], ALU.add)
                            if c == 0:
                                added.done(ins)
                        ins.then_inc(E[0]["combined"], QT_)
                for g in range(GB):
                    rstd(own, b * (2 * GB) + GB + g + 1)
                    after(pool, a["ln_done"], b * (2 * GB) + GB + g + 1)
                    if (b, g) != (NB - 1, GB - 1):
                        t = b * NTB + g * QT_
                        nc.gpsimd.tensor_copy(XNt[:, t:t + QT_, 0:D], XNR).then_inc(a["xn_kept"], 1)
            if L:
                after(pool, a["xn_kept"], GB * NB - 1)
                pool.dma_start(xslots[NS * P:(NS + NT) * P, 0:D].rearrange("(t p) d -> p t d", p=P),
                               XNt[:, :, 0:D]).then_inc(r["shared_stored"], 16)
            pool.wait_ge(r["router_on"], 1)
            nc.gpsimd.iota(R_i.rearrange("p (t e) -> p t e", t=NT), pattern=[[0, NT], [1, NE]], base=0,
                           channel_multiplier=0, allow_small_or_imprecise_dtypes=True).then_inc(r["r_consts"], 1)
            nc.gpsimd.memset(R_u, 1.0).then_inc(r["r_consts"], 1)
            nc.gpsimd.memset(R_1, 1.0).then_inc(r["r_consts"], 1)
            nc.gpsimd.memset(R_rs, 1.0).then_inc(r["r_consts"], 1)
            nc.gpsimd.iota(R_j, pattern=[[1, NS + 1]], base=0, channel_multiplier=0,
                           allow_small_or_imprecise_dtypes=True).then_inc(r["r_consts"], 1)
            pool.wait_ge(r["r_consts"], 5)
            nc.gpsimd.affine_select(out=R_u, in_=R_u, compare_op=ALU.is_gt, fill=0.0, base=0,
                                    pattern=[[1, P]], channel_multiplier=-1).then_inc(r["r_consts"], 1)
            rs = R_rs.rearrange("p (e g) -> p e g", e=NE)
            nc.gpsimd.affine_select(out=rs, in_=rs, compare_op=ALU.not_equal, fill=0.0, base=0,
                                    pattern=[[0, NE], [1, NG]], channel_multiplier=0).then_inc(r["r_consts"], 1)
            def number_rows(c):
                nc.gpsimd.iota(XNt[:, :, D].bitcast(I32), pattern=[[P, NT]], base=1 + c * T, channel_multiplier=1,
                               allow_small_or_imprecise_dtypes=True).then_inc(r["numbered"], 1)

            if L:
                pool.wait_ge(r["shared_stored"], 16)
            number_rows(0)
            pool.wait_ge(r["routed"], 1)
            for c in range(TOPK):
                if c:
                    pool.wait_ge(r["scattered"], 16 * NT)
                    number_rows(c)
                pool.wait_ge(r["numbered"], c + 1)
                for t in range(NT):
                    g = c * NT + t
                    pool.indirect_dma_start(xslots[0:NS * P], bass.IndirectOffsetOnAxis(ap=slot[:, g:g + 1], axis=0),
                                            XNt[:, t], None).then_inc(r["scattered"], 16)
            lead = NT // 2 if L else 0

            def keep_rows(h, u):
                pool.wait_ge(e[f"xs_loaded_{u}"], (h + lead) * 16 + 16)
                if not (isinstance(h, int) and h == 0):
                    pool.wait_ge(e[f"y_stored_{u}"], h * 16)
                settle(pool)
                nc.gpsimd.tensor_copy(YID[:, u:u + 1], FB[L]["XS"][:, u, D:DX].bitcast(U32)).then_inc(e["row_kept"], 1)

            def store(h, u):
                pool.wait_ge(e["row_kept"], h * 2 + u + 1)
                pool.wait_ge(e["y_copied"], (h + lead) * 2 + u + 1)
                if u:
                    pool.wait_ge(e["y_stored_0"], h * 16 + 16)
                elif not (isinstance(h, int) and h == 0):
                    pool.wait_ge(e["y_stored_1"], h * 16)
                settle(pool)
                pool.indirect_dma_start(results, bass.IndirectOffsetOnAxis(ap=YID[:, u:u + 1], axis=0),
                                        FB[L]["Y"][:, u], None).then_inc(e[f"y_stored_{u}"], 16)

            keep_rows(0, 0)
            keep_rows(0, 1)
            store(0, 0)
            with pool.Fori(1, NS // 2) as h:
                keep_rows(h, 0)
                store(h - 1, 1)
                keep_rows(h, 1)
                store(h, 0)
            for j in range(NS // 2 * 2 - 1, NS):
                if j + 1 < NS:
                    keep_rows((j + 1) // 2, (j + 1) % 2)
                store(j // 2, j % 2)

        @block.gpsimd
        def _(pool):
            count_from_one(pool, "pool")
            own = Chain(pool, U["own_pool"])
            nc.gpsimd.memset(zeros, 0.0).then_inc(U["zeros_set"], 1)
            nc.gpsimd.memset(HALF, -0.5)
            nc.gpsimd.memset(onesb[:], 1.0)
            nc.gpsimd.memset(onec[:], 1.0)
            nc.gpsimd.memset(blockm[:], 1.0)
            nc.gpsimd.memset(maskv[:], 1.0)
            nc.gpsimd.memset(IND, -1.0)
            nc.gpsimd.memset(bm, 1.0)
            nc.gpsimd.iota(prow, pattern=[[0, 1]], base=0, channel_multiplier=1,
                           allow_small_or_imprecise_dtypes=True)
            nc.gpsimd.iota(iota77[:], pattern=[[1, NK]], base=0, channel_multiplier=0,
                           allow_small_or_imprecise_dtypes=True)
            own.done(nc.gpsimd.memset(ident[:], 0.0))
            own.done(nc.gpsimd.affine_select(out=ident[:], in_=ident[:], compare_op=ALU.not_equal, fill=1.0,
                                             base=0, pattern=[[-1, P]], channel_multiplier=1))

            def band(ap, pattern, base, mult, width):
                own.done(nc.gpsimd.affine_select(out=ap, in_=ap, compare_op=ALU.is_ge, fill=0.0, base=base,
                                                 pattern=pattern, channel_multiplier=mult))
                own.done(nc.gpsimd.affine_select(out=ap, in_=ap, compare_op=ALU.is_ge, fill=0.0,
                                                 base=width - 1 - base, pattern=[[-s, n] for s, n in pattern],
                                                 channel_multiplier=-mult))

            band(bm, [[-NE, 3]], 0, 1, NE)
            band(blockm[:], [[-HD, HH]], 0, 1, HD)
            band(maskv[:], [[P, JT], [-NK, HH]], 0, 1, NK)
            for f in range(2):
                band(IND[:, f], [[1, HK]], f * HH * NK, -NK, NK)
            nc.gpsimd.tensor_copy(identb[:], ident[:]).then_inc(U["consts_set"], 1)
            pool_layer(pool, 0)
            pool_layer(pool, 1)

        def act_attention(act, L):
            a, r = A[L], R[L]
            nh = 1 if L else 2

            def keep_transposed(b, n):
                after(act, a["x_t"], b * TURNS + n)
                nc.scalar.activation(XNT, PS[:, 0:2], ACT.Copy).then_inc(a["x_t_copied"], 1)

            def keep_maxima(n0):
                after(act, a["mx_t"], n0 + 1)
                nc.scalar.activation(MT, PS[0:H, 0, 0:G // 2].bitcast(BF16), ACT.Copy).then_inc(a["mx_copied"], 1)

            def keep_row(b, g, q):
                after(act, a["x_t"], b * TURNS + GB + g * QT_ + q + 1)
                after(act, a["row_used"], b * NTB + g * QT_ + max(q - 1, 0))
                nc.scalar.activation(RT[:, q % 2], PS[:, 2 + q % 2, 0:D].rearrange("p (k q) -> p k q", k=KC),
                                     ACT.Copy).then_inc(a["x_t_copied"], 1)

            def keep_logits(b, g):
                after(act, a["row_used"], b * NTB + (g + 1) * QT_)
                w = NW[L]
                nc.scalar.activation(LG[:, bass.ds(b * (NTB * w) + g * QT_ * w, QT_ * w)],
                                     PS[:, 6, 0:QT_ * w], ACT.Copy).then_inc(a["logits_copied"], 1)

            with act.Fori(0, NB) as b:
                for g in range(GB):
                    keep_transposed(b, g + 1)
                    after(act, a["q_ready"], b * GB + g + 1)
                    nc.scalar.activation(QF[:, g], PS[:, q_bank(L, g):q_bank(L, g) + 2], ACT.Copy).then_inc(a["q_copied"], 1)
                    if g == 0:
                        after(act, a["k_built"], b + 1)
                        nc.scalar.activation(KB[:, 0:nh], KF[:, 0:nh], ACT.Copy).then_inc(a["kb_copied"], 1)
                        after(act, a["smax"], b * (GB * 4 * QT_))
                        after(act, a["q_copied"], b * GB + 1)
                        nc.scalar.activation(QB, QF[:, g], ACT.Copy).then_inc(a["qb_copied"], 1)
                for g in range(GB):
                    n0 = b * GB + g
                    if g == 0:
                        after(act, a["q_copied"], b * GB + GB)
                        keep_maxima(n0)
                    if L:
                        after(act, a["cnt_bias"], b + 1)
                    for i in range(2 * JT):
                        if g == 1 and R_AT < i <= R_AT + QT_:
                            keep_row(b, 0, i - R_AT - 1)
                        if g + 1 < GB and i == 2:
                            after(act, a["smax"], (n0 + 1) * (4 * QT_))
                            nc.scalar.activation(QB, QF[:, g + 1], ACT.Copy).then_inc(a["qb_copied"], 1)
                        rows = ROWS[i % JT]
                        after(act, a["s_ready"], n0 * (2 * JT) + i + 1)
                        bias = {"bias": KBI[0:rows, i % JT:i % JT + 1]} if L else {}
                        nc.scalar.activation(PR[0:rows, i], PS[0:rows, 4 + i % 2], ACT.Exp, scale=SCALE,
                                             **bias).then_inc(a["exp_done"], 1)
                    if g == 1:
                        keep_logits(b, 0)
                    for q in range(QT_):
                        if q == QT_ - 1 and g + 1 < GB:
                            keep_maxima(n0 + 1)
                        after(act, a["o_t"], n0 * QT_ + q + 1)
                        nc.scalar.activation(OT[:, q % 2], PS[:, 0, 0:D].rearrange("p (k q) -> p k q", k=KC),
                                             ACT.Copy).then_inc(a["o_t_copied"], 1)
                for q in range(QT_):
                    keep_row(b, 1, q)
                keep_logits(b, 1)
            act.wait_ge(r["exp_in"], 1)
            nc.scalar.activation(wgt[:, 0], wgt[:, 0], ACT.Exp).then_inc(r["exp_out"], 1)
            if L:
                lg = LG[:, 0:NT * NW[1]].rearrange("p (t e) -> p t e", t=NT)
                nc.scalar.activation(wgt[:, 2], lg[:, :, NE], ACT.Exp, scale=-1.0).then_inc(r["exp_out"], 1)

        def act_experts(act, L):
            e, n = E[L], NS + (NT if L else 0)

            def keep_xt(i, u):
                act.wait_ge(e["xs_t"], i + 1)
                nc.scalar.activation(FB[L]["XT"][:, u], PS[:, 7, 0:D].rearrange("p (k q) -> p k q", k=KC),
                                     ACT.Copy).then_inc(e["xt_copied"], 1)

            def step(h, u):
                i = h * 2 + u
                later = not (isinstance(i, int) and i < 2)
                if L:
                    act.wait_ge(e["h_ready"], i * 2 + 1)
                    if later:
                        act.wait_ge(e["h_mul"], i - 1)
                    nc.scalar.activation(FB[L]["H"][:, u, 0:F1], PS[:, 2 * u, 0:F1], ACT.Silu).then_inc(e["h_act"], 1)
                else:
                    if later:
                        act.wait_ge(e["h_t"], i - 1)
                    for s in range(2):
                        act.wait_ge(e["h_ready"], i * 2 + s + 1)
                        nc.scalar.activation(FB[L]["H"][:, u, s * 512:(s + 1) * 512], PS[:, 2 * u + s],
                                             ACT.Gelu).then_inc(e["h_act"], 1)
                if not (isinstance(i, int) and i == n - 1):
                    keep_xt(i + 1, 1 - u)

            keep_xt(0, 0)
            over_tiles(act, L, step)

        @block.scalar
        def _(act):
            for part in range(3):
                act.dma_start(bst[part * NE:(part + 1) * NE, 0:F0], b1).then_inc(U["bias_loaded"], 16)
                act.dma_start(bst[part * NE:(part + 1) * NE, F0:], b2).then_inc(U["bias_loaded"], 16)
            act.dma_start(TG[:, 0:2], g_xattn.partition_broadcast(P)).then_inc(U["gates_loaded"], 16)
            act.dma_start(TG[:, 2:4], g_ffn.partition_broadcast(P)).then_inc(U["gates_loaded"], 16)
            act.dma_start(bproj[:], bproj0.partition_broadcast(P)).then_inc(U["gates_loaded"], 16)
            act.dma_start(gwt[:, :, 0:NE], gate0.rearrange("(k p) e -> p k e", p=P)).then_inc(U["gate_w_loaded"], 16)
            count_from_one(act, "act")
            act.wait_ge(U["gates_loaded"], 48)
            nc.scalar.activation(TG[:], TG[:], ACT.Tanh).then_inc(U["tanh_done"], 1)
            act.wait_ge(U["tanh_done"], 1)
            nc.scalar.activation(bproj[:], bproj[:], ACT.Copy, scale=TG[:, 0:1]).then_inc(U["bproj_ready"], 1)
            act.wait_ge(U["ctx_t"], 1)
            nc.scalar.activation(CT[:], PS[:, 0, 0:KC * NB * NK].rearrange("p (k n) -> p k n", k=KC),
                                 ACT.Copy).then_inc(U["ctx_copied"], 1)
            act_attention(act, 0)
            act_experts(act, 0)
            act.wait_ge(U["w1_t"], 1)
            nc.scalar.activation(AW[:, :, 0:D], PS[:, 0:2, 0:D], ACT.Copy)
            nc.scalar.activation(AW[:, :, 3 * D:4 * D], PS[:, 2:4, 0:D], ACT.Copy)
            for i in range(2):
                for k in range(KC):
                    nc.scalar.activation(
                        AW[:, k, (1 + i) * D:(1 + i) * D + P].rearrange("p (h d) -> p h d", h=HH),
                        PS[:, 4 + k, i * HD:(i + 1) * HD][:, None, :].to_broadcast([P, HH, HD]), ACT.Copy)
            nc.scalar.activation(gwt[:], PS[:, 6:8, 0:NE + 1], ACT.Copy).then_inc(U["w1_copied"], 1)
            act_attention(act, 1)
            act_experts(act, 1)

        def dve_attention(dve, L):
            a = A[L]
            nh = 1 if L else 2
            mask = maskc if L else maskv
            gate = TG[:, L:L + 1]

            def measure(own, b, n):
                g = n % GB
                if n < GB:
                    for q in range(QT_):
                        last = nc.vector.bn_stats(STAT[:, q], X[:, bass.ds(tile_at(b, g, q), D)])
                    own.done(last, settle)
                for q in range(QT_):
                    last = nc.vector.bn_aggr(MV[:, q], STAT[:, q])
                last.then_inc(a["stats"], 1)

            def norm(b, n):
                g = n % GB
                to = XNR if n >= GB else XNA
                after(dve, a["rstd"], b * (2 * GB) + n + 1)
                after(dve, a["x_t"], b * TURNS + (GB + g * QT_ if n >= GB else n))
                if n >= GB:
                    after(dve, a["xn_kept"], b * GB + g)
                for q in range(QT_):
                    last = nc.vector.tensor_scalar(to[:, q], X[:, bass.ds(tile_at(b, g, q), D)], MV[:, q, 0:1],
                                                   RSTD[:, q:q + 1], ALU.subtract, ALU.mult)
                last.then_inc(a["ln_done"], 1)

            def choose(own, b, g):
                sc = PS[:, 6 + g, 0:QT_ * NK].rearrange("p (t m) -> p t m", t=QT_)
                after(dve, a["s77"], b * GB + g + 1)
                settle(dve)
                for q in range(QT_):
                    last = nc.vector.max(TOP[:, q], sc[:, q])
                own.done(last, settle)
                for q in range(QT_):
                    last = nc.vector.max_index(TOPI[:, q], TOP[:, q], sc[:, q])
                last.then_inc(a["s77_used"], 1)
                after(dve, a["s77_used"], b * GB + g + 1)
                own.done(nc.vector.tensor_copy(IDX, TOPI[:, :, 0]))
                for q in range(QT_):
                    if g == 0 and q == 0:
                        own.done(nc.vector.tensor_scalar(SQ[:], iota77[:], IDX[:, 0:1], None, ALU.is_equal))
                    else:
                        own.done(nc.vector.scalar_tensor_tensor(SQ[:], iota77[:], IDX[:, q:q + 1], SQ[:],
                                                                ALU.is_equal, ALU.add))

            def maximum(n0, i):
                q, c = i // 4, i % 4
                if i == 0:
                    after(dve, a["mx_t"], n0)
                after(dve, a["smax"], n0 * (4 * QT_) + i + 1)
                nc.vector.tensor_reduce(MX[:, q, c * 4:c * 4 + 4],
                                        PS[:, 2 + i % 2, 0:QK].rearrange("p (h m) -> p h m", h=4),
                                        AX.X, ALU.max).then_inc(a["smax_used"], 1)

            if L:
                added = Chain(dve, a["own_first"])
                for g in range(GB):
                    combine(dve, 0, added, 0, g, g)

            with dve.Fori(0, NB) as b:
                own = Chain(dve, a["own_dve"], b, 2 * GB + NTB + ((2 + QT_) * GB + 4 if L else 0))
                if L:
                    dve.wait_ge(E[0]["combined"], b * NTB + NTB)
                else:
                    dve.wait_ge(U["x_loaded"], b * 16 + 16)
                settle(dve)
                measure(own, b, 0)
                norm(b, 0)
                measure(own, b, 1)
                if L == 0:
                    dve.wait_ge(U["ctx_copied"], 1)
                for k in range(KC):
                    last = nc.vector.tensor_copy(CR[:, k].rearrange("p (h m) -> p h m", h=HH),
                                                 CT[:, k, bass.ds(b * NK, NK)][:, None, :].to_broadcast([P, HH, NK]))
                last.then_inc(a["ctx_rep"], 1)
                after(dve, a["k_ready"], b + 1)
                for f in range(nh):
                    last = nc.vector.tensor_tensor(KF[:, f].rearrange("p (h m) -> p h m", h=HH),
                                                   PS[:, 7 - f, 0:NK][:, None, :].to_broadcast([P, HH, NK]),
                                                   blockm[:, :, None].to_broadcast([P, HH, NK]), ALU.mult)
                last.then_inc(a["k_built"], 1)
                norm(b, 1)
                if L:
                    for g in range(GB):
                        choose(own, b, g)
                if L:
                    own.done(nc.vector.memset(SR[:, HK:], 0.0))
                    nc.vector.tensor_copy(SR[:, 0:HK].rearrange("p (h m) -> p h m", h=HH),
                                          SQ[:, None, :].to_broadcast([P, HH, NK])).then_inc(a["counted"], 1)
                    after(dve, a["c_ready"], b + 1)
                    own.done(nc.vector.tensor_copy(CNT, PS[:, 6, 0:JT]))
                    own.done(nc.vector.tensor_scalar(KBI, CNT, 0.0, -BIG, ALU.is_equal, ALU.mult))
                    own.done(nc.vector.tensor_scalar(used[:].rearrange("p (w n) -> p w n", w=2), PS[0:1, 2:4, 0:QK],
                                                     0.0, -BIG, ALU.is_equal, ALU.mult))
                    nc.vector.tensor_tensor(maskc[:], maskv[:], CNT[:, :, None].to_broadcast([P, JT, HH]),
                                            ALU.mult).then_inc(a["cnt_bias"], 1)
                    after(dve, a["cnt_bias"], b + 1)
                for f in range(nh):
                    for j in range(JT):
                        for i in first_maxima(L, f, j):
                            maximum(b * GB, i)
                    after(dve, a["v_ready"], b * nh + f + 1)
                    rows = ROWS[JT - 1]
                    nc.vector.tensor_tensor(VF[:, f, 0:4, :, 0:HD],
                                            PS[:, 4].rearrange("p (j h d) -> p j h d", j=4, h=HH),
                                            mask[:, 0:4, :, None].to_broadcast([P, 4, HH, HD]), ALU.mult)
                    nc.vector.tensor_copy(VF[:, f, :, :, HD], mask[:])
                    nc.vector.tensor_tensor(VF[0:rows, f, 4, :, 0:HD],
                                            PS[0:rows, 5, 0:P].rearrange("p (h d) -> p h d", h=HH),
                                            mask[0:rows, 4, :, None].to_broadcast([rows, HH, HD]),
                                            ALU.mult).then_inc(a["v_built"], 1)
                if L:
                    for i in range(4 * QT_):
                        maximum(b * GB, i)
                for g in range(GB):
                    n0 = b * GB + g
                    if g == 1:
                        if L == 0:
                            dve.wait_ge(U["rows_zeroed"], 16 * 2 * FILLS)
                        measure(own, b, GB)
                        norm(b, GB)
                    for s in range(QT_ + 2):
                        between = s < QT_ and g + 1 < GB
                        if between:
                            for i in range(4 * s, 4 * s + 2):
                                maximum(n0 + 1, i)
                        if s < QT_:
                            o = PS[:, 6 + s % 2, 0:2 * HH * VW].rearrange("p (h v) -> p h v", h=H)
                            after(dve, a["o_ready"], n0 * QT_ + s + 1)
                            own.done(nc.vector.reciprocal(RD[s % 2], o[:, :, HD]))
                            if s >= 2:
                                after(dve, a["o_t"], n0 * QT_ + s - 1)
                            nc.vector.tensor_tensor(OA[:, s % 2].rearrange("p (h d) -> p h d", h=H), o[:, :, 0:HD],
                                                    RD[s % 2][:, :, None].to_broadcast([P, H, HD]),
                                                    ALU.mult).then_inc(a["o_done"], 1)
                        if between:
                            for i in range(4 * s + 2, 4 * s + 4):
                                maximum(n0 + 1, i)
                        if s >= 2:
                            xq = X[:, bass.ds(tile_at(b, g, s - 2), D)]
                            after(dve, a["y_ready"], n0 * QT_ + s - 1)
                            if L == 0:
                                after(dve, a["xb_added"], b * GB + GB)
                            nc.vector.scalar_tensor_tensor(xq, PS[:, 1, 0:D], gate, xq, ALU.mult,
                                                           ALU.add).then_inc(a["x_added"], 1)
                        for q in ([s - 3] if s >= 3 else []) + ([QT_ - 1] if s == QT_ + 1 else []):
                            after(dve, a["x_added"], n0 * QT_ + q + 1)
                            settle(dve)
                            last = nc.vector.bn_stats(STAT[:, q], X[:, bass.ds(tile_at(b, g, q), D)])
                            if s == QT_ + 1 and q == QT_ - 1:
                                own.done(last, settle)
                measure(own, b, GB + 1)
                norm(b, GB + 1)
                own.close()

        def dve_router(dve, L, own):
            a, r = A[L], R[L]
            after(dve, a["logits_copied"], GB * NB)
            nc.vector.memset(mark[:, 0:1], 0.0).then_inc(r["router_on"], 1)
            lg = LG[:, 0:NT * NW[L]].rearrange("p (t e) -> p t e", t=NT)[:, :, 0:NE]
            te = lambda ap: ap[:, 0:NT * NE].rearrange("p (t e) -> p t e", t=NT)
            wide = lambda ap: ap[:, :, None].to_broadcast([P, NT, NE])
            dve.wait_ge(r["r_consts"], 1)
            first = R_c[:, 0:NT]
            for c in range(TOPK):
                src = lg if c == 0 else te(R_d)
                own.done(nc.vector.tensor_reduce(wgt[:, c], src, AX.X, ALU.max))
                own.done(nc.vector.tensor_tensor(te(R_a), src, wide(wgt[:, c]), ALU.is_equal))
                own.done(nc.vector.scalar_tensor_tensor(te(R_b), te(R_a), -99.0, te(R_i), ALU.mult, ALU.add))
                own.done(nc.vector.tensor_reduce(first, te(R_b), AX.X, ALU.min))
                own.done(nc.vector.tensor_scalar(first, first, 99.0, None, ALU.add))
                oh = R_M[:, c * NT:(c + 1) * NT]
                nc.vector.tensor_tensor(oh, te(R_i), wide(first), ALU.is_equal).then_inc(r["onehot"], 1)
                dve.wait_ge(r["onehot"], c + 1)
                if c == 0:
                    own.done(nc.vector.scalar_tensor_tensor(te(R_d), oh, -BIG, lg, ALU.mult, ALU.add))
            nc.vector.tensor_tensor(wgt[:, 0], wgt[:, 1], wgt[:, 0], ALU.subtract).then_inc(r["exp_in"], 1)
            eg = lambda ap: ap.rearrange("p (e g) -> p e g", e=NE)
            dve.wait_ge(r["totals"], 1)
            dve.wait_ge(r["r_consts"], 7)
            own.done(nc.vector.tensor_copy(eg(R_a), PS[:, 5, 0:GE].rearrange("p (g e) -> p e g", e=NE)))
            own.done(nc.vector.tensor_tensor_scan(R_b, R_rs, R_a, 0.0, ALU.mult, ALU.add))
            ni, nsh, nf, ends, base = [R_c[:, 48 + 8 * i:56 + 8 * i] for i in range(5)]
            own.done(nc.vector.tensor_scalar(ni.bitcast(I32), eg(R_b)[:, :, NG - 1], float(P - 1), None, ALU.add))
            own.done(nc.vector.tensor_scalar(nsh.bitcast(I32), ni.bitcast(I32), P.bit_length() - 1, None,
                                             ALU.arith_shift_right))
            own.done(nc.vector.tensor_copy(nf, nsh.bitcast(I32)))
            own.done(nc.vector.tensor_tensor_scan(ends, R_1[:, 0:NE], nf, 0.0, ALU.mult, ALU.add))
            own.done(nc.vector.tensor_tensor(base, ends, nf, ALU.subtract))
            jt = R_d[:, 0:NS * (NE - 1)].rearrange("p (j e) -> p j e", j=NS)
            own.done(nc.vector.tensor_tensor(jt, R_j[:, 0:NS, None].to_broadcast([P, NS, NE - 1]),
                                             ends[:, None, 0:NE - 1].to_broadcast([P, NS, NE - 1]), ALU.is_ge))
            tex = R_c[:, 96:96 + NS]
            own.done(nc.vector.tensor_reduce(tex, jt, AX.X, ALU.add))
            own.done(nc.vector.tensor_copy(texp[:], tex))
            own.done(nc.vector.tensor_scalar(selc[:], tex[0:3 * NE], rmod, None, ALU.is_equal))
            own.done(nc.vector.tensor_tensor(R_a, R_b, R_a, ALU.subtract))
            own.done(nc.vector.scalar_tensor_tensor(eg(R_a), base[:, :, None].to_broadcast([P, NE, NG]), float(P),
                                                    eg(R_a), ALU.mult, ALU.add))
            ge = R_b.rearrange("p (g e) -> p g e", g=NG)
            own.done(nc.vector.tensor_tensor(ge, PS[:, 4, 0:GE].rearrange("p (g e) -> p g e", g=NG),
                                             R_a.rearrange("p (e g) -> p g e", e=NE), ALU.add))
            own.done(nc.vector.tensor_tensor(ge, ge, R_M, ALU.mult))
            own.done(nc.vector.tensor_reduce(R_c[:, 144:144 + NG], ge, AX.X, ALU.add))
            nc.vector.tensor_copy(slot[:], R_c[:, 144:144 + NG]).then_inc(r["routed"], 1)
            dve.wait_ge(r["exp_out"], 2 if L else 1)
            gate = TG[:, 2 + L:3 + L]
            own.done(nc.vector.tensor_scalar(R_c[:, 0:NT], wgt[:, 0], 1.0, None, ALU.add))
            own.done(nc.vector.reciprocal(R_c[:, 16:16 + NT], R_c[:, 0:NT]))
            own.done(nc.vector.scalar_tensor_tensor(wgt[:, 1], wgt[:, 0], gate, R_c[:, 16:16 + NT], ALU.mult,
                                                    ALU.mult))
            own.done(nc.vector.tensor_scalar(wgt[:, 0], R_c[:, 16:16 + NT], gate, None, ALU.mult))
            if L:
                own.done(nc.vector.tensor_scalar(R_c[:, 0:NT], wgt[:, 2], 1.0, None, ALU.add))
                own.done(nc.vector.reciprocal(R_c[:, 16:16 + NT], R_c[:, 0:NT]))
                own.done(nc.vector.tensor_scalar(wgt[:, 2], R_c[:, 16:16 + NT], gate, None, ALU.mult))

        def dve_experts(dve, L):
            e, n = E[L], NS + (NT if L else 0)

            def select(w, i, u, later=True):
                if later:
                    dve.wait_ge(e["yt_ready"], i - 1) if w else dve.wait_ge(e["h_ready"], i * 2 - 2)
                nc.vector.tensor_copy(SEL[:, w, u], selc[:, bass.ds(i, 1)].to_broadcast([3 * NE, P])
                                      ).then_inc(e["sel_down" if w else "sel_up"], 1)

            def multiply(i, u, later=True):
                dve.wait_ge(e["h_act"], i + 1)
                dve.wait_ge(e["h_ready"], i * 2 + 2)
                if later:
                    dve.wait_ge(e["h_t"], i - 1)
                nc.vector.tensor_tensor(FB[L]["H"][:, u, 512:512 + F1], PS[:, 2 * u + 1, 0:F1], FB[L]["H"][:, u, 0:F1],
                                        ALU.mult).then_inc(e["h_mul"], 1)

            def keep_ht(i, u, later=True):
                dve.wait_ge(e["h_t"], i + 1)
                if later:
                    dve.wait_ge(e["yt_ready"], i - 1)
                if L:
                    for c, (_, w) in enumerate(C1):
                        last = nc.vector.tensor_copy(FB[L]["HT"][0:w, u, c], PS[0:w, 4, c * P:(c + 1) * P])
                    last.then_inc(e["ht_copied"], 1)
                else:
                    nc.vector.tensor_copy(FB[L]["HT"][:, u], PS[:, 4:6].rearrange("p b (c q) -> p (b c) q", c=4)
                                          ).then_inc(e["ht_copied"], 1)

            def keep_y(h, u):
                dve.wait_ge(e["yt_ready"], h * 2 + u + 1)
                if shared(h):
                    i = h * 2 + u
                    xt = X[:, bass.ds(i * D, D)]
                    nc.vector.scalar_tensor_tensor(xt, PS[:, 6, 0:D], wgt[:, 2, bass.ds(i, 1)], xt, ALU.mult,
                                                   ALU.add).then_inc(e["y_copied"], 1)
                    return
                if not (isinstance(h, int) and h == lead):
                    dve.wait_ge(e[f"y_stored_{u}"], (h - lead) * 16)
                nc.vector.tensor_copy(FB[L]["Y"][:, u], PS[:, 6, 0:D]).then_inc(e["y_copied"], 1)

            lead, loops = (NT // 2 if L else 0), [0]

            def shared(h):
                return h < lead if isinstance(h, int) else L == 1 and loops[0] == 0

            def step(h, u):
                i = h * 2 + u
                first, last = (isinstance(i, int) and i == k for k in (0, n - 1))
                hp, up = (h, 0) if u else (h - 1, 1)
                if not L and not last:
                    select(0, i + 1, 1 - u, later=not (isinstance(i, int) and i < 1))
                if not L and not first:
                    select(1, i - 1, up, later=not (isinstance(i, int) and i < 3))
                if not first:
                    keep_ht(i - 1, up, later=not (isinstance(i, int) and i < 3))
                if L:
                    multiply(i, u, later=not (isinstance(i, int) and i < 2))
                if not first:
                    keep_y(hp, up)
                if u and not isinstance(h, int):
                    loops[0] += 1

            if not L:
                select(0, 0, 0, later=False)
            over_tiles(dve, L, step)
            if not L:
                select(1, n - 1, (n - 1) % 2)
            keep_ht(n - 1, (n - 1) % 2)
            keep_y((n - 1) // 2, (n - 1) % 2)

        @block.vector
        def _(dve):
            count_from_one(dve, "dve")
            dve_attention(dve, 0)
            own = Chain(dve, U["own_dve"])
            own.done(nc.vector.scalar_tensor_tensor(rmod, bm[:, 1:2], -float(NE), prow, ALU.mult, ALU.add))
            own.done(nc.vector.scalar_tensor_tensor(rmod, bm[:, 2:3], -2.0 * NE, rmod, ALU.mult, ALU.add))
            dve_router(dve, 0, Chain(dve, R[0]["router_own"]))
            dve_experts(dve, 0)
            dve.wait_ge(U["w1_copied"], 1)
            dve_attention(dve, 1)
            dve_router(dve, 1, Chain(dve, R[1]["router_own"]))
            dve_experts(dve, 1)
            own = Chain(dve, E[1]["own"])
            for j in range(NB * GB):
                combine(dve, 1, own, j // GB, j % GB, j)

        def pe_attention(pe, L):
            a, r = A[L], R[L]
            nh = 1 if L else 2
            f_of = (lambda f: 0) if L else (lambda f: f)

            def turn(b, n):
                after(pe, a["ln_done"], b * (2 * GB) + n + 1)
                after(pe, a["x_t_copied"], b * TURNS + n)
                for q in range(QT_):
                    for k in range(KC):
                        last = nc.tensor.transpose(PS[:, k, q * P:(q + 1) * P], XNA[:, q, k * P:(k + 1) * P],
                                                   ident[:])
                last.then_inc(a["x_t"], 1)
                if n == 0:
                    after(pe, a["logits_copied"], b * GB)
                    after(pe, a["o_done"], b * NTB)
                    for f in range(nh):
                        for k in range(KC):
                            last = nc.tensor.matmul(PS[:, 7 - f, 0:NK], AW[:, k, D + f * P:D + (f + 1) * P],
                                                    CT[:, k, bass.ds(b * NK, NK)], start=k == 0, stop=k == KC - 1)
                    last.then_inc(a["k_ready"], 1)
                else:
                    values(b, 0)
                after(pe, a["x_t_copied"], b * TURNS + n + 1)

            def turn_row(b, g, q):
                if q == 0:
                    after(pe, a["ln_done"], b * (2 * GB) + GB + g + 1)
                after(pe, a["x_t_copied"], b * TURNS + GB + g * QT_ + max(q - 1, 0))
                for k in range(KC):
                    last = nc.tensor.transpose(PS[:, 2 + q % 2, k * P:(k + 1) * P], XNR[:, q, k * P:(k + 1) * P],
                                               ident[:])
                last.then_inc(a["x_t"], 1)

            def route(b, g, q):
                after(pe, a["x_t_copied"], b * TURNS + GB + g * QT_ + q + 1)
                if q == 0:
                    after(pe, a["logits_copied"], b * GB + g)
                    after(pe, a["o_done"], b * NTB + (g + 1) * QT_)
                w = NW[L]
                for k in range(KC):
                    last = nc.tensor.matmul(PS[:, 6, q * w:(q + 1) * w], RT[:, q % 2, k], gwt[:, k, 0:w],
                                            start=k == 0, stop=k == KC - 1)
                last.then_inc(a["row_used"], 1)

            def maximum(n0, i):
                q, c = i // 4, i % 4
                if i == 0:
                    after(pe, a["qb_copied"], n0 + 1)
                after(pe, a["smax_used"], n0 * (4 * QT_) + max(i - 1, 0))
                cols = slice(c % 2 * QK, (c % 2 + 1) * QK)
                last = nc.tensor.matmul(PS[:, 2 + i % 2, 0:QK], QB[:, c // 2, q * P:(q + 1) * P],
                                        KB[:, f_of(c // 2), cols], start=True, stop=not L)
                if L:
                    last = nc.tensor.matmul(PS[:, 2 + i % 2, 0:QK], onesb[0:1], used[:, cols],
                                            start=False, stop=True)
                last.then_inc(a["smax"], 1)

            def match(b, g):
                if g == 0:
                    after(pe, a["logits_copied"], b * GB)
                    after(pe, a["x_added"], b * NTB)
                else:
                    after(pe, a["k_built"], b + 1)
                after(pe, a["q_copied"], b * GB + g + 1)
                for q in range(QT_):
                    for f in range(2):
                        last = nc.tensor.matmul(PS[:, 6 + g, q * NK:(q + 1) * NK], QF[:, g, f, q * P:(q + 1) * P],
                                                CT[:, f, bass.ds(b * NK, NK)], start=f == 0, stop=f == 1)
                last.then_inc(a["s77"], 1)

            def values(b, f):
                after(pe, a["ctx_rep"], b + 1)
                after(pe, a["v_built"], b * nh + f)
                for j in range(JT):
                    for k in range(KC):
                        last = nc.tensor.matmul(PS[0:ROWS[j], 4 + j // 4, (j % 4) * P:(j % 4 + 1) * P],
                                                CR[:, k, j * P:j * P + ROWS[j]],
                                                AW[:, k, 2 * D + f * P:2 * D + (f + 1) * P],
                                                start=k == 0, stop=k == KC - 1)
                    if j == JT - 1:
                        last.then_inc(a["v_ready"], 1)
                    for i in first_maxima(L, f, j):
                        maximum(b * GB, i)

            def turn_maxima(n0):
                after(pe, a["smax_used"], n0 * (4 * QT_) + 4 * QT_)
                for q in range(QT_):
                    last = nc.tensor.transpose(PS[0:H, 0, 0:G // 2].bitcast(BF16)[:, q * P:(q + 1) * P],
                                               MX[:, q], identb[:])
                last.then_inc(a["mx_t"], 1)

            def scores(n0, g, i):
                f, j = i // JT, i % JT
                rows = ROWS[j]
                after(pe, a["exp_done"], n0 * (2 * JT) + max(i - 1, 0))
                nc.tensor.matmul(PS[0:rows, 4 + i % 2], KF[:, f_of(f), j * P:j * P + rows], QF[:, g, f],
                                 start=True, stop=False)
                if i == 0:
                    after(pe, a["mx_copied"], n0 + 1)
                nc.tensor.matmul(PS[0:rows, 4 + i % 2], IND[:, f, j * P:j * P + rows], MT,
                                 start=False, stop=True).then_inc(a["s_ready"], 1)

            with pe.Fori(0, NB) as b:
                for g in range(GB):
                    turn(b, g)
                    if g == 0:
                        after(pe, a["smax_used"], b * (GB * 4 * QT_))
                    elif L == 0:
                        after(pe, a["k_built"], b + 1)
                    else:
                        match(b, 0)
                    for f in range(2):
                        for k in range(KC):
                            last = nc.tensor.matmul(PS[:, q_bank(L, g) + f], AW[:, k, f * P:(f + 1) * P], XNT[:, k],
                                                    start=k == 0, stop=k == KC - 1)
                    last.then_inc(a["q_ready"], 1)
                if L:
                    match(b, 1)
                if L == 0:
                    values(b, 1)
                if L:
                    after(pe, a["counted"], b + 1)
                    after(pe, a["s77_used"], b * GB + GB)
                    for j in range(JT):
                        nc.tensor.matmul(PS[:, 6, j:j + 1], SR[:, j * P:(j + 1) * P], onec[:], start=True, stop=True)
                    for w in range(2):
                        last = nc.tensor.matmul(PS[0:1, 2 + w, 0:QK], onec[:], SR[:, w * QK:(w + 1) * QK],
                                                start=True, stop=True)
                    last.then_inc(a["c_ready"], 1)
                if L:
                    after(pe, a["cnt_bias"], b + 1)
                    for i in range(4 * QT_):
                        maximum(b * GB, i)
                for g in range(GB):
                    n0 = b * GB + g
                    if g == 0:
                        after(pe, a["k_built"], b + 1)
                        after(pe, a["v_built"], b * nh + nh)
                        turn_maxima(n0)
                    for i in range(AHEAD if g else 0, 2 * JT):
                        scores(n0, g, i)
                        if g == 1:
                            if i > R_AT + 1:
                                route(b, 0, i - R_AT - 2)
                            if R_AT <= i < R_AT + QT_:
                                turn_row(b, 0, i - R_AT)
                    if g == 1:
                        after(pe, a["logits_copied"], b * GB + 1)
                    for s in range(QT_ + 2):
                        if s < QT_:
                            after(pe, a["o_done"], n0 * QT_ + max(s - 1, 0))
                            for f in range(2):
                                after(pe, a["exp_done"], n0 * (2 * JT) + (f + 1) * JT)
                                for j in range(JT):
                                    last = nc.tensor.matmul(
                                        PS[:, 6 + s % 2, f * HH * VW:(f + 1) * HH * VW],
                                        PR[0:ROWS[j], f * JT + j, s * P:(s + 1) * P],
                                        VF[0:ROWS[j], f_of(f), j].rearrange("p h v -> p (h v)"),
                                        start=j == 0, stop=j == JT - 1)
                                if f == 1:
                                    last.then_inc(a["o_ready"], 1)
                                if g + 1 < GB:
                                    for i in range(4 * s + 2 * f, 4 * s + 2 * f + 2):
                                        maximum(n0 + 1, i)
                        if s == QT_ and g + 1 < GB:
                            after(pe, a["o_t_copied"], n0 * QT_ + QT_ - 1)
                            turn_maxima(n0 + 1)
                        if s >= 2:
                            u = s % 2
                            after(pe, a["o_t_copied"], n0 * QT_ + s - 1)
                            after(pe, a["x_added"], n0 * QT_ + s - 2)
                            for k in range(KC):
                                last = nc.tensor.matmul(PS[:, 1, 0:D], OT[:, u, k], AW[:, k, 3 * D:4 * D],
                                                        start=k == 0, stop=k == KC - 1)
                            last.then_inc(a["y_ready"], 1)
                        if 1 <= s <= QT_:
                            after(pe, a["o_done"], n0 * QT_ + s)
                            after(pe, a["o_t_copied"], n0 * QT_ + s - 1)
                            if s == QT_ and g + 1 < GB:
                                after(pe, a["mx_copied"], n0 + 2)
                            for k in range(KC):
                                last = nc.tensor.transpose(PS[:, 0, k * P:(k + 1) * P],
                                                           OA[:, (s - 1) % 2, k * P:(k + 1) * P], ident[:])
                            last.then_inc(a["o_t"], 1)
                        if s == QT_ and g + 1 < GB:
                            for i in range(AHEAD):
                                scores(n0 + 1, g + 1, i)
                for q in range(QT_ + 1):
                    if q < QT_:
                        turn_row(b, 1, q)
                    if q:
                        route(b, 1, q - 1)
            pe.wait_ge(r["onehot"], TOPK)
            pe.wait_ge(r["r_consts"], 7)
            nc.tensor.matmul(PS[:, 4, 0:GE], R_u, R_M.rearrange("p g e -> p (g e)"), start=True, stop=True)
            nc.tensor.matmul(PS[:, 5, 0:GE], R_1, R_M.rearrange("p g e -> p (g e)"), start=True,
                             stop=True).then_inc(r["totals"], 1)

        def pe_experts(pe, L):
            e, n, lead = E[L], NS + (NT if L else 0), (NT if L else 0)
            hw = F1 if L else 512

            held = [pe.alloc_register(f"expert{u}_{L}") for u in range(2)]

            def look_up(i, u):
                pe.reg_load(held[u], texp[0:1, bass.ds(i - lead, 1)])

            def expert(u, shared):
                return NE if shared else pe.snap(held[u], min_val=0, max_val=NE - 1)

            def turn(h, u):
                i = h * 2 + u
                pe.wait_ge(e[f"xs_loaded_{u}"], h * 16 + 16)
                pe.wait_ge(e["xt_copied"], i)
                for k in range(KC):
                    last = nc.tensor.transpose(PS[:, 7, k * P:(k + 1) * P], FB[L]["XS"][:, u, k * P:(k + 1) * P], ident[:])
                last.then_inc(e["xs_t"], 1)

            def up(i, u, s, ex, later):
                if later:
                    if L:
                        pe.wait_ge(e["h_mul" if s else "h_act"], i - 1)
                    else:
                        pe.wait_ge(e["h_act"], i * 2 + s - 3)
                for k in range(KC):
                    if L:
                        rhs = W1a[:, bass.ds(ex * WG1 + (s * KC + k) * F1, F1)]
                    else:
                        rhs = W0a[:, bass.ds(ex * W0E + k * F0 + s * 512, 512)]
                    last = nc.tensor.matmul(PS[:, 2 * u + s, 0:hw], FB[L]["XT"][:, u, k], rhs, start=k == 0,
                                            stop=bool(L) and k == KC - 1)
                if not L:
                    if s == 0:
                        pe.wait_ge(e["sel_up"], i + 1)
                    last = nc.tensor.matmul(PS[:, 2 * u + s], SEL[:, 0, u], b1t[:, s * 512:(s + 1) * 512],
                                            start=False, stop=True)
                last.then_inc(e["h_ready"], 1)

            def turn_hidden(i, u):
                pe.wait_ge(e["h_mul"], i + 1) if L else pe.wait_ge(e["h_act"], i * 2 + 2)
                pe.wait_ge(e["ht_copied"], i)
                for c in range(3 if L else FC0):
                    if L:
                        at, w = C1[c]
                        last = nc.tensor.transpose(PS[0:w, 4, c * P:(c + 1) * P], FB[L]["H"][:, u, 512 + at:512 + at + w], ident[:])
                    else:
                        last = nc.tensor.transpose(PS[:, 4 + c // 4, c % 4 * P:(c % 4 + 1) * P],
                                                   FB[L]["H"][:, u, c * P:(c + 1) * P], ident[:])
                last.then_inc(e["h_t"], 1)

            def down(i, u, ex):
                pe.wait_ge(e["ht_copied"], i + 1)
                pe.wait_ge(e["y_copied"], i)
                nch = 3 if L else FC0
                for c in range(nch):
                    w = C1[c][1] if L else P
                    base = W1b[0:w, bass.ds(ex * WD1 + c * D, D)] if L else W0b[:, bass.ds(ex * W0E + c * D, D)]
                    last = nc.tensor.matmul(PS[:, 6, 0:D], FB[L]["HT"][0:w, u, c], base, start=c == 0,
                                            stop=bool(L) and c == nch - 1)
                if not L:
                    pe.wait_ge(e["sel_down"], i + 1)
                    last = nc.tensor.matmul(PS[:, 6, 0:D], SEL[:, 1, u], b2t[:], start=False, stop=True)
                last.then_inc(e["yt_ready"], 1)

            def step(h, u):
                i = h * 2 + u
                fixed = isinstance(i, int)
                now = L == 1 and (i < lead if fixed else loops[0] == 0)
                before = L == 1 and (i <= lead if fixed else loops[0] == 0)
                ex = expert(u, now)
                pe.wait_ge(e["xt_copied"], i + 1)
                later = not (fixed and i < 2)
                up(i, u, 0, ex, later)
                if not (fixed and i == 0):
                    turn_hidden(i - 1, 1 - u)
                up(i, u, 1, ex, later)
                if not (fixed and i == n - 1):
                    turn(*((h, 1) if u == 0 else (h + 1, 0)))
                if not (fixed and i == 0):
                    down(i - 1, 1 - u, expert(1 - u, before))
                if L and fixed and i == lead - 1:
                    pe.wait_ge(R[1]["routed"], 1)
                if not fixed and loops[0] or not L or fixed and lead - 1 <= i:
                    if not (fixed and i == n - 1):
                        look_up(i + 1, 1 - u)
                if not fixed and u == 1:
                    loops[0] += 1

            loops = [0]
            pe.wait_ge(U["w1_loaded"] if L else U["w0_loaded"], 16 * (4 * (NE + 1) if L else 2 * NE))
            turn(0, 0)
            if not L:
                pe.wait_ge(U["bias_split"], 1)
                pe.wait_ge(R[0]["routed"], 1)
                look_up(0, 0)
            over_tiles(pe, L, step)
            turn_hidden(n - 1, (n - 1) % 2)
            down(n - 1, (n - 1) % 2, expert((n - 1) % 2, False))

        @block.tensor
        def _(pe):
            count_from_one(pe, "pe")
            pe.wait_ge(U["ctx_loaded"], 16)
            pe.wait_ge(U["consts_set"], 1)
            for b in range(NB):
                for k in range(KC):
                    last = nc.tensor.transpose(PS[:, 0, (k * NB + b) * NK:(k * NB + b + 1) * NK],
                                               ctx_raw[:, b, k * P:(k + 1) * P], ident[0:NK, 0:NK])
            last.then_inc(U["ctx_t"], 1)
            pe.wait_ge(U["ctx_copied"], 1)
            pe.wait_ge(U["attn_w_loaded"], 32)
            pe.wait_ge(U["gate_w_loaded"], 16)
            pe_attention(pe, 0)
            pe_experts(pe, 0)
            pe.wait_ge(U["w1_raw_loaded"], 80)
            pe.wait_ge(E[0]["y_copied"], NS)
            for k in range(KC):
                for c in range(2):
                    nc.tensor.transpose(PS[:, k, c * P:(c + 1) * P], rq[:, c, k * P:(k + 1) * P], ident[:])
                    nc.tensor.transpose(PS[:, 2 + k, c * P:(c + 1) * P], rc[:, c, k * P:(k + 1) * P], ident[:])
                nc.tensor.transpose(PS[:, 4 + k, 0:2 * HD], rkv[:, k * P:(k + 1) * P], ident[0:2 * HD, 0:2 * HD])
                last = nc.tensor.transpose(PS[:, 6 + k, 0:NE + 1], rg[:, k * P:(k + 1) * P],
                                           ident[0:NE + 1, 0:NE + 1])
            last.then_inc(U["w1_t"], 1)
            pe.wait_ge(U["w1_copied"], 1)
            pe_attention(pe, 1)
            pe_experts(pe, 1)


_INS = ['x', 'ctx_1024', 'g_xattn', 'g_ffn', 'L0_xattn_W_qkv', 'L0_xattn_W_proj', 'L0_xattn_b_proj',
        'L0_ffn_gate_w', 'L0_ffn_w1', 'L0_ffn_b1', 'L0_ffn_w2', 'L0_ffn_b2', 'L1_xattn_Wq', 'L1_xattn_Wkv',
        'L1_xattn_Wc', 'L1_ffn_gate_w', 'L1_ffn_w_gate', 'L1_ffn_w_up', 'L1_ffn_w_down', 'L1_ffn_sw_gate',
        'L1_ffn_sw_up', 'L1_ffn_sw_down', 'L1_ffn_shared_gate_w']
_OUTS = [((NB, S, D), 'float32')]


def kernel(**inputs):
    import numpy as _np
    import concourse.bacc as _bacc
    from concourse import mybir as _mybir
    from concourse.bass_utils import run_bass_kernel_spmd as _run

    nc = _bacc.Bacc("TRN2", target_bir_lowering=False, num_devices=1)
    arrays, args = {}, []
    for name in _INS:
        a = _np.ascontiguousarray(inputs[name])
        arrays[f"in_{name}_dram"] = a
        args.append(nc.dram_tensor(f"in_{name}_dram", a.shape, _mybir.dt.from_np(a.dtype), kind="ExternalInput").ap())
    for i, (shape, dtype) in enumerate(_OUTS):
        dt = _mybir.dt.from_np(_np.dtype(dtype))
        args.append(nc.dram_tensor(f"out_{i}_dram", shape, dt, kind="ExternalOutput").ap())
    program(nc, *args)
    r = _run(nc, [arrays], core_ids=[0])
    return r.results[0]["out_0_dram"]
```
